# Optimizing a Trainium2 kernel written in Bass

```python
import numpy as np
import jax
import jax.numpy as jnp

def _softmax(x, axis=-1):
    return jax.nn.softmax(x, axis=axis)
def _gelu(x):
    return jax.nn.gelu(x, approximate=True)
def _silu(x):
    return jax.nn.silu(x)
def _sigmoid(x):
    return jax.nn.sigmoid(x)
def _layernorm(x, axis=-1, eps=1e-5):
    m = jnp.mean(x, axis=axis, keepdims=True)
    v = jnp.var(x, axis=axis, keepdims=True)
    return (x - m) / jnp.sqrt(v + eps)
def _scatter_add(tgt, idx, src, axis=0):
    return tgt.at[idx].add(src)
def _segment_sum(src, seg, n):
    return jax.ops.segment_sum(src, seg, n)

kernel_name = 'mk_metaformer_d2_conv_nhwc128_bff358'

def setup_inputs(seed: int = 0):
    np.random.seed(seed)
    _w = jnp.asarray
    def _rec_inputs():
        import jax
        import jax.numpy as jnp
        _gk = jax.random.key(seed)
        x = -0.0002091 + 1 * jax.random.normal(jax.random.fold_in(_gk, 1), (64, 56, 56, 128), jnp.float32)
        return x
    x = _rec_inputs()
    def _L0_conv_setup():
        import jax, jax.numpy as jnp
        import numpy as np
        WINDOW = 7
        HEADS = 4
        HEAD_DIM = 32
        DISP = WINDOW // 2
        SCALE = HEADS ** (-0.5)

        def _create_mask(ws, d, upper_lower, left_right):
            m = np.zeros((ws * ws, ws * ws), dtype=np.float32)
            if upper_lower:
                m[-d * ws:, :-d * ws] = -np.inf
                m[:-d * ws, -d * ws:] = -np.inf
            if left_right:
                m = m.reshape(ws, ws, ws, ws)
                m[:, -d:, :, :-d] = -np.inf
                m[:, :-d, :, -d:] = -np.inf
                m = m.reshape(ws * ws, ws * ws)
            return m

        def _relative_indices(ws):
            coords = np.array([[x, y] for x in range(ws) for y in range(ws)])
            return coords[None, :, :] - coords[:, None, :] + ws - 1

        def _to_windows(t, ws, heads, hd):
            b, H, W, _ = t.shape
            nwh, nww = (H // ws, W // ws)
            t = t.reshape(b, nwh, ws, nww, ws, heads, hd)
            return t.transpose(0, 5, 1, 3, 2, 4, 6).reshape(b, heads, nwh * nww, ws * ws, hd)

        def _from_windows(t, ws, nwh, nww):
            b, h, nw, s2, d = t.shape
            t = t.reshape(b, h, nwh, nww, ws, ws, d)
            return t.transpose(0, 2, 4, 3, 5, 1, 6).reshape(b, nwh * ws, nww * ws, h * d)
        key = jax.random.key(seed)
        k1, k2, k3, k4 = jax.random.split(key, 4)
        inner = HEADS * HEAD_DIM
        return {'x': jax.random.normal(k1, (64, 56, 56, 128), dtype=jnp.float32), 'w_qkv': jax.random.normal(k2, (3 * inner, 128), dtype=jnp.float32) * 0.02, 'pos_embedding': jax.random.normal(k3, (2 * WINDOW - 1, 2 * WINDOW - 1), dtype=jnp.float32), 'w_out': jax.random.normal(k4, (128, inner), dtype=jnp.float32) * 0.02, 'b_out': jnp.zeros((128,), dtype=jnp.float32)}
    _L0_conv_all = _L0_conv_setup()
    _L0_conv_in = {k: v for k, v in _L0_conv_all.items() if k in ('w_qkv', 'pos_embedding', 'w_out', 'b_out', )}
    del _L0_conv_all

    def _L0_ffn_setup():
        import jax, jax.numpy as jnp
        import numpy as np
        BN_EPS = 1e-05
        key = jax.random.key(seed)
        k1, k2, k3 = jax.random.split(key, 3)
        B, T, I, H = (64, 2048, 128, 128)
        x = jax.random.normal(k1, (B, T, I), dtype=jnp.float32)
        W = jax.random.normal(k2, (H, I), dtype=jnp.float32) * (1.0 / np.sqrt(I))
        V = jnp.linalg.qr(jax.random.normal(k3, (H, H), dtype=jnp.float32))[0]
        gamma = jnp.ones((H,), dtype=jnp.float32)
        beta = jnp.zeros((H,), dtype=jnp.float32)
        return {'x': x, 'W': W, 'V': V, 'gamma': gamma, 'beta': beta}
    _L0_ffn_all = _L0_ffn_setup()
    _L0_ffn_in = {k: v for k, v in _L0_ffn_all.items() if k in ('W', 'V', 'gamma', 'beta', )}
    del _L0_ffn_all

    def _L1_conv_setup():
        import jax, jax.numpy as jnp
        import numpy as np
        EPS = 1e-06

        def kernel_to_freq_2d(kernel, H, W):
            C, kh, kw = kernel.shape
            th = (jnp.arange(kh) - kh // 2) % H
            tw = (jnp.arange(kw) - kw // 2) % W
            TH, TW = jnp.meshgrid(th, tw, indexing='ij')
            padded = jnp.zeros((C, H, W), dtype=kernel.dtype).at[:, TH, TW].set(kernel)
            return jnp.fft.fft2(padded, axes=(1, 2))

        def heinsen_scan_log(log_coeffs, log_values):

            def op(left, right):
                la, lb = left
                ra, rb = right
                return (la + ra, jnp.logaddexp(ra + lb, rb))
            _, log_h = jax.lax.associative_scan(op, (log_coeffs, log_values), axis=0)
            return log_h
        key = jax.random.key(seed)
        ks = jax.random.split(key, 7)
        B, H, W, C, k = (4, 128, 128, 128, 7)
        fan_in = k * k
        x = jax.random.normal(ks[0], (B, H, W, C), dtype=jnp.float32)
        A_kernel = jax.random.normal(ks[1], (C, k, k), dtype=jnp.float32) / np.sqrt(fan_in)
        B_kernel = jax.random.normal(ks[2], (C, k, k), dtype=jnp.float32) / np.sqrt(fan_in)
        gate_A_kernel = jax.random.normal(ks[3], (C, k, k), dtype=jnp.float32) * 0.02
        gate_B_kernel = jax.random.normal(ks[4], (C, k, k), dtype=jnp.float32) * 0.02
        W_out = jax.random.normal(ks[5], (C, C), dtype=jnp.float32) / np.sqrt(C)
        b_out = jnp.zeros((C,), dtype=jnp.float32)
        return dict(x=x, A_kernel=A_kernel, B_kernel=B_kernel, gate_A_kernel=gate_A_kernel, gate_B_kernel=gate_B_kernel, W_out=W_out, b_out=b_out, T=8)
    _L1_conv_all = _L1_conv_setup()
    _L1_conv_in = {k: v for k, v in _L1_conv_all.items() if k in ('A_kernel', 'B_kernel', 'gate_A_kernel', 'gate_B_kernel', 'W_out', 'b_out', )}
    del _L1_conv_all

    def _L1_ffn_setup():
        import jax, jax.numpy as jnp
        import numpy as np
        B, S, D, E, H, O, K = (512, 2048, 128, 64, 512, 128, 8)
        key = jax.random.key(seed)
        k0, k1, k2, k3 = jax.random.split(key, 4)
        x = jax.random.normal(k0, (B, S, D), dtype=jnp.float32)
        gate_w = jax.random.normal(k1, (E, D), dtype=jnp.float32) * (1.0 / np.sqrt(D))
        gate_b = jnp.zeros((E,), dtype=jnp.float32)
        weight1 = jax.random.uniform(k2, (E, D + 1, H), dtype=jnp.float32, minval=-1.0, maxval=1.0) * (1.0 / np.sqrt(D + 1))
        weight2 = jax.random.uniform(k3, (E, H + 1, O), dtype=jnp.float32, minval=-1.0, maxval=1.0) * (1.0 / np.sqrt(H + 1))
        return {'x': x, 'gate_w': gate_w, 'gate_b': gate_b, 'weight1': weight1, 'weight2': weight2}
    _L1_ffn_all = _L1_ffn_setup()
    _L1_ffn_in = {k: v for k, v in _L1_ffn_all.items() if k in ('gate_w', 'gate_b', 'weight1', 'weight2', )}
    del _L1_ffn_all

    return {
        "x": x,
        "L0_conv_w_qkv": _L0_conv_in["w_qkv"],
        "L0_conv_pos_embedding": _L0_conv_in["pos_embedding"],
        "L0_conv_w_out": _L0_conv_in["w_out"],
        "L0_conv_b_out": _L0_conv_in["b_out"],
        "L0_ffn_W": _L0_ffn_in["W"],
        "L0_ffn_V": _L0_ffn_in["V"],
        "L0_ffn_gamma": _L0_ffn_in["gamma"],
        "L0_ffn_beta": _L0_ffn_in["beta"],
        "L1_conv_A_kernel": _L1_conv_in["A_kernel"],
        "L1_conv_B_kernel": _L1_conv_in["B_kernel"],
        "L1_conv_gate_A_kernel": _L1_conv_in["gate_A_kernel"],
        "L1_conv_gate_B_kernel": _L1_conv_in["gate_B_kernel"],
        "L1_conv_W_out": _L1_conv_in["W_out"],
        "L1_conv_b_out": _L1_conv_in["b_out"],
        "L1_ffn_gate_w": _L1_ffn_in["gate_w"],
        "L1_ffn_gate_b": _L1_ffn_in["gate_b"],
        "L1_ffn_weight1": _L1_ffn_in["weight1"],
        "L1_ffn_weight2": _L1_ffn_in["weight2"],
    }

def reference(x, L0_conv_w_qkv, L0_conv_pos_embedding, L0_conv_w_out, L0_conv_b_out, L0_ffn_W, L0_ffn_V, L0_ffn_gamma, L0_ffn_beta, L1_conv_A_kernel, L1_conv_B_kernel, L1_conv_gate_A_kernel, L1_conv_gate_B_kernel, L1_conv_W_out, L1_conv_b_out, L1_ffn_gate_w, L1_ffn_gate_b, L1_ffn_weight1, L1_ffn_weight2):
    import jax
    import jax.numpy as jnp
    def _L0_conv_ref(x, w_qkv, pos_embedding, w_out, b_out):
        import jax, jax.numpy as jnp
        import numpy as np
        WINDOW = 7
        HEADS = 4
        HEAD_DIM = 32
        DISP = WINDOW // 2
        SCALE = HEADS ** (-0.5)

        def _create_mask(ws, d, upper_lower, left_right):
            m = np.zeros((ws * ws, ws * ws), dtype=np.float32)
            if upper_lower:
                m[-d * ws:, :-d * ws] = -np.inf
                m[:-d * ws, -d * ws:] = -np.inf
            if left_right:
                m = m.reshape(ws, ws, ws, ws)
                m[:, -d:, :, :-d] = -np.inf
                m[:, :-d, :, -d:] = -np.inf
                m = m.reshape(ws * ws, ws * ws)
            return m

        def _relative_indices(ws):
            coords = np.array([[x, y] for x in range(ws) for y in range(ws)])
            return coords[None, :, :] - coords[:, None, :] + ws - 1

        def _to_windows(t, ws, heads, hd):
            b, H, W, _ = t.shape
            nwh, nww = (H // ws, W // ws)
            t = t.reshape(b, nwh, ws, nww, ws, heads, hd)
            return t.transpose(0, 5, 1, 3, 2, 4, 6).reshape(b, heads, nwh * nww, ws * ws, hd)

        def _from_windows(t, ws, nwh, nww):
            b, h, nw, s2, d = t.shape
            t = t.reshape(b, h, nwh, nww, ws, ws, d)
            return t.transpose(0, 2, 4, 3, 5, 1, 6).reshape(b, nwh * ws, nww * ws, h * d)
        ws = WINDOW
        b, H, W, _ = x.shape
        nwh, nww = (H // ws, W // ws)
        x = jnp.roll(x, shift=(-DISP, -DISP), axis=(1, 2))
        qkv = x @ w_qkv.T
        q, k, v = jnp.split(qkv, 3, axis=-1)
        q = _to_windows(q, ws, HEADS, HEAD_DIM)
        k = _to_windows(k, ws, HEADS, HEAD_DIM)
        v = _to_windows(v, ws, HEADS, HEAD_DIM)
        scores = jnp.einsum('bhwid,bhwjd->bhwij', q, k) * SCALE
        ri = _relative_indices(ws)
        bias = pos_embedding[ri[:, :, 0], ri[:, :, 1]]
        scores = scores + bias
        ul = _create_mask(ws, DISP, True, False)
        lr = _create_mask(ws, DISP, False, True)
        full_mask = np.zeros((nwh * nww, ws * ws, ws * ws), dtype=np.float32)
        full_mask[-nww:] += ul
        full_mask[nww - 1::nww] += lr
        scores = scores + jnp.asarray(full_mask)
        probs = jax.nn.softmax(scores, axis=-1)
        attn = jnp.einsum('bhwij,bhwjd->bhwid', probs, v)
        out = _from_windows(attn, ws, nwh, nww)
        out = out @ w_out.T + b_out
        out = jnp.roll(out, shift=(DISP, DISP), axis=(1, 2))
        return out

    def _L0_ffn_ref(x, W, V, gamma, beta):
        import jax, jax.numpy as jnp
        import numpy as np
        BN_EPS = 1e-05
        B, T, H = (x.shape[0], x.shape[1], W.shape[0])
        Wx = jnp.einsum('bti,hi->bth', x, W)
        flat = Wx.reshape(B * T, H)
        mean = jnp.mean(flat, axis=0)
        var = jnp.var(flat, axis=0)
        Wx = ((flat - mean) * jax.lax.rsqrt(var + BN_EPS) * gamma + beta).reshape(B, T, H)
        Vt = V.T

        def step(yt, wx_t):
            yt = jax.nn.sigmoid(wx_t + yt @ Vt)
            return (yt, yt)
        y0 = jnp.zeros((B, H), dtype=Wx.dtype)
        _, ys = jax.lax.scan(step, y0, jnp.swapaxes(Wx, 0, 1))
        return jnp.swapaxes(ys, 0, 1)

    def _L1_conv_ref(x, A_kernel, B_kernel, gate_A_kernel, gate_B_kernel, W_out, b_out, T):
        import jax, jax.numpy as jnp
        import numpy as np
        EPS = 1e-06

        def kernel_to_freq_2d(kernel, H, W):
            C, kh, kw = kernel.shape
            th = (jnp.arange(kh) - kh // 2) % H
            tw = (jnp.arange(kw) - kw // 2) % W
            TH, TW = jnp.meshgrid(th, tw, indexing='ij')
            padded = jnp.zeros((C, H, W), dtype=kernel.dtype).at[:, TH, TW].set(kernel)
            return jnp.fft.fft2(padded, axes=(1, 2))

        def heinsen_scan_log(log_coeffs, log_values):

            def op(left, right):
                la, lb = left
                ra, rb = right
                return (la + ra, jnp.logaddexp(ra + lb, rb))
            _, log_h = jax.lax.associative_scan(op, (log_coeffs, log_values), axis=0)
            return log_h
        B, H, W, C = x.shape

        def ifft_real(z_bhwc):
            return jnp.fft.ifft2(z_bhwc.transpose(0, 3, 1, 2), axes=(2, 3)).real.transpose(0, 2, 3, 1)
        A_f = kernel_to_freq_2d(A_kernel, H, W).transpose(1, 2, 0)
        B_f = kernel_to_freq_2d(B_kernel, H, W).transpose(1, 2, 0)
        gA_f = kernel_to_freq_2d(gate_A_kernel, H, W).transpose(1, 2, 0)
        gB_f = kernel_to_freq_2d(gate_B_kernel, H, W).transpose(1, 2, 0)
        x_f = jnp.fft.fft2(x.transpose(0, 3, 1, 2), axes=(2, 3)).transpose(0, 2, 3, 1)
        gate_A = jax.nn.sigmoid(ifft_real(gA_f[None] * x_f))
        gate_B = jax.nn.sigmoid(ifft_real(gB_f[None] * x_f))
        a_spatial = ifft_real(jnp.broadcast_to(A_f[None], (B, H, W, C)))
        b_spatial = ifft_real(B_f[None] * x_f)
        a_t = a_spatial * gate_A
        b_t = b_spatial * gate_B
        gate_seq = jnp.tile(a_t[None], (T, 1, 1, 1, 1))
        h_tilde_seq = jnp.tile(b_t[None], (T, 1, 1, 1, 1))
        log_z = -jax.nn.softplus(-gate_seq)
        log_coeffs = -jax.nn.softplus(gate_seq)
        log_values = log_z + jnp.log(jax.nn.softplus(h_tilde_seq) + EPS)
        log_h = heinsen_scan_log(log_coeffs, log_values)
        h_final = jnp.exp(log_h[-1])
        return h_final @ W_out + b_out

    def _L1_ffn_ref(x, gate_w, gate_b, weight1, weight2):
        import jax, jax.numpy as jnp
        import numpy as np
        B, S, D, E, H, O, K = (512, 2048, 128, 64, 512, 128, 8)
        Bn, Sn, Dn = x.shape
        logits = jnp.einsum('bsd,ed->bse', x, gate_w) + gate_b
        probs = jax.nn.softmax(logits, axis=1)
        vals, idx = jax.lax.top_k(probs.transpose(0, 2, 1), K)
        topv = vals.transpose(0, 2, 1)
        topi = idx.transpose(0, 2, 1)
        flat_idx = topi.reshape(Bn, K * E)
        gathered = jnp.take_along_axis(x, flat_idx[:, :, None], axis=1)
        gathered = gathered.reshape(Bn, K, E, Dn)
        pooled = jnp.einsum('bked,bke->bed', gathered, topv)
        ones = jnp.ones((E, Bn, 1), dtype=x.dtype)
        h = jnp.concatenate([pooled.transpose(1, 0, 2), ones], axis=-1)
        h = jax.nn.gelu(jnp.einsum('ebd,edh->ebh', h, weight1), approximate=False)
        h = jnp.concatenate([h, ones], axis=-1)
        out = jnp.einsum('ebh,eho->ebo', h, weight2)
        out = out.transpose(1, 0, 2)
        weighted = jnp.einsum('beo,bke->bkeo', out, topv).reshape(Bn, K * E, O)
        outputs = jnp.zeros((Bn, Sn, O), dtype=x.dtype)
        outputs = outputs.at[jnp.arange(Bn)[:, None], flat_idx].add(weighted)
        return outputs

    def _gn(v, G=32, eps=1e-5):
        B_, H_, W_, C_ = v.shape
        g = v.reshape(B_, H_, W_, G, C_ // G)
        m = jnp.mean(g, axis=(1, 2, 4), keepdims=True)
        s = jnp.var(g, axis=(1, 2, 4), keepdims=True)
        return ((g - m) / jnp.sqrt(s + eps)).reshape(v.shape)

    def _ln_c(v, eps=1e-6):
        m = jnp.mean(v, axis=-1, keepdims=True)
        s = jnp.var(v, axis=-1, keepdims=True)
        return (v - m) / jnp.sqrt(s + eps)

    def _ln_t(v, eps=1e-5):
        m = jnp.mean(v, axis=-1, keepdims=True)
        s = jnp.var(v, axis=-1, keepdims=True)
        return (v - m) / jnp.sqrt(s + eps)

    def _to_tokens(v):
        B_, H_, W_, C_ = v.shape
        return v.reshape(B_, H_ * W_, C_)
    def _from_tokens(t, like):
        return t.reshape(like.shape)

    x = x + _L0_conv_ref(_ln_c(x), L0_conv_w_qkv, L0_conv_pos_embedding, L0_conv_w_out, L0_conv_b_out)
    t = _to_tokens(x)
    t = t + _L0_ffn_ref(_ln_t(t), L0_ffn_W, L0_ffn_V, L0_ffn_gamma, L0_ffn_beta)
    x = _from_tokens(t, x)
    x = x + _L1_conv_ref(_ln_c(x), L1_conv_A_kernel, L1_conv_B_kernel, L1_conv_gate_A_kernel, L1_conv_gate_B_kernel, L1_conv_W_out, L1_conv_b_out, 8)
    t = _to_tokens(x)
    t = t + _L1_ffn_ref(_ln_t(t), L1_ffn_gate_w, L1_ffn_gate_b, L1_ffn_weight1, L1_ffn_weight2)
    x = _from_tokens(t, x)
    return x


_drawn_inputs = setup_inputs


def setup_inputs(seed=0):
    import zlib

    import numpy as np

    out = dict(_drawn_inputs(seed))
    spreads = {'L0_conv_b_out': (0.0, 0.1),
     'L0_ffn_gamma': (1.0, 0.6),
     'L0_ffn_beta': (0.0, 0.467),
     'L1_conv_b_out': (0.0, 0.1),
     'L1_ffn_gate_b': (0.0, 0.8)}
    factors = {'L0_conv_w_qkv': 5.411,
     'L0_conv_pos_embedding': 6.855,
     'L0_conv_w_out': 5.456,
     'L1_conv_A_kernel': 64.0,
     'L1_conv_gate_A_kernel': 64.0,
     'L1_conv_gate_B_kernel': 3.919,
     'L1_ffn_gate_w': 8.0,
     'L1_ffn_weight1': 8.0,
     'L1_ffn_weight2': 8.0}
    for name, (base, spread) in spreads.items():
        noise = np.random.default_rng([zlib.crc32(name.encode()), seed]).standard_normal(out[name].shape)
        drawn = base * np.exp(spread * noise) if base else spread * noise
        out[name] = jnp.asarray(drawn.astype(out[name].dtype))
    for name, factor in factors.items():
        out[name] = (out[name] * factor).astype(out[name].dtype)
    return out
```

```python
from contextlib import ExitStack

import concourse.bass as bass
from concourse import mybir
import numpy as np

F32 = mybir.dt.float32
ALU = mybir.AluOpType
ACT = mybir.ActivationFunctionType
AX = mybir.AxisListType

B, H, W, C = 64, 56, 56, 128
TOKENS = H * W

WS = 7
SHIFT = WS // 2
HEADS, HEAD_DIM = 4, 32
QK_SCALE = HEADS ** -0.5
WIN = WS * WS
WROWS, WCOLS = H // WS, W // WS
STRIP = WS * W
SP4 = STRIP // 4
PAIRS = WCOLS // 2
UPPER = 64
ROWS2 = UPPER + WIN
HALF = PAIRS // 2 * HEADS * WIN
MASKED = -1e30


def wait(eng, sem, value):
    if isinstance(value, int) and value <= 0:
        return
    eng.wait_ge(sem, value)


def clear(nc, semaphores):
    block = nc.Block()
    with block:
        @block.gpsimd
        def _(pool):
            for semaphore in semaphores:
                pool.sem_clear(semaphore)


def phase_block(nc, ctx, semaphores):
    ctx.callback(clear, nc, semaphores)
    return ctx.enter_context(nc.Block())


def make_identity(pool, ident, filled, ready):
    pool.memset(ident[:, :], 0.0).then_inc(filled, 1)
    pool.wait_ge(filled, 1)
    pool.affine_select(out=ident[:, :], in_=ident[:, :], compare_op=ALU.not_equal, fill=1.0, base=0,
                       pattern=[[-1, 128]], channel_multiplier=1).then_inc(ready, 1)


def attention_phase(nc, x, w_qkv_t, pos, pos_rows, mask, head_own, w_out_t, b_out, x1, gram):
    N = B * WROWS
    nc.disable_value_cache = True
    with ExitStack() as ctx:
        def sb(name, shape):
            return ctx.enter_context(nc.sbuf_tensor("a_" + name, shape, F32))

        def bank(name):
            return ctx.enter_context(nc.psum_tensor("a_" + name, [128, 512], F32))

        semaphores = []

        def sem(name):
            semaphores.append(ctx.enter_context(nc.semaphore("a_" + name)))
            return semaphores[-1]

        ident = sb("ident", [128, 128])
        wqkv = sb("wqkv", [128, 3 * C])
        wout = sb("wout", [128, C])
        bout = sb("bout", [SP4, 4, C])
        bias49 = sb("bias49", [ROWS2, WIN])
        masks = sb("masks", [ROWS2, 2, PAIRS, WIN])
        bias = sb("bias", [ROWS2, 2, PAIRS, HEADS, WIN])
        half_neg = sb("half_neg", [128, 4])
        eps5 = sb("eps5", [128, 4])
        eps6 = sb("eps6", [128, 4])
        carrier = sb("carrier", [128, 2])
        own = sb("own", [128, HEADS])
        X = sb("X", [SP4, WROWS, 4, C])
        X1 = sb("X1", [SP4, WROWS, 4, C])
        bn1 = sb("bn1", [SP4, 4, 6])
        mv1 = sb("mv1", [SP4, 2, 4, 2])
        ve1 = sb("ve1", [SP4, 4])
        rs1 = sb("rs1", [SP4, 2, 4])
        bn2 = sb("bn2", [SP4, 4, 6])
        mv2 = sb("mv2", [SP4, 2, 4, 2])
        ve2 = sb("ve2", [SP4, 4])
        minus = sb("minus", [SP4, 4])
        nb2 = sb("nb2", [SP4, 2, 4])
        rs2 = sb("rs2", [SP4, 2, 4])
        xn = sb("xn", [SP4, 2, 4, C])
        xg = sb("xg", [SP4, 2, 4, C + 1])
        xT = sb("xT", [128, 2, STRIP])
        qT = sb("qT", [128, 2, STRIP])
        kT = sb("kT", [128, STRIP])
        kh = sb("kh", [128, 2, WCOLS, HEADS, WIN])
        vh = sb("vh", [ROWS2, 4, WCOLS, 2, 64])
        sc = sb("sc", [ROWS2, 2, 8, WIN])
        nmax = sb("nmax", [ROWS2, 2, 8])
        psum_ = sb("psum", [ROWS2, 2, 8])
        prec = sb("prec", [ROWS2, 2, 8])
        pr = sb("pr", [ROWS2, 2, 8, 64])
        prT = sb("prT", [ROWS2, 2, 4, ROWS2])
        aT = sb("aT", [128, STRIP])

        t_bank, qk_bank, v_bank, pt_bank, av_bank, out_bank = [bank(n) for n in ("t", "qk", "v", "pt", "av", "out")]
        s_bank = [bank("s0"), bank("s1")]

        names = """eps_ready ident_zero ident_ready const_landed pos_stored bias_landed zeroed bias_ready
            stats1 aggr1 var1 rstd1 xn_ready residual_ready
            xT_psum xT_ready k_psum k_ready kh_ready q_psum q_ready v_psum v_ready
            s_psum s_biased s_max s_shifted p_exp p_sum p_recip p_ready pt_psum pt_ready
            av_psum aT_ready out_psum x1_ready stats2 aggr2 var2 inv2 rstd2 xg_ready gram_psum gram_added
            gram_zero""".split()
        S = {n: sem(n) for n in names}
        x_landed = [sem(f"x_landed{i}") for i in range(WROWS)]
        x1_stored = [sem(f"x1_stored{i}") for i in range(WROWS)]

        def strip_dmas(dram, img, wr, tile):
            down = [(0, WS, WS * wr + SHIFT)] if wr < WROWS - 1 else \
                   [(0, WS - SHIFT, WS * wr + SHIFT), (WS - SHIFT, WS, 0)]
            for r0, r1, y in down:
                yield (dram[img, y:y + r1 - r0].rearrange("r (q k) c -> (r q) (k c)", k=4),
                       tile[W // 4 * r0:W // 4 * r1, wr].rearrange("p k c -> p (k c)"))

        def window_order(image, strip):
            rows = image.rearrange("c (r y) -> c r y", r=WS)
            inner = rows[:, :, SHIFT:SHIFT + (WCOLS - 1) * WS].rearrange("c r (w k) -> c w r k", w=WCOLS - 1)
            windows = strip.rearrange("c (w r k) -> c w r k", w=WCOLS, r=WS)
            return [(inner, windows[:, 0:WCOLS - 1]),
                    (rows[:, :, W - WS + SHIFT:W], windows[:, WCOLS - 1, :, 0:WS - SHIFT]),
                    (rows[:, :, 0:SHIFT], windows[:, WCOLS - 1, :, WS - SHIFT:WS])]

        COUNT = [16] * (WROWS - 1) + [32]

        def load(sp, img, wr):
            for d, s in strip_dmas(x, img, wr, X):
                sp.dma_start(s, d).then_inc(x_landed[wr], 16)

        def store(sp, img, wr):
            for d, s in strip_dmas(x1, img, wr, X1):
                sp.dma_start(d, s).then_inc(x1_stored[wr], 16)

        def turns(eng, turn):
            def span(img, lo, hi, base):
                for wr in range(lo, hi):
                    turn(img, wr, lambda o, n=base + wr: 0 <= n + o < N)
            span(-1, WROWS - 4, WROWS, -WROWS)
            span(0, 0, WROWS, 0)
            with eng.Fori(1, B - 1) as img:
                for wr in range(WROWS):
                    turn(img, wr, lambda o: True)
            span(B - 1, 0, WROWS, WROWS * (B - 1))
            span(B, 0, 3, N)

        def at(img, wr):
            return img + wr // WROWS, wr % WROWS

        block = phase_block(nc, ctx, semaphores)

        @block.sync
        def _(sp):
            sp.dma_start(wqkv[:, :], w_qkv_t).then_inc(S["const_landed"], 16)
            sp.dma_start(wout[:, :], w_out_t).then_inc(S["const_landed"], 16)
            sp.dma_start(bout[:, :, :], bass.AP(b_out.tensor, 0, [[0, SP4], [0, 4], [1, C]])).then_inc(S["const_landed"], 16)
            sp.dma_start(own[:, :], head_own).then_inc(S["const_landed"], 16)
            sp.dma_start(masks[:, :, :, :], mask).then_inc(S["const_landed"], 16)
            wide = 2 * WS - 1
            sp.dma_start(pos_rows.rearrange("a r b -> r a b"), bass.AP(pos.tensor, WS - 1, [[wide, wide], [-1, WS], [1, WS]])
                         ).then_inc(S["pos_stored"], 16)
            sp.wait_ge(S["pos_stored"], 16)
            sp.wait_ge(S["zeroed"], 1)
            for u in range(2):
                for xi in range(WS):
                    p = UPPER * u + WS * xi
                    sp.dma_start(bias49[p:p + WS, :].rearrange("p (a b) -> p a b", a=WS), pos_rows[:, WS - 1 - xi:2 * WS - 1 - xi, :]
                                 ).then_inc(S["bias_landed"], 16)

            def turn(img, wr, has):
                n = WROWS * img + wr
                if has(4):
                    wait(sp, S["x1_ready"], n + 4 - WROWS + 1)
                    load(sp, *at(img, wr + 4))
                if has(-1):
                    i, w = at(img, wr - 1)
                    wait(sp, S["x1_ready"], n)
                    store(sp, i, w)
            turns(sp, turn)
            for w in range(WROWS):
                sp.wait_ge(x1_stored[w], COUNT[w] * B)

        @block.gpsimd
        def _(pool):
            make_identity(pool, ident, S["ident_zero"], S["ident_ready"])
            pool.memset(half_neg[:, :], -0.5)
            pool.memset(eps5[:, :], 1e-5)
            pool.memset(eps6[:, :], 1e-6).then_inc(S["eps_ready"], 1)
            pool.wait_ge(S["eps_ready"], 1)
            pool.wait_ge(S["const_landed"], 80)

            def turn(img, wr, has):
                n = WROWS * img + wr

                def rstd(o, mv, ve, rs, eps, stats, var, ready):
                    m, b = n + o, (wr + o) % 2
                    pool.wait_ge(S[stats], m + 1)
                    op = pool.tensor_tensor(ve[:, :], mv[:, b, :, 1], eps[0:SP4, :], ALU.add)
                    if o == -1:
                        op = pool.tensor_scalar(minus[:, :], mv[:, b, :, 0], -1.0, 1.0, ALU.mult, ALU.mult)
                    op.then_inc(S[var], 1)
                    pool.wait_ge(S[var], m + 1)
                    pool.tensor_tensor(rs[:, b, :], ve[:, :], half_neg[0:SP4, :], ALU.pow).then_inc(S[ready], 1)

                if has(2):
                    rstd(2, mv1, ve1, rs1, eps6, "aggr1", "var1", "rstd1")
                if has(0):
                    for h in range(2):
                        pool.wait_ge(S["s_max"], 2 * n + h + 1)
                        pool.tensor_tensor(sc[:, h, :, :], sc[:, h, :, :],
                                           nmax[:, h, :].unsqueeze(2).to_broadcast([ROWS2, 8, WIN]),
                                           ALU.add).then_inc(S["s_shifted"], 1)
                if has(1):
                    m, b = n + 1, (wr + 1) % 2
                    wait(pool, S["s_psum"], 2 * (m - 1))
                    pool.wait_ge(S["k_ready"], m + 1)
                    pool.tensor_tensor(carrier[:, 1:2], half_neg[:, 0:1], half_neg[:, 1:2], ALU.mult)
                    for h in range(HEADS):
                        op = pool.tensor_scalar(kh[:, b, :, h, :], kT[:, :].rearrange("p (w k) -> p w k", w=WCOLS),
                                                own[:, h:h + 1], 1.0, ALU.mult, ALU.mult)
                    op.then_inc(S["kh_ready"], 1)
                if has(0):
                    for h in range(2):
                        pool.wait_ge(S["p_recip"], 2 * n + h + 1)
                        pool.tensor_tensor(pr[:, h, :, 0:WIN], pr[:, h, :, 0:WIN],
                                           prec[:, h, :].unsqueeze(2).to_broadcast([ROWS2, 8, WIN]),
                                           ALU.mult).then_inc(S["p_ready"], 1)
                if has(-1):
                    rstd(-1, mv2, ve2, rs2, eps5, "aggr2", "var2", "inv2")
                    pool.wait_ge(S["inv2"], n)
                    b = (wr - 1) % 2
                    pool.tensor_tensor(nb2[:, b, :], minus[:, :], rs2[:, b, :], ALU.mult).then_inc(S["rstd2"], 1)
            turns(pool, turn)

        @block.scalar
        def _(act):
            def turn(img, wr, has):
                n = WROWS * img + wr
                b1 = (wr + 1) % 2

                def turn_probs(h):
                    act.wait_ge(S["pt_psum"], 2 * (n - 1) + h + 1)
                    act.copy(prT[:, h, :, :], pt_bank[0:ROWS2, 0:4 * ROWS2].rearrange("p (a b) -> p a b", a=4)).then_inc(S["pt_ready"], 1)

                def exps(h):
                    act.wait_ge(S["s_shifted"], 2 * n + h + 1)
                    act.activation(pr[:, h, :, 0:WIN], sc[:, h, :, :], ACT.Exp).then_inc(S["p_exp"], 1)

                if has(1):
                    act.wait_ge(S["xT_psum"], n + 2)
                    for rows, windows in window_order(t_bank[:, 0:STRIP], xT[:, b1, :]):
                        op = act.copy(windows, rows)
                    op.then_inc(S["xT_ready"], 1)
                if has(-1):
                    turn_probs(0)
                if has(-2):
                    act.wait_ge(S["rstd2"], n - 1)
                    wait(act, S["gram_psum"], n - 3)
                    for k in range(4):
                        op = act.activation(xg[:, wr % 2, k, 0:C], X1[:, (wr - 2) % WROWS, k, :], ACT.Identity,
                                            bias=nb2[:, wr % 2, k:k + 1], scale=rs2[:, wr % 2, k:k + 1])
                    op.then_inc(S["xg_ready"], 1)
                if has(1):
                    act.wait_ge(S["k_psum"], n + 2)
                    wait(act, S["kh_ready"], n + 1)
                    act.copy(kT[:, :], qk_bank[:, 0:STRIP]).then_inc(S["k_ready"], 1)
                if has(0):
                    exps(0)
                if has(-1):
                    turn_probs(1)
                if has(1):
                    act.wait_ge(S["v_psum"], n + 2)
                    act.copy(vh[0:WIN, (wr + 1) % 4, :, :, 0:HEAD_DIM].rearrange("p w a d -> p (w a) d"),
                             v_bank[0:WIN, :].rearrange("p (w d) -> p w d", d=HEAD_DIM))
                    act.copy(vh[UPPER:ROWS2, (wr + 1) % 4, :, :, HEAD_DIM:64].rearrange("p w a d -> p (w a) d"),
                             v_bank[UPPER:ROWS2, :].rearrange("p (w d) -> p w d", d=HEAD_DIM)).then_inc(S["v_ready"], 1)
                    act.wait_ge(S["q_psum"], n + 2)
                    act.activation(qT[:, b1, :], qk_bank[:, 0:STRIP], ACT.Copy, scale=QK_SCALE).then_inc(S["q_ready"], 1)
                if has(0):
                    exps(1)
                if has(-1):
                    act.wait_ge(S["av_psum"], n)
                    wait(act, S["out_psum"], n - 1)
                    for rows, windows in window_order(aT[:, :], av_bank[:, 0:STRIP]):
                        op = act.copy(rows, windows)
                    op.then_inc(S["aT_ready"], 1)
            act.wait_ge(S["zeroed"], 1)
            turns(act, turn)

        @block.vector
        def _(dve):
            dve.memset(pr[:, :, :, :], 0.0)
            dve.memset(vh[:, :, :, :, :], 0.0)
            dve.memset(xg[:, :, :, C:C + 1], 1.0)
            dve.memset(gram[:, :], 0.0)
            dve.memset(s_bank[0][:, :], 0.0)
            dve.memset(s_bank[1][:, :], 0.0)
            dve.memset(bias49[:, :], 0.0).then_inc(S["zeroed"], 1)
            dve.wait_ge(S["const_landed"], 80)
            dve.wait_ge(S["bias_landed"], 16 * 2 * WS)
            for kind in range(2):
                for g in range(PAIRS):
                    op = dve.tensor_tensor(bias[:, kind, g], masks[:, kind, g].unsqueeze(1).to_broadcast([ROWS2, HEADS, WIN]),
                                           bias49[:, :].unsqueeze(1).to_broadcast([ROWS2, HEADS, WIN]), ALU.add)
            op.then_inc(S["bias_ready"], 1)
            dve.wait_ge(S["bias_ready"], 1)

            def turn(img, wr, has):
                n = WROWS * img + wr

                def stats(o, tile, bn, mv, done, aggr):
                    m, b, slot = n + o, (wr + o) % 2, (wr + o) % WROWS
                    for k in range(4):
                        op = dve.bn_stats(bn[:, k, :], tile[:, slot, k, :])
                    op.then_inc(S[done], 1)
                    dve.wait_ge(S[done], m + 1)
                    dve.memset(carrier[:, 0:1], 0.0)
                    for k in range(4):
                        op = dve.bn_aggr(mv[:, b, k, :], bn[:, k, :])
                    op.then_inc(S[aggr], 1)

                def normalise(o, tile, mv, rs, out, ready, done):
                    m, b, slot = n + o, (wr + o) % 2, (wr + o) % WROWS
                    dve.wait_ge(S[ready], m + 1)
                    for k in range(4):
                        op = dve.tensor_scalar(out[:, b, k, 0:C], tile[:, slot, k, :], mv[:, b, k, 0:1], rs[:, b, k:k + 1],
                                               ALU.subtract, ALU.mult)
                    op.then_inc(S[done], 1)

                if has(2):
                    i, w = at(img, wr + 2)
                    dve.wait_ge(x_landed[w], COUNT[w] * (i + 1))
                    stats(2, X, bn1, mv1, "stats1", "aggr1")
                if has(0):
                    for h in range(2):
                        dve.wait_ge(S["s_psum"], 2 * n + h + 1)
                        wait(dve, S["p_exp"], 2 * n + h - 1)
                        kind = int(wr == WROWS - 1)
                        dve.tensor_tensor(sc[:, h, :, :].rearrange("p a b -> p (a b)"), s_bank[h][0:ROWS2, 0:HALF],
                                          bias[:, kind, 2 * h:2 * h + 2].rearrange("p g a b -> p (g a b)"), ALU.add).then_inc(S["s_biased"], 1)
                        dve.wait_ge(S["s_biased"], 2 * n + h + 1)
                        dve.tensor_reduce(nmax[:, h, :], sc[:, h, :, :], AX.X, ALU.max, negate=True).then_inc(S["s_max"], 1)
                if has(2):
                    wait(dve, S["xT_psum"], n + 1)
                    normalise(2, X, mv1, rs1, xn, "rstd1", "xn_ready")
                    dve.wait_ge(S["xn_ready"], n + 3)
                    dve.tensor_tensor(X[:, (wr + 2) % WROWS], X[:, (wr + 2) % WROWS], bout[:, :, :], ALU.add).then_inc(S["residual_ready"], 1)
                if has(0):
                    for h in range(2):
                        dve.wait_ge(S["p_exp"], 2 * n + h + 1)
                        dve.tensor_reduce(psum_[:, h, :], pr[:, h, :, 0:WIN], AX.X, ALU.add).then_inc(S["p_sum"], 1)
                        dve.wait_ge(S["p_sum"], 2 * n + h + 1)
                        dve.reciprocal(prec[:, h, :], psum_[:, h, :]).then_inc(S["p_recip"], 1)
                if has(-2):
                    dve.wait_ge(S["gram_psum"], n - 1)
                    wait(dve, S["gram_added"], n - 2)
                    dve.tensor_tensor(gram[:, :], t_bank[:, 0:C + 1], gram[:, :], ALU.add).then_inc(S["gram_added"], 1)
                if has(-1):
                    i, w = at(img, wr - 1)
                    dve.wait_ge(S["out_psum"], n)
                    dve.wait_ge(S["residual_ready"], n)
                    wait(dve, x1_stored[w], COUNT[w] * i)
                    dve.tensor_tensor(X1[:, w].rearrange("p k c -> p (k c)"), out_bank[0:SP4, :],
                                      X[:, w].rearrange("p k c -> p (k c)"), ALU.add).then_inc(S["x1_ready"], 1)
                    dve.wait_ge(S["x1_ready"], n)
                    stats(-1, X1, bn2, mv2, "stats2", "aggr2")
            turns(dve, turn)
            dve.wait_ge(S["gram_added"], N)

        @block.tensor
        def _(pe):
            pe.wait_ge(S["ident_ready"], 1)
            pe.wait_ge(S["const_landed"], 80)
            pe.wait_ge(S["zeroed"], 1)

            def turn(img, wr, has):
                n = WROWS * img + wr
                b0, b1 = wr % 2, (wr + 1) % 2

                def scores(h):
                    pe.wait_ge(S["kh_ready"], n + 1)
                    pe.wait_ge(S["q_ready"], n + 1)
                    wait(pe, S["s_biased"], 2 * n + h - 1)
                    for g in range(2):
                        for u in range(2):
                            w = 4 * h + 2 * g + u
                            op = pe.matmul(s_bank[h][UPPER * u:UPPER * u + WIN, HALF // 2 * g:HALF // 2 * (g + 1)],
                                           qT[:, b0, WIN * w:WIN * (w + 1)], kh[:, b0, w].rearrange("c h k -> c (h k)"), start=True, stop=True)
                    op.then_inc(S["s_psum"], 1)

                def turn_probs(h):
                    m = n - 1
                    pe.wait_ge(S["p_ready"], 2 * m + h + 1)
                    wait(pe, S["pt_ready"], 2 * m + h)
                    for g in range(2):
                        for a in range(2):
                            q = 2 * g + a
                            op = pe.transpose(pt_bank[:, q * ROWS2:(q + 1) * ROWS2],
                                              pr[:, h, 4 * g + 2 * a:4 * g + 2 * a + 2, :].rearrange("p a b -> p (a b)"),
                                              ident[0:ROWS2, 0:ROWS2])
                    op.then_inc(S["pt_psum"], 1)

                def attend(h):
                    m, b = n - 1, (wr - 1) % 4
                    pe.wait_ge(S["pt_ready"], 2 * m + h + 1)
                    if h == 0:
                        pe.wait_ge(S["v_ready"], m + 1)
                        wait(pe, S["aT_ready"], m)
                    for g in range(2):
                        for u in range(2):
                            w = 4 * h + 2 * g + u
                            for a in range(2):
                                op = pe.matmul(av_bank[64 * a:64 * (a + 1), w * WIN:(w + 1) * WIN], vh[:, b, w, a, :],
                                               prT[:, h, 2 * g + a, UPPER * u:UPPER * u + WIN], start=True, stop=True)
                    if h == 1:
                        op.then_inc(S["av_psum"], 1)

                if has(1):
                    pe.wait_ge(S["xn_ready"], n + 2)
                    wait(pe, S["gram_added"], n - 2)
                    for k in range(4):
                        op = pe.transpose(t_bank[:, k:STRIP:4], xn[:, b1, k, :], ident[0:SP4, 0:SP4])
                    op.then_inc(S["xT_psum"], 1)
                if has(0):
                    scores(0)
                if has(-1):
                    turn_probs(0)
                if has(0):
                    scores(1)
                if has(1):
                    pe.wait_ge(S["xT_ready"], n + 2)
                    wait(pe, S["q_ready"], n + 1)
                    pe.matmul(qk_bank[:, 0:STRIP], wqkv[:, C:2 * C], xT[:, b1, :], start=True, stop=True).then_inc(S["k_psum"], 1)
                if has(-1):
                    attend(0)
                    turn_probs(1)
                if has(1):
                    wait(pe, S["v_ready"], n + 1)
                    for w in range(WCOLS):
                        for e in range(2):
                            op = pe.matmul(v_bank[UPPER * e:UPPER * e + WIN, 64 * w:64 * (w + 1)], xT[:, b1, WIN * w:WIN * (w + 1)],
                                           wqkv[:, 2 * C:].rearrange("c (a e d) -> c e a d", a=2, e=2)[:, e], start=True, stop=True)
                    op.then_inc(S["v_psum"], 1)
                    pe.wait_ge(S["k_ready"], n + 2)
                    pe.matmul(qk_bank[:, 0:STRIP], wqkv[:, 0:C], xT[:, b1, :], start=True, stop=True).then_inc(S["q_psum"], 1)
                if has(-1):
                    attend(1)
                if has(-2):
                    pe.wait_ge(S["xg_ready"], n - 1)
                    for k in range(4):
                        op = pe.matmul(t_bank[:, 0:C + 1], xg[:, wr % 2, k, 0:C], xg[:, wr % 2, k, :], start=k == 0, stop=k == 3)
                    op.then_inc(S["gram_psum"], 1)
                if has(-1):
                    pe.wait_ge(S["aT_ready"], n)
                    wait(pe, S["x1_ready"], n - 1)
                    for k in range(4):
                        op = pe.matmul(out_bank[0:SP4, k * C:(k + 1) * C], aT[:, k::4], wout[:, :], start=True, stop=True)
                    op.then_inc(S["out_psum"], 1)
            turns(pe, turn)


def head_channels():
    return np.repeat(np.eye(HEADS, dtype=np.float32), HEAD_DIM, 0)


def window_masks():
    m = np.zeros((ROWS2, 2, PAIRS, WIN), np.float32)
    r, c = np.divmod(np.arange(WIN), WS)
    low, right = r >= WS - SHIFT, c >= WS - SHIFT
    up_down = low[:, None] != low[None, :]
    left_right = right[:, None] != right[None, :]
    for kind in range(2):
        for g in range(PAIRS):
            for u in range(2):
                bad = np.zeros((WIN, WIN), bool)
                if kind == 1:
                    bad |= up_down
                if g == PAIRS - 1 and u == 1:
                    bad |= left_right
                m[UPPER * u:UPPER * u + WIN, kind, g][bad] = MASKED
    return m


BF16 = mybir.dt.bfloat16
STEPS = 32
RUN = STEPS // 2
CHUNKS = TOKENS // STEPS
PART = B // 2


def recurrent_phase(nc, x1, w, w_t, v_t, gamma, beta, gram, x2, xc):
    nc.disable_value_cache = True
    with ExitStack() as ctx:
        def sb(name, shape, dt=F32):
            return ctx.enter_context(nc.sbuf_tensor("r_" + name, shape, dt))

        def bank(name):
            return ctx.enter_context(nc.psum_tensor("r_" + name, [128, 512], F32))

        semaphores = []

        def sem(name):
            semaphores.append(ctx.enter_context(nc.semaphore("r_" + name)))
            return semaphores[-1]

        ident = sb("ident", [128, 128])
        wn = sb("wn", [128, C])
        wt = sb("wt", [128, C])
        vt = sb("vt", [128, C])
        gb = sb("gb", [128, 2])
        ones = sb("ones", [128, 1])
        ones3 = sb("ones3", [3, 512], BF16)
        prod = sb("prod", [128, C])
        mom = sb("mom", [128, 4])
        col = sb("col", [128, 8])
        half_neg = sb("half_neg", [128, RUN])
        eps5 = sb("eps5", [128, RUN])
        eps6 = sb("eps6", [128, RUN])
        carrier = sb("carrier", [128, 2])
        ws = sb("ws", [128, C])
        wst = sb("wst", [128, C])
        part16 = sb("part16", [128, 4], BF16)
        parts = sb("parts", [128, 3])
        shift = sb("shift", [3, C], BF16)
        X = sb("X", [128, 4, RUN, C])
        xn = sb("xn", [128, 2, RUN, C])
        xT = sb("xT", [128, 2, 2, 2, RUN, PART])
        Y = sb("Y", [128, 2, RUN, 2, B])
        X2 = sb("X2", [128, 2, RUN, C])
        XC = sb("XC", [128, 2, RUN, C])
        bn = [sb("bn1", [128, RUN, 6]), sb("bn2", [128, RUN, 6])]
        mv = [sb("mv1", [128, RUN, 2]), sb("mv2", [128, RUN, 2])]
        ve = [sb("ve1", [128, RUN]), sb("ve2", [128, RUN])]
        rs = [sb("rs1", [128, RUN]), sb("rs2", [128, RUN])]
        nm = [sb("nm1", [128, RUN]), sb("nm2", [128, RUN])]
        nb = [sb("nb1", [128, RUN]), sb("nb2", [128, RUN])]

        z_bank = [[bank(f"z{a}{s}") for s in range(2)] for a in range(2)]
        t_bank = [bank("t0"), bank("t1")]
        o_bank = [bank("o0"), bank("o1")]

        names = """eps_ready ident_zero ident_ready const_landed zeroed moments prod_ready sums col_step
            scaled transposed parts_ready parts_turned shift_ready bn_norm
            t_psum xT_ready o_psum x2_ready stats1 aggr1 stats2 aggr2
            var1 inv1 nb1 xn_ready var2 inv2 nb2 xc_ready z0 z1 y0 y1""".split()
        S = {n: sem(n) for n in names}
        x_landed = [sem(f"x_landed{i}") for i in range(4)]
        x2_stored = [sem(f"x2_stored{i}") for i in range(2)]
        xc_stored = [sem(f"xc_stored{i}") for i in range(2)]
        z_psum, y_ready = [S["z0"], S["z1"]], [S["y0"], S["y1"]]

        def turns(eng, turn):
            def one(q):
                turn(q, q % 4, lambda o: 0 <= q + o < CHUNKS)
            for q in range(-3, 2):
                one(q)
            with eng.Fori(0, (CHUNKS - 6) // 4) as i:
                for j in range(2, 6):
                    turn(4 * i + j, j % 4, lambda o: True)
            for q in range(CHUNKS - 4, CHUNKS + 2):
                one(q)

        def chunk(dram, q, s):
            return dram.rearrange("b h w c -> b (h w) c").rearrange("b (n k) c -> b n k c", k=RUN)[:, 2 * q + s]

        block = phase_block(nc, ctx, semaphores)

        @block.sync
        def _(sp):
            for dst, src in ((wn, w), (wt, w_t), (vt, v_t)):
                sp.dma_start(dst[:, :], src).then_inc(S["const_landed"], 16)
            for i, src in enumerate((gamma, beta)):
                sp.dma_start(gb[:, i:i + 1], src.rearrange("(p a) -> p a", a=1)).then_inc(S["const_landed"], 16)

            def turn(q, j, has):
                if has(3):
                    wait(sp, S["x2_ready"], 4 * q)
                    for s in range(2):
                        sp.dma_start(X[B * s:B * (s + 1), (j + 3) % 4], chunk(x1, q + 3, s)).then_inc(x_landed[(j + 3) % 4], 16)
                if has(-1):
                    wait(sp, S["x2_ready"], 4 * q)
                    for s in range(2):
                        sp.dma_start(chunk(x2, q - 1, s), X2[B * s:B * (s + 1), (j - 1) % 2]).then_inc(x2_stored[(j - 1) % 2], 16)
                if has(-2):
                    wait(sp, S["xc_ready"], q - 1)
                    for s in range(2):
                        sp.dma_start(chunk(xc, q - 2, s), XC[B * s:B * (s + 1), j % 2]).then_inc(xc_stored[j % 2], 16)
            turns(sp, turn)
            for i in range(2):
                sp.wait_ge(x2_stored[i], 16 * CHUNKS)
                sp.wait_ge(xc_stored[i], 16 * CHUNKS)

        @block.gpsimd
        def _(pool):
            make_identity(pool, ident, S["ident_zero"], S["ident_ready"])
            pool.memset(half_neg[:, :], -0.5)
            pool.memset(eps5[:, :], 1e-5)
            pool.memset(eps6[:, :], 1e-6).then_inc(S["eps_ready"], 1)
            pool.wait_ge(S["eps_ready"], 1)
            pool.wait_ge(S["sums"], 2)
            pool.tensor_tensor(mom[:, 3:4], mom[:, 2:3], half_neg[:, 0:1], ALU.pow).then_inc(S["bn_norm"], 1)

            def turn(q, j, has):
                def normalise(w, o, m, eps, src, dst, done):
                    a, b, c = f"var{w + 1}", f"inv{w + 1}", f"nb{w + 1}"
                    pool.wait_ge(S[f"aggr{w + 1}"], m + 1)
                    pool.tensor_tensor(ve[w][:, :], mv[w][:, :, 1], eps[:, :], ALU.add)
                    pool.tensor_scalar(nm[w][:, :], mv[w][:, :, 0], -1.0, 1.0, ALU.mult, ALU.mult).then_inc(S[a], 1)
                    pool.wait_ge(S[a], m + 1)
                    pool.tensor_tensor(rs[w][:, :], ve[w][:, :], half_neg[:, :], ALU.pow).then_inc(S[b], 1)
                    pool.wait_ge(S[b], m + 1)
                    pool.tensor_tensor(nb[w][:, :], nm[w][:, :], rs[w][:, :], ALU.mult).then_inc(S[c], 1)
                    pool.wait_ge(S[c], m + 1)
                    pool.tensor_tensor(carrier[:, 0:1], half_neg[:, 0:1], half_neg[:, 1:2], ALU.mult)
                    for k in range(RUN):
                        op = pool.tensor_scalar(dst[:, k, :], src[:, k, :], rs[w][:, k:k + 1], nb[w][:, k:k + 1], ALU.mult, ALU.add)
                    op.then_inc(S[done], 1)
                if has(-2):
                    wait(pool, xc_stored[j % 2], 16 * (q - 2) if j % 2 == 0 else 16 * (q - 3))
                    normalise(1, -2, q - 2, eps6, X2[:, j % 2], XC[:, j % 2], "xc_ready")
                if has(2):
                    wait(pool, S["t_psum"], 4 * (q + 1))
                    normalise(0, 2, q + 2, eps5, X[:, (j + 2) % 4], xn[:, j % 2], "xn_ready")
            turns(pool, turn)

        @block.scalar
        def _(act):
            def turn(q, j, has):
                if has(0):
                    for t in range(STEPS):
                        for a in range(2):
                            act.wait_ge(z_psum[a], STEPS * q + t + 1)
                            act.activation(Y[:, j % 2, t % RUN, t // RUN, PART * a:PART * (a + 1)],
                                           z_bank[a][t // RUN][:, PART * (t % RUN):PART * (t % RUN + 1)], ACT.Sigmoid
                                           ).then_inc(y_ready[a], 1)
            turns(act, turn)

        @block.vector
        def _(dve):
            inv_n = 1.0 / (B * TOKENS)
            dve.memset(ones[:, :], 1.0)
            dve.memset(ones3[:, :], 1.0)
            dve.memset(Y[:, 1, RUN - 1, 1, :], 0.0).then_inc(S["zeroed"], 1)
            dve.wait_ge(S["const_landed"], 80)
            dve.wait_ge(S["moments"], 1)
            dve.tensor_tensor(prod[:, :], t_bank[0][:, 0:C], wt[:, :], ALU.mult).then_inc(S["prod_ready"], 1)
            dve.wait_ge(S["moments"], 2)
            dve.tensor_scalar(mom[:, 0:2], t_bank[1][:, 0:2], inv_n, None, ALU.mult).then_inc(S["col_step"], 1)
            dve.wait_ge(S["col_step"], 1)
            dve.tensor_tensor(col[:, 0:1], mom[:, 1:2], mom[:, 1:2], ALU.mult).then_inc(S["col_step"], 1)
            dve.wait_ge(S["col_step"], 2)
            dve.tensor_tensor(col[:, 1:2], mom[:, 0:1], col[:, 0:1], ALU.subtract).then_inc(S["col_step"], 1)
            dve.wait_ge(S["col_step"], 3)
            dve.tensor_scalar(mom[:, 2:3], col[:, 1:2], 1e-5, None, ALU.add).then_inc(S["sums"], 2)
            dve.wait_ge(S["bn_norm"], 1)
            dve.tensor_tensor(col[:, 2:3], mom[:, 3:4], gb[:, 0:1], ALU.mult).then_inc(S["col_step"], 1)
            dve.wait_ge(S["col_step"], 4)
            dve.tensor_scalar(ws[:, :], wn[:, :], col[:, 2:3], None, ALU.mult).then_inc(S["scaled"], 1)
            dve.tensor_tensor(col[:, 3:4], mom[:, 1:2], col[:, 2:3], ALU.mult).then_inc(S["col_step"], 1)
            dve.wait_ge(S["col_step"], 5)
            dve.tensor_tensor(col[:, 4:5], gb[:, 1:2], col[:, 3:4], ALU.subtract).then_inc(S["col_step"], 1)
            for i in range(3):
                dve.wait_ge(S["col_step"], 6 + 3 * i)
                dve.tensor_copy(part16[:, i:i + 1], col[:, 4 + i:5 + i]).then_inc(S["col_step"], 1)
                dve.wait_ge(S["col_step"], 7 + 3 * i)
                dve.tensor_copy(parts[:, i:i + 1], part16[:, i:i + 1]).then_inc(S["col_step"], 1)
                dve.wait_ge(S["col_step"], 8 + 3 * i)
                dve.tensor_tensor(col[:, 5 + i:6 + i], col[:, 4 + i:5 + i], parts[:, i:i + 1], ALU.subtract).then_inc(S["col_step"], 1)
            dve.wait_ge(S["col_step"], 15)
            dve.wait_ge(S["transposed"], 1)
            dve.tensor_copy(wst[:, :], o_bank[0][:, 0:C])
            dve.wait_ge(S["transposed"], 2)
            dve.tensor_copy(shift[:, :], o_bank[1][0:3, 0:C]).then_inc(S["shift_ready"], 1)

            def turn(q, j, has):
                for g in range(4):
                    if has(1):
                        dve.wait_ge(S["t_psum"], 4 * (q + 1) + g + 1)
                        src = t_bank[g % 2][:, :].rearrange("c (k s a b) -> c a k s b", k=4, s=2, a=2)
                        for a in range(2):
                            op = dve.tensor_copy(xT[:, (j + 1) % 2, a, :, 4 * g:4 * g + 4, :].rearrange("c s k b -> c k s b"), src[:, a])
                        op.then_inc(S["xT_ready"], 1)
                    if has(2):
                        if g == 0:
                            dve.wait_ge(x_landed[(j + 2) % 4], 32 * ((q + 2) // 4 + 1) if isinstance(q, int) else 8 * (q + 2) - 8 * ((j + 2) % 4) + 32)
                            wait(dve, S["nb1"], q + 2)
                        for k in range(4 * g, 4 * g + 4):
                            op = dve.bn_stats(bn[0][:, k, :], X[:, (j + 2) % 4, k, :])
                if has(2):
                    op.then_inc(S["stats1"], 1)
                    dve.wait_ge(S["stats1"], q + 3)
                    dve.memset(carrier[:, 1:2], 0.0)
                    for k in range(RUN):
                        op = dve.bn_aggr(mv[0][:, k, :], bn[0][:, k, :])
                    op.then_inc(S["aggr1"], 1)
                if has(-1):
                    p = (j - 1) % 2
                    wait(dve, x2_stored[p], (32 * ((q - 1) // 2)) if isinstance(q, int) else 16 * (q - 1) - 16 * p)
                    wait(dve, S["nb2"], q - 1)
                    wait(dve, S["xc_ready"], q - 2)
                    for g in range(4):
                        dve.wait_ge(S["o_psum"], 4 * (q - 1) + g + 1)
                        dve.tensor_tensor(X2[:, p, 4 * g:4 * g + 4, :].rearrange("p k c -> p (k c)"), o_bank[g % 2][:, :],
                                          X[:, (j - 1) % 4, 4 * g:4 * g + 4, :].rearrange("p k c -> p (k c)"), ALU.add
                                          ).then_inc(S["x2_ready"], 1)
                        dve.wait_ge(S["x2_ready"], 4 * (q - 1) + g + 1)
                        for k in range(4 * g, 4 * g + 4):
                            op = dve.bn_stats(bn[1][:, k, :], X2[:, p, k, :])
                    op.then_inc(S["stats2"], 1)
                    dve.wait_ge(S["stats2"], q)
                    dve.memset(carrier[:, 1:2], 0.0)
                    for k in range(RUN):
                        op = dve.bn_aggr(mv[1][:, k, :], bn[1][:, k, :])
                    op.then_inc(S["aggr2"], 1)
            turns(dve, turn)

        @block.tensor
        def _(pe):
            pe.wait_ge(S["const_landed"], 80)
            pe.wait_ge(S["zeroed"], 1)
            pe.matmul(t_bank[0][:, 0:C], gram[:, 0:C], wt[:, :], start=True, stop=True).then_inc(S["moments"], 1)
            pe.wait_ge(S["prod_ready"], 1)
            pe.matmul(t_bank[1][:, 0:1], prod[:, :], ones[:, :], start=True, stop=True)
            pe.matmul(t_bank[1][:, 1:2], wt[:, :], gram[:, C:C + 1], start=True, stop=True).then_inc(S["moments"], 1)
            pe.wait_ge(S["ident_ready"], 1)
            pe.wait_ge(S["scaled"], 1)
            pe.transpose(o_bank[0][:, 0:C], ws[:, :], ident[:, :]).then_inc(S["transposed"], 1)
            pe.wait_ge(S["col_step"], 15)
            pe.transpose(o_bank[1][0:3, 0:C], parts[:, :], ident[:, :]).then_inc(S["transposed"], 1)
            pe.wait_ge(S["shift_ready"], 1)

            def turn(q, j, has):
                def turn_in(k):
                    if k == 0:
                        pe.wait_ge(S["xn_ready"], q + 2)
                    if k % 4 == 0:
                        wait(pe, S["xT_ready"], 4 * (q + 1) + k // 4 - 1)
                    g = k // 4
                    op = pe.transpose(t_bank[g % 2][:, C * (k % 4):C * (k % 4 + 1)], xn[:, (j + 1) % 2, k, :], ident[:, :])
                    if k % 4 == 3:
                        op.then_inc(S["t_psum"], 1)

                def turn_out(k):
                    if k == 0:
                        for a in range(2):
                            pe.wait_ge(y_ready[a], STEPS * q)
                    if k % 4 == 0:
                        wait(pe, S["x2_ready"], 4 * (q - 1) + k // 4 - 1)
                    g = k // 4
                    op = pe.transpose(o_bank[g % 2][:, C * (k % 4):C * (k % 4 + 1)],
                                      Y[:, (j - 1) % 2, k].rearrange("c s b -> c (s b)"), ident[:, :])
                    if k % 4 == 3:
                        op.then_inc(S["o_psum"], 1)

                def inputs(o, s, a, piece):
                    bank = z_bank[a][s]
                    if piece == 0:
                        if s == 0:
                            pe.wait_ge(S["xT_ready"], 4 * (q + o) + 4)
                            wait(pe, y_ready[a], STEPS * (q + o) - RUN)
                        else:
                            wait(pe, y_ready[a], STEPS * (q + o))
                        pe.matmul(bank[:, :], shift[:, :], ones3[:, :], start=True, stop=True)
                        return
                    n = RUN * PART // 4
                    cols = slice(n * (piece - 1), n * piece)
                    pe.matmul(bank[:, cols], wst[:, :], xT[:, (j + o) % 2, a, s].rearrange("c k b -> c (k b)")[:, cols],
                              start=False, stop=True, skip_group_check=True)

                def step(t, a):
                    before = Y[:, j % 2, (t - 1) % RUN, (t - 1) // RUN] if t else Y[:, (j - 1) % 2, RUN - 1, 1]
                    wait(pe, y_ready[a], STEPS * q + t)
                    pe.matmul(z_bank[a][t // RUN][:, PART * (t % RUN):PART * (t % RUN + 1)], vt[:, :],
                              before[:, PART * a:PART * (a + 1)], start=False, stop=True, skip_group_check=True
                              ).then_inc(z_psum[a], 1)

                for t in range(STEPS):
                    if has(0):
                        for a in range(2):
                            step(t, a)
                    if has(1) and t < RUN:
                        turn_in(t)
                    if has(-1) and RUN - 1 <= t < 2 * RUN - 1:
                        turn_out(t - (RUN - 1))
                    if has(0) and 2 <= t < 12:
                        inputs(0, 1, *divmod(t - 2, 5))
                    if has(1) and RUN + 3 <= t < RUN + 13:
                        inputs(1, 0, *divmod(t - RUN - 3, 5))
            turns(pe, turn)


KS = 7
REACH = KS // 2
BLOCK = 2 * W
BLOCKS = H // 2
GROUP = 8
GROUPS = B // GROUP
SLOTS = BLOCKS + 3
NPIX = GROUP * BLOCKS
CHUNK = 4
TAPS = KS + 1
TZ = TAPS * W
SCAN = 8
EPS = 1e-6
NCORNER = KS * KS * GROUP
CR, CC = 2 * KS, 2 * KS - 1


def expand_phase(nc, k_b, k_gb, rows, toeplitz):
    nc.disable_value_cache = True
    with ExitStack() as ctx:
        kern = ctx.enter_context(nc.sbuf_tensor("e_kern", [128, 2, KS * KS], F32))
        ext = ctx.enter_context(nc.sbuf_tensor("e_ext", [128, 2, TAPS + 1, 2 * W], F32))
        semaphores = [ctx.enter_context(nc.semaphore("e_" + n)) for n in ("landed", "zeroed", "spread", "rows_stored", "stored")]
        landed, zeroed, spread, rows_stored, stored = semaphores
        block = phase_block(nc, ctx, semaphores)

        @block.vector
        def _(dve):
            dve.memset(ext[:, :, :, :], 0.0).then_inc(zeroed, 1)
            dve.wait_ge(zeroed, 1)
            dve.wait_ge(landed, 32)
            for i in range(2):
                k = kern[:, i, :].rearrange("c (a b) -> c a b", a=KS)
                dve.tensor_copy(ext[:, i, 1:1 + KS, W - REACH:W + REACH + 1], k)
                dve.tensor_copy(ext[:, i, 1:1 + KS, 0:REACH + 1], k[:, :, REACH:KS])
                op = dve.tensor_copy(ext[:, i, 1:1 + KS, 2 * W - REACH:2 * W], k[:, :, 0:REACH])
            op.then_inc(spread, 1)

        @block.sync
        def _(sp):
            for i, src in enumerate((k_b, k_gb)):
                sp.dma_start(kern[:, i, :], src.rearrange("c a b -> c (a b)")).then_inc(landed, 16)
            sp.wait_ge(spread, 1)
            sp.dma_start(rows, ext[:, :, :, :]).then_inc(rows_stored, 16)
            sp.wait_ge(rows_stored, 16)
            src = rows.rearrange("c i a b -> (c i) a b")
            for r in range(2):
                with sp.Fori(0, W) as w:
                    sp.dma_start(toeplitz[w + W * r].rearrange("c i (a b) -> (c i) a b", a=TAPS),
                                 src[:, 1 - r:1 - r + TAPS, bass.ds(W - w, W)]).then_inc(stored, 16)
            sp.wait_ge(stored, 16 * 2 * W)


def convolution_phase(nc, xc, x2, toeplitz, k_a, k_ga, w_out, b_out, x3):
    nc.disable_value_cache = True
    with ExitStack() as ctx:
        def sb(name, shape):
            return ctx.enter_context(nc.sbuf_tensor("c_" + name, shape, F32))

        semaphores = []

        def sem(name):
            semaphores.append(ctx.enter_context(nc.semaphore("c_" + name)))
            return semaphores[-1]

        ident = sb("ident", [128, 128])
        wout = sb("wout", [128, C])
        bout = sb("bout", [BLOCK, 4, C])
        ka = sb("ka", [128, KS * KS])
        kga = sb("kga", [128, KS * KS])
        xt = sb("xt", [BLOCK, GROUP, SLOTS, C])
        tz = sb("tz", [BLOCK, 2, CHUNK, 2, TZ])
        e1 = sb("e1", [BLOCK, 2, 2, NPIX])
        bt = sb("bt", [BLOCK, 2, 2, NPIX])
        ab = sb("ab", [BLOCK, 2, 2, NPIX])
        around = sb("around", [128, CR, CC, GROUP])
        tap = sb("tap", [128, 2, NCORNER])
        gate = sb("gate", [128, NCORNER])
        fac = sb("fac", [128, 4, NCORNER])
        hT = sb("hT", [128, 2, 4, BLOCK])
        XR = sb("XR", [BLOCK, 4, 4, C])
        X3 = sb("X3", [BLOCK, 4, 4, C])
        conv = [ctx.enter_context(nc.psum_tensor(f"c_conv{i}", [128, 2, 512], F32)) for i in range(2)]
        th = [ctx.enter_context(nc.psum_tensor(f"c_th{i}", [128, 512], F32)) for i in range(2)]
        ob = [ctx.enter_context(nc.psum_tensor(f"c_ob{i}", [128, 512], F32)) for i in range(2)]

        names = """ident_zero ident_ready const_landed conv_psum gate_exp plus1 recip b_ready abs_ready
            b_exp b_log h_ready turned evacuated around_ready tap_step gated corner_exp corner_step
            corner_ready ob_psum x3_ready residual_ready""".split()
        S = {n: sem(n) for n in names}
        image_landed = [sem(f"image_landed{i}") for i in range(GROUP)]
        tz_landed = [sem(f"tz_landed{i}") for i in range(2)]
        xr_landed = [sem(f"xr_landed{i}") for i in range(4)]
        x3_stored = [sem(f"x3_stored{i}") for i in range(4)]

        PAIRS_G = C // 2
        NEAR = 2 * GROUP
        STRIPS = BLOCKS // 4
        SECOND = GROUP * STRIPS
        TURNS = NEAR + SECOND
        CORNER_STEPS = 10
        near_blocks = [[BLOCKS - 3, BLOCKS - 2, BLOCKS - 1, 0], [1, 2, 3]]

        def second_dmas(s):
            img, k = divmod(s, STRIPS)
            if k < STRIPS - 1:
                return img, [(slice(0, BLOCK), slice(0, 4), 8 * k + 1)]
            return img, [(slice(0, BLOCK), slice(0, 3), 8 * k + 1), (slice(0, W), slice(3, 4), H - 1),
                         (slice(W, BLOCK), slice(3, 4), 0)]
        before = {s: 16 * sum(len(second_dmas(t)[1]) for t in range(s % 4, s, 4)) for s in range(SECOND + 4)}
        whole = [before[SECOND + i] if (SECOND + i) % 4 == i else None for i in range(4)]

        def second_views(dram, tile, g, s):
            img, parts = second_dmas(s)
            for p, k, row in parts:
                rows = (p.stop - p.start) // W
                n = k.stop - k.start
                tokens = dram[g * GROUP + img].rearrange("h w c -> (h w) c")
                yield (bass.AP(tokens.tensor, tokens.offset + row * W * C, [[C, rows * W], [BLOCK * C, n], [1, C]]),
                       tile[p, s % 4, k, :])

        block = phase_block(nc, ctx, semaphores)

        @block.sync
        def _(sp):
            sp.dma_start(wout[:, :], w_out).then_inc(S["const_landed"], 16)
            sp.dma_start(bout[:, :, :], bass.AP(b_out.tensor, 0, [[0, BLOCK], [0, 4], [1, C]])).then_inc(S["const_landed"], 16)
            sp.dma_start(ka[:, :], k_a.rearrange("c a b -> c (a b)")).then_inc(S["const_landed"], 16)
            sp.dma_start(kga[:, :], k_ga.rearrange("c a b -> c (a b)")).then_inc(S["const_landed"], 16)

            def image(g, i):
                src = xc[g * GROUP + i].rearrange("(n r) w c -> (r w) n c", r=2)
                sp.dma_start(xt[:, i, 1:1 + BLOCKS, :], src).then_inc(image_landed[i], 16)
                sp.dma_start(xt[:, i, 0:1, :], src[:, BLOCKS - 1:BLOCKS]).then_inc(image_landed[i], 16)
                sp.dma_start(xt[:, i, 1 + BLOCKS:SLOTS, :], src[:, 0:2]).then_inc(image_landed[i], 16)

            def matrices(g):
                with sp.Fori(0, C // (2 * CHUNK)) as i:
                    for b in range(2):
                        sp.wait_ge(S["b_ready"], PAIRS_G * g + 4 * i + 2 * b + 1)
                        sp.dma_start(tz[:, b].rearrange("p c i t -> p (c i t)"),
                                     toeplitz.rearrange("p (n c) i t -> p n (c i t)", c=CHUNK)[:, 2 * i + b]).then_inc(tz_landed[b], 16)

            for i in range(GROUP):
                image(0, i)
            with sp.Fori(0, GROUPS - 1) as g:
                matrices(g)
                for i in range(GROUP):
                    sp.wait_ge(S["turned"], TURNS * g + NEAR + STRIPS * (i + 1))
                    image(g + 1, i)
            matrices(GROUPS - 1)

        @block.gpsimd
        def _(pool):
            make_identity(pool, ident, S["ident_zero"], S["ident_ready"])
            pool.wait_ge(S["const_landed"], 64)
            with pool.Fori(0, GROUPS) as g:
                pool.wait_ge(S["around_ready"], g + 1)
                pool.tensor_tensor(tap[:, 0, 0:1], ka[:, 0:1], ka[:, 0:1], ALU.mult)
                for t in range(KS * KS):
                    a, b = KS - 1 - t // KS, KS - 1 - t % KS
                    view = around[:, a:a + KS, b:b + KS, :].rearrange("c a b i -> c a (b i)")
                    out = gate[:, :] if t == 0 else tap[:, t % 2, :]
                    pool.tensor_scalar(out.rearrange("c (a b) -> c a b", a=KS), view, kga[:, t:t + 1], 1.0, ALU.mult, ALU.mult
                                       ).then_inc(S["tap_step"], 1)
                    if t:
                        pool.wait_ge(S["tap_step"], 2 * KS * KS * g + 2 * t)
                        pool.tensor_tensor(gate[:, :], gate[:, :], tap[:, t % 2, :], ALU.add).then_inc(S["tap_step"], 1)
                pool.wait_ge(S["tap_step"], 2 * KS * KS * g + 2 * KS * KS - 1)
                pool.tensor_tensor(tap[:, 0, 0:1], ka[:, 0:1], ka[:, 0:1], ALU.mult).then_inc(S["tap_step"], 1)
                pool.tensor_tensor(tap[:, 1, 0:1], ka[:, 0:1], ka[:, 0:1], ALU.mult).then_inc(S["gated"], 1)
                for s in range(SECOND):
                    pool.wait_ge(xr_landed[s % 4], whole[s % 4] * g + before[s + 4])
                    pool.tensor_tensor(XR[:, s % 4], XR[:, s % 4], bout[:, :, :], ALU.add).then_inc(S["residual_ready"], 1)

        def load_residual(act, g, s):
            for d, t in second_views(x2, XR, g, s):
                act.dma_start(t, d).then_inc(xr_landed[s % 4], 16)

        @block.scalar
        def _(act):
            with act.Fori(0, GROUPS) as g:
                with act.Fori(0, C // (2 * CHUNK)) as i:
                    for k in range(4):
                        n = PAIRS_G * g + 4 * i + k
                        p = k % 2
                        act.wait_ge(S["conv_psum"], n + 1)
                        act.activation(e1[:, p], conv[p][0:BLOCK, :, NPIX:2 * NPIX], ACT.Exp, scale=-1.0).then_inc(S["gate_exp"], 1)
                        act.wait_ge(S["abs_ready"], n + 1)
                        act.activation(ab[:, p], ab[:, p], ACT.Exp, scale=-1.0).then_inc(S["b_exp"], 1)
                        act.wait_ge(S["b_exp"], n + 1)
                        act.activation(ab[:, p], ab[:, p], ACT.Ln, bias=1.0).then_inc(S["b_log"], 1)
                for s in range(3):
                    load_residual(act, g, s)
                act.wait_ge(S["gated"], g + 1)
                act.activation(fac[:, 0, :], gate[:, :], ACT.Exp, scale=-1.0).then_inc(S["corner_exp"], 1)
                act.wait_ge(S["corner_step"], CORNER_STEPS * g + 3)
                act.activation(fac[:, 1, :], fac[:, 0, :], ACT.Exp).then_inc(S["corner_exp"], 1)
                act.activation(fac[:, 2, :], fac[:, 0, :], ACT.Exp, scale=-1.0).then_inc(S["corner_exp"], 1)
                for s in range(SECOND + 1):
                    if s + 3 < SECOND:
                        if s:
                            act.wait_ge(S["x3_ready"], SECOND * g + s + 2)
                        load_residual(act, g, s + 3)
                    if s:
                        act.wait_ge(S["x3_ready"], SECOND * g + s + 2)
                        for d, t in second_views(x3, X3, g, s - 1):
                            act.dma_start(d, t).then_inc(x3_stored[(s - 1) % 4], 16)
                for i in range(4):
                    act.wait_ge(x3_stored[i], whole[i] * g + whole[i])

        @block.vector
        def _(dve):
            dve.memset(e1[:, :, :, :], 0.0).then_inc(S["b_ready"], 3)
            dve.memset(hT[:, :, :, :], 0.0).then_inc(S["evacuated"], 2)
            dve.memset(X3[:, :, :, :], 0.0).then_inc(S["x3_ready"], 2)
            dve.wait_ge(S["const_landed"], 64)
            with dve.Fori(0, GROUPS) as g:
                n = 0
                for img in range(GROUP):
                    for half, blocks in enumerate(near_blocks):
                        dve.wait_ge(S["turned"], TURNS * g + n + 1)
                        m = len(blocks)
                        src = th[n % 2][:, 0:m * BLOCK].rearrange("c (a b) -> c a b", b=W)
                        rows = around[:, 8 * half:8 * half + 2 * m, :, img]
                        dve.tensor_copy(rows[:, :, 0:KS - 1], src[:, :, W - KS + 1:W])
                        op = dve.tensor_copy(rows[:, :, KS - 1:CC], src[:, :, 0:KS])
                        op.then_inc(S["evacuated"], 1)
                        n += 1
                dve.wait_ge(S["evacuated"], TURNS * g + NEAR + 2)
                dve.memset(tap[:, 0, 0:1], 0.0).then_inc(S["around_ready"], 1)
                with dve.Fori(0, C // (2 * CHUNK)) as i:
                    for k in range(4):
                        n = PAIRS_G * g + 4 * i + k
                        p = k % 2
                        dve.wait_ge(S["gate_exp"], n + 1)
                        dve.tensor_scalar(e1[:, p], e1[:, p], 1.0, None, ALU.add).then_inc(S["plus1"], 1)
                        dve.wait_ge(S["plus1"], n + 1)
                        dve.reciprocal(e1[:, p], e1[:, p]).then_inc(S["recip"], 1)
                        dve.wait_ge(S["recip"], n + 1)
                        dve.tensor_tensor(bt[:, p], conv[p][0:BLOCK, :, 0:NPIX], e1[:, p], ALU.mult).then_inc(S["b_ready"], 1)
                        dve.wait_ge(S["b_ready"], n + 4)
                        dve.scalar_tensor_tensor(out=ab[:, p], in0=bt[:, p], scalar=-1.0, in1=bt[:, p], op0=ALU.mult, op1=ALU.max).then_inc(S["abs_ready"], 1)
                        dve.wait_ge(S["b_log"], n + 1)
                        for c in range(2):
                            ch = 8 * i + 2 * k + c
                            op = dve.scalar_tensor_tensor(out=xt[:, :, 1:1 + BLOCKS, bass.ds(ch, 1)].rearrange("p a b c -> p a (b c)"),
                                                          in0=bt[:, p, c, :].rearrange("p (a b) -> p a b", a=GROUP), scalar=0.0,
                                                          in1=ab[:, p, c, :].rearrange("p (a b) -> p a b", a=GROUP), op0=ALU.max, op1=ALU.add)
                        op.then_inc(S["h_ready"], 1)

                done = [CORNER_STEPS * g]

                def link(op):
                    done[0] = done[0] + 1
                    op.then_inc(S["corner_step"], 1)
                    dve.wait_ge(S["corner_step"], done[0])
                f = [fac[:, k, :] for k in range(4)]
                impulse = ka[:, :].unsqueeze(2).to_broadcast([128, KS * KS, GROUP])
                dve.wait_ge(S["corner_exp"], 3 * g + 1)
                link(dve.tensor_scalar(f[0], f[0], 1.0, None, ALU.add))
                link(dve.reciprocal(f[0], f[0]))
                link(dve.tensor_tensor(f[0].rearrange("c (a b) -> c a b", b=GROUP), f[0].rearrange("c (a b) -> c a b", b=GROUP), impulse, ALU.mult))
                dve.wait_ge(S["corner_exp"], 3 * g + 3)
                link(dve.tensor_scalar(fac[:, 1:3, :], fac[:, 1:3, :], 1.0, None, ALU.add))
                link(dve.reciprocal(fac[:, 1:3, :], fac[:, 1:3, :]))
                link(dve.scalar_tensor_tensor(out=f[2], in0=f[1], scalar=1.0, in1=f[2], op0=ALU.add, op1=ALU.mult))
                link(dve.tensor_tensor(f[3], f[1], f[1], ALU.mult))
                link(dve.scalar_tensor_tensor(out=f[2], in0=f[3], scalar=1.0, in1=f[2], op0=ALU.add, op1=ALU.mult))
                link(dve.tensor_tensor(f[1], f[3], f[3], ALU.mult))
                link(dve.scalar_tensor_tensor(out=f[2], in0=f[1], scalar=1.0, in1=f[2], op0=ALU.add, op1=ALU.mult))
                factor = f[2].rearrange("c (a b i) -> c a b i", a=KS, b=KS)

                def corner(s):
                    img, k = divmod(s, STRIPS)
                    cols = [(slice(0, REACH + 1), slice(REACH, KS)), (slice(W - REACH, W), slice(0, REACH))]
                    for j, rows, a in {0: [(0, 2, 4), (1, 1, 6)], STRIPS - 1: [(2, 2, 0), (3, 2, 2)]}.get(k, []):
                        for w, b in cols:
                            yield (hT[:, s % 2, j, :].rearrange("c (r w) -> c r w", r=2)[:, 0:rows, w],
                                   th[s % 2][:, BLOCK * j:BLOCK * (j + 1)].rearrange("c (r w) -> c r w", r=2)[:, 0:rows, w],
                                   factor[:, a:a + rows, b, img])

                def evacuate(s):
                    dve.wait_ge(S["turned"], TURNS * g + NEAR + s + 1)
                    op = dve.tensor_scalar(hT[:, s % 2].rearrange("c a b -> c (a b)"), th[s % 2][:, 0:4 * BLOCK],
                                           EPS, 1.0 - 0.5 ** SCAN, ALU.add, ALU.mult)
                    op.then_inc(S["evacuated"], 1)
                    own = list(corner(s))
                    if own:
                        dve.wait_ge(S["evacuated"], TURNS * g + NEAR + s + 3)
                    for dst, src, by in own:
                        op = dve.scalar_tensor_tensor(out=dst, in0=src, scalar=EPS, in1=by, op0=ALU.add, op1=ALU.mult)
                    if own:
                        op.then_inc(S["corner_ready"], 1)

                evacuate(0)
                for s in range(SECOND):
                    if s + 1 < SECOND:
                        evacuate(s + 1)
                    dve.wait_ge(S["ob_psum"], SECOND * g + s + 1)
                    dve.wait_ge(S["residual_ready"], SECOND * g + s + 1)
                    if s >= 4:
                        dve.wait_ge(x3_stored[s % 4], whole[s % 4] * g + before[s])
                    dve.tensor_tensor(X3[:, s % 4].rearrange("p a b -> p (a b)"), ob[s % 2][0:BLOCK, :],
                                      XR[:, s % 4].rearrange("p a b -> p (a b)"), ALU.add).then_inc(S["x3_ready"], 1)

        @block.tensor
        def _(pe):
            pe.wait_ge(S["ident_ready"], 1)
            pe.wait_ge(S["const_landed"], 64)
            with pe.Fori(0, GROUPS) as g:
                n = 0
                for img in range(GROUP):
                    pe.wait_ge(image_landed[img], 48 * g + 48)
                    for blocks in near_blocks:
                        pe.wait_ge(S["evacuated"], TURNS * g + n + 1)
                        for k, i in enumerate(blocks):
                            op = pe.transpose(th[n % 2][:, k * BLOCK:(k + 1) * BLOCK], xt[:, img, i + 1, :], ident[0:BLOCK, 0:BLOCK])
                        op.then_inc(S["turned"], 1)
                        n += 1
                with pe.Fori(0, C // (2 * CHUNK)) as i:
                    for k in range(4):
                        n = PAIRS_G * g + 4 * i + k
                        if k % 2 == 0:
                            pe.wait_ge(tz_landed[k // 2], C // CHUNK * 8 * g + 16 * i + 16)
                        pe.wait_ge(S["b_ready"], n + 2)
                        for c in range(2):
                            ch = 8 * i + 2 * k + c
                            for kernel in range(2):
                                for o in range(4):
                                    q = 6 - 2 * o
                                    op = pe.matmul(conv[k % 2][0:BLOCK, c, NPIX * kernel:NPIX * (kernel + 1)],
                                                   tz[:, k // 2, 2 * (k % 2) + c, kernel, W * q:W * (q + 2)],
                                                   xt[:, :, o:o + BLOCKS, bass.ds(ch, 1)].rearrange("p a b c -> p a (b c)"),
                                                   start=o == 0, stop=o == 3)
                        op.then_inc(S["conv_psum"], 1)
                pe.wait_ge(S["h_ready"], PAIRS_G * g + PAIRS_G)

                def turn(s):
                    img, k = divmod(s, STRIPS)
                    pe.wait_ge(S["evacuated"], TURNS * g + NEAR + s + 1)
                    for b in range(4):
                        op = pe.transpose(th[s % 2][:, b * BLOCK:(b + 1) * BLOCK], xt[:, img, 4 * k + b + 1, :], ident[0:BLOCK, 0:BLOCK])
                    op.then_inc(S["turned"], 1)
                turn(0)
                for s in range(SECOND):
                    if s + 1 < SECOND:
                        turn(s + 1)
                    if s % STRIPS in (0, STRIPS - 1):
                        pe.wait_ge(S["corner_ready"], 2 * GROUP * g + 2 * (s // STRIPS) + (1 if s % STRIPS == 0 else 2))
                    else:
                        pe.wait_ge(S["evacuated"], TURNS * g + NEAR + s + 3)
                    pe.wait_ge(S["x3_ready"], SECOND * g + s + 1)
                    for b in range(4):
                        op = pe.matmul(ob[s % 2][0:BLOCK, b * C:(b + 1) * C], hT[:, s % 2, b, :], wout[:, :], start=True, stop=True)
                    op.then_inc(S["ob_psum"], 1)


EXPERTS = 64
TOP = 8
HIDDEN = 512
HCHUNKS = HIDDEN // 128
TP = 112
TK = TOKENS // TP
TQ = 4
TGROUPS = TK // TQ
TWINS = B // 2
TAKEN = -2.0 ** 127


def route_phase(nc, x3, gate_w_t, gate_b, probs, pooled):
    nc.disable_value_cache = True
    with ExitStack() as ctx:
        def sb(name, shape):
            return ctx.enter_context(nc.sbuf_tensor("m_" + name, shape, F32))

        def bank(name):
            return ctx.enter_context(nc.psum_tensor("m_" + name, [128, 512], F32))

        semaphores = []

        def sem(name):
            semaphores.append(ctx.enter_context(nc.semaphore("m_" + name)))
            return semaphores[-1]

        NT = 2 * TK
        ident = sb("ident", [128, 128])
        gwt = sb("gwt", [128, EXPERTS])
        gb = sb("gb", [128, 1])
        half_neg = sb("half_neg", [TP, NT])
        eps5 = sb("eps5", [TP, NT])
        carrier = sb("carrier", [128, 6])
        X = sb("X", [TP, 2, 2, TK, C])
        xn = sb("xn", [TP, 2, 2, TK, C])
        xT = sb("xT", [128, 2, 2, TQ * TP])
        L = sb("L", [128, 2, TOKENS])
        E = sb("E", [128, TOKENS])
        P = sb("P", [128, 2, TOKENS])
        PT = sb("PT", [TP, 2, TQ, 128])
        top = sb("top", [128, 2, TOP])
        neg_max = sb("neg_max", [128, 2])
        total = sb("total", [128, 1])
        inv = sb("inv", [128, 1])
        bn = sb("bn", [TP, NT, 6])
        mv = sb("mv", [TP, NT, 2])
        ve = sb("ve", [TP, NT])
        rs = sb("rs", [TP, NT])
        nm = sb("nm", [TP, NT])
        nb = sb("nb", [TP, NT])

        th = [bank("th0"), bank("th1")]
        lg = [bank("lg0"), bank("lg1")]
        pt = [bank("pt0"), bank("pt1")]
        pb = [bank("pb0"), bank("pb1")]

        names = """ident_zero ident_ready const_landed consts stats aggr var dev shift xn_ready turned xT_ready
            lg_psum l_ready top_ready max_ready replaced exp_ready inv_ready masked p_ready pt_psum PT_ready
            pooled_psum pooled_out""".split()
        S = {n: sem(n) for n in names}
        x_landed = [sem(f"x_landed{i}") for i in range(2)]
        p_stored = [sem(f"p_stored{i}") for i in range(2)]

        def turns(eng, turn):
            def one(t):
                turn(t, t % 2, lambda o: 0 <= t + o < TWINS)
            for t in range(-2, 2):
                one(t)
            with eng.Fori(0, (TWINS - 4) // 2) as i:
                for j in range(2):
                    turn(2 * i + 2 + j, j, lambda o: True)
            for t in range(TWINS - 2, TWINS + 1):
                one(t)

        block = phase_block(nc, ctx, semaphores)

        @block.sync
        def _(sp):
            sp.dma_start(gwt[:, :], gate_w_t).then_inc(S["const_landed"], 16)
            for u in range(2):
                sp.dma_start(gb[EXPERTS * u:EXPERTS * (u + 1), :], gate_b.rearrange("(p a) -> p a", a=1)
                             ).then_inc(S["const_landed"], 16)

            def turn(t, j, has):
                if has(2):
                    wait(sp, S["xn_ready"], TGROUPS * (t + 1))
                    for u in range(2):
                        sp.dma_start(X[:, j, u], x3.rearrange("b h w c -> b (h w) c").rearrange(
                            "b (p k) c -> b p k c", k=TK)[2 * (t + 2) + u]).then_inc(x_landed[j], 16)
                if has(-1):
                    sp.wait_ge(S["p_ready"], t)
                    sp.dma_start(probs[t - 1], P[:, (j - 1) % 2]).then_inc(p_stored[(j - 1) % 2], 16)
            turns(sp, turn)
            for i in range(2):
                sp.wait_ge(p_stored[i], 16 * (TWINS // 2))

        @block.gpsimd
        def _(pool):
            make_identity(pool, ident, S["ident_zero"], S["ident_ready"])
            pool.memset(half_neg[:, :], -0.5)
            pool.memset(eps5[:, :], 1e-5).then_inc(S["consts"], 1)
            pool.wait_ge(S["consts"], 1)

            def turn(t, j, has):
                if not has(1):
                    return
                m, p = t + 1, (j + 1) % 2
                pool.wait_ge(S["aggr"], m + 1)
                pool.tensor_tensor(ve[:, :], mv[:, :, 1], eps5[:, :], ALU.add)
                pool.tensor_scalar(nm[:, :], mv[:, :, 0], -1.0, 1.0, ALU.mult, ALU.mult).then_inc(S["var"], 1)
                pool.wait_ge(S["var"], m + 1)
                pool.tensor_tensor(rs[:, :], ve[:, :], half_neg[:, :], ALU.pow).then_inc(S["dev"], 1)
                pool.wait_ge(S["dev"], m + 1)
                pool.tensor_tensor(nb[:, :], nm[:, :], rs[:, :], ALU.mult).then_inc(S["shift"], 1)
                pool.wait_ge(S["shift"], m + 1)
                pool.tensor_tensor(carrier[0:TP, 0:1], half_neg[:, 0:1], half_neg[:, 1:2], ALU.mult)
                wait(pool, S["pooled_psum"], m - 1)
                pool.tensor_tensor(carrier[0:TP, 3:4], half_neg[:, 0:1], half_neg[:, 1:2], ALU.mult)
                for g in range(TGROUPS):
                    for u in range(2):
                        for k in range(TQ * g, TQ * (g + 1)):
                            n = TK * u + k
                            op = pool.tensor_scalar(xn[:, p, u, k], X[:, p, u, k], rs[:, n:n + 1], nb[:, n:n + 1], ALU.mult, ALU.add)
                    op.then_inc(S["xn_ready"], 1)
            turns(pool, turn)

        @block.scalar
        def _(act):
            act.wait_ge(S["const_landed"], 48)

            def turn(t, j, has):
                m, p = t - 1, (j - 1) % 2

                def logits_out(g):
                    act.wait_ge(S["lg_psum"], TGROUPS * t + g + 1)
                    if g == 0:
                        wait(act, S["replaced"], t - 1)
                    act.activation(L[:, j].rearrange("e (p k) -> e k p", k=TK)[:, TQ * g:TQ * (g + 1), :],
                                   lg[g % 2][:, 0:TQ * TP].rearrange("e (k p) -> e k p", k=TQ),
                                   ACT.Identity, bias=gb[:, 0:1]).then_inc(S["l_ready"], 1)
                for g in range(TGROUPS):
                    if has(-1) and g == 2:
                        wait(act, S["masked"], m)
                        act.wait_ge(S["max_ready"], m + 1)
                        act.activation(E[:, :], L[:, p], ACT.Exp, bias=neg_max[:, p:p + 1], accum_out=total[:, 0:1]
                                       ).then_inc(S["exp_ready"], 1)
                    if has(0):
                        if g >= 2:
                            act.wait_ge(S["lg_psum"], TGROUPS * t + g - 1)
                        else:
                            wait(act, S["lg_psum"], TGROUPS * t + g - 1)
                        for u in range(2):
                            act.wait_ge(S["turned"], 2 * (TGROUPS * t + g) + u + 1)
                            act.activation(xT[:, g % 2, u], th[u][:, 0:TQ * TP], ACT.Copy).then_inc(S["xT_ready"], 1)
                        if g:
                            logits_out(g - 1)
                if has(0):
                    logits_out(TGROUPS - 1)
                if has(-1):
                    act.wait_ge(S["inv_ready"], m + 1)
                    act.wait_ge(S["masked"], m + 1)
                    act.activation(P[:, p], P[:, p], ACT.Copy, scale=inv[:, 0:1]).then_inc(S["p_ready"], 1)
                    for g in range(TGROUPS):
                        act.wait_ge(S["pt_psum"], TGROUPS * m + g + 1)
                        act.activation(PT[:, g % 2].rearrange("p k e -> p (k e)"), pt[g % 2][0:TP, :], ACT.Copy
                                       ).then_inc(S["PT_ready"], 1)
                    act.wait_ge(S["pooled_psum"], m + 1)
                    for u in range(2):
                        op = act.activation(pooled[:, :, bass.ds(2 * m + u, 1)].rearrange("c e a -> c (e a)"),
                                            pb[u][:, 0:EXPERTS], ACT.Copy)
                    op.then_inc(S["pooled_out"], 1)
            turns(act, turn)

        @block.vector
        def _(dve):
            def turn(t, j, has):
                m, p = t - 1, (j - 1) % 2

                def stats(u):
                    if u == 0:
                        wait(dve, S["aggr"], t + 1)
                        dve.wait_ge(x_landed[(j + 1) % 2], 16 * (t + 1 - (j + 1) % 2) + 32)
                        dve.memset(carrier[:, 1:2], 0.0)
                    for k in range(TK):
                        op = dve.bn_stats(bn[:, TK * u + k, :], X[:, (j + 1) % 2, u, k, :])
                    op.then_inc(S["stats"], 1)
                if has(-1):
                    dve.wait_ge(S["l_ready"], TGROUPS * (m + 1))
                    dve.memset(carrier[:, 2:3], 0.0)
                    dve.max(top[:, p], L[:, p]).then_inc(S["top_ready"], 1)
                    dve.wait_ge(S["top_ready"], m + 1)
                    dve.tensor_scalar(neg_max[:, p:p + 1], top[:, p, 0:1], -1.0, None, ALU.mult).then_inc(S["max_ready"], 1)
                    wait(dve, p_stored[p], 8 * (m - p))
                    wait(dve, S["pooled_psum"], m - 1)
                    dve.memset(carrier[:, 5:6], 0.0)
                    dve.match_replace(P[:, p], top[:, p], L[:, p], TAKEN).then_inc(S["replaced"], 1)
                if has(1):
                    stats(0)
                if has(-1):
                    dve.wait_ge(S["exp_ready"], m + 1)
                    dve.reciprocal(inv[:, 0:1], total[:, 0:1]).then_inc(S["inv_ready"], 1)
                    dve.wait_ge(S["replaced"], m + 1)
                    dve.scalar_tensor_tensor(out=P[:, p], in0=P[:, p], scalar=TAKEN, in1=E[:, :], op0=ALU.is_equal,
                                             op1=ALU.mult).then_inc(S["masked"], 1)
                if has(1):
                    stats(1)
                    dve.wait_ge(S["stats"], 2 * (t + 2))
                    wait(dve, S["shift"], t + 1)
                    dve.memset(carrier[:, 4:5], 0.0)
                    for n in range(NT):
                        op = dve.bn_aggr(mv[:, n, :], bn[:, n, :])
                    op.then_inc(S["aggr"], 1)
            turns(dve, turn)

        @block.tensor
        def _(pe):
            pe.wait_ge(S["ident_ready"], 1)
            pe.wait_ge(S["const_landed"], 48)

            def turn(t, j, has):
                m, p = t - 1, (j - 1) % 2

                def transposes(g):
                    pe.wait_ge(S["xn_ready"], TGROUPS * t + g + 1)
                    for u in range(2):
                        wait(pe, S["xT_ready"], 2 * (TGROUPS * t + g - 1) + u + 1)
                        for k in range(TQ):
                            op = pe.transpose(th[u][:, TP * k:TP * (k + 1)], xn[:, j, u, TQ * g + k, :], ident[0:TP, 0:TP])
                        op.then_inc(S["turned"], 1)
                if has(0):
                    transposes(0)
                    for g in range(TGROUPS):
                        if g + 1 < TGROUPS:
                            transposes(g + 1)
                        pe.wait_ge(S["xT_ready"], 2 * (TGROUPS * t + g) + 2)
                        wait(pe, S["l_ready"], TGROUPS * t + g - 1)
                        for u in range(2):
                            op = pe.matmul(lg[g % 2][EXPERTS * u:EXPERTS * (u + 1), 0:TQ * TP], gwt[:, :], xT[:, g % 2, u],
                                           start=True, stop=True)
                        op.then_inc(S["lg_psum"], 1)
                if has(-1):
                    pe.wait_ge(S["p_ready"], m + 1)
                    wait(pe, S["pooled_out"], m)

                    def turn_probs(g):
                        wait(pe, S["PT_ready"], TGROUPS * m + g - 1)
                        for k in range(TQ):
                            rows = P[:, p].rearrange("e (p k) -> e k p", k=TK)[:, TQ * g + k, :]
                            op = pe.transpose(pt[g % 2][0:TP, 128 * k:128 * (k + 1)], rows, ident[:, :])
                        op.then_inc(S["pt_psum"], 1)
                    turn_probs(0)
                    for g in range(TGROUPS):
                        if g + 1 < TGROUPS:
                            turn_probs(g + 1)
                        pe.wait_ge(S["PT_ready"], TGROUPS * m + g + 1)
                        for k in range(TQ):
                            for u in range(2):
                                n = TQ * g + k
                                op = pe.matmul(pb[u][:, 0:EXPERTS], xn[:, p, u, n, :], PT[:, g % 2, k, EXPERTS * u:EXPERTS * (u + 1)],
                                               start=n == 0, stop=n == TK - 1)
                    op.then_inc(S["pooled_psum"], 1)
            turns(pe, turn)


def expert_phase(nc, pooled, weight1, weight2, expert_out):
    nc.disable_value_cache = True
    with ExitStack() as ctx:
        def sb(name, shape):
            return ctx.enter_context(nc.sbuf_tensor("x_" + name, shape, F32))

        def bank(name):
            return ctx.enter_context(nc.psum_tensor("x_" + name, [128, 512], F32))

        semaphores = []

        def sem(name):
            semaphores.append(ctx.enter_context(nc.semaphore("x_" + name)))
            return semaphores[-1]

        DEPTH = 4
        one = sb("one", [1, B])
        w1 = sb("w1", [128, DEPTH, HIDDEN])
        w1_bias = sb("w1_bias", [1, DEPTH, HIDDEN])
        w2 = sb("w2", [128, DEPTH, HCHUNKS, C])
        w2_bias = sb("w2_bias", [1, DEPTH, C])
        hid = sb("hid", [128, 2, HCHUNKS * B])
        OE = sb("OE", [B, EXPERTS, C])
        h_bank = [bank("h0"), bank("h1")]
        o_bank = [bank("o0"), bank("o1")]
        S = {n: sem(n) for n in "ready h_psum h_ready o_psum o_ready stored".split()}
        w_landed = [sem(f"w_landed{i}") for i in range(DEPTH)]

        block = phase_block(nc, ctx, semaphores)

        @block.sync
        def _(sp):
            def load(e, i):
                sp.dma_start(w1[:, i], weight1[e, 0:C, :]).then_inc(w_landed[i], 16)
                sp.dma_start(w1_bias[:, i], weight1[e, C:C + 1, :]).then_inc(w_landed[i], 16)
                sp.dma_start(w2[:, i], weight2[e, 0:HIDDEN, :].rearrange("(p k) o -> p k o", k=HCHUNKS)).then_inc(w_landed[i], 16)
                sp.dma_start(w2_bias[:, i], weight2[e, HIDDEN:HIDDEN + 1, :]).then_inc(w_landed[i], 16)
            for i in range(DEPTH):
                load(i, i)
            with sp.Fori(0, EXPERTS // DEPTH - 1) as n:
                for i in range(DEPTH):
                    sp.wait_ge(S["o_psum"], DEPTH * n + i + 1)
                    load(DEPTH * n + DEPTH + i, i)
            sp.wait_ge(S["o_ready"], EXPERTS + 2)
            sp.dma_start(expert_out.rearrange("b e o -> b (e o)"), OE.ap().rearrange("b e o -> b (e o)")).then_inc(S["stored"], 16)
            sp.wait_ge(S["stored"], 16)

        @block.scalar
        def _(act):
            with act.Fori(0, EXPERTS // 2) as n:
                for i in range(2):
                    act.wait_ge(S["h_psum"], 2 * n + i + 1)
                    act.activation(hid[:, i], h_bank[i][:, 0:HCHUNKS * B], ACT.Gelu).then_inc(S["h_ready"], 1)

        @block.vector
        def _(dve):
            dve.memset(one[:, :], 1.0).then_inc(S["ready"], 1)
            dve.memset(OE[:, 0, 0:1], 0.0).then_inc(S["o_ready"], 2)
            dve.wait_ge(S["o_ready"], 2)
            with dve.Fori(0, EXPERTS // 2) as n:
                for i in range(2):
                    dve.wait_ge(S["o_psum"], 2 * n + i + 1)
                    dve.tensor_copy(OE[:, bass.ds(2 * n + i, 1), :].rearrange("b e o -> b (e o)"), o_bank[i][0:B, 0:C]
                                    ).then_inc(S["o_ready"], 1)

        @block.tensor
        def _(pe):
            pe.wait_ge(S["ready"], 1)

            def expert(e, slot, landed):
                i = slot % 2
                pe.wait_ge(w_landed[slot], landed)
                pe.wait_ge(S["o_ready"], e + 1)
                for k in range(HCHUNKS):
                    part = slice(k, HIDDEN, HCHUNKS)
                    out = h_bank[i][:, B * k:B * (k + 1)]
                    pe.matmul(out, w1[:, slot, part], pooled[:, bass.ds(e, 1), :].rearrange("c e b -> c (e b)"), start=True, stop=False)
                    op = pe.matmul(out, w1_bias[:, slot, part], one[:, :], start=False, stop=True)
                op.then_inc(S["h_psum"], 1)
                pe.wait_ge(S["h_ready"], e + 1)
                for k in range(HCHUNKS):
                    pe.matmul(o_bank[i][0:B, 0:C], hid[:, i, B * k:B * (k + 1)], w2[:, slot, k], start=k == 0, stop=False)
                pe.matmul(o_bank[i][0:B, 0:C], one[:, :], w2_bias[:, slot], start=False, stop=True).then_inc(S["o_psum"], 1)
            with pe.Fori(0, EXPERTS // DEPTH) as n:
                for i in range(DEPTH):
                    expert(DEPTH * n + i, i, 64 * n + 64)


def spread_phase(nc, x3, probs, expert_out, out):
    nc.disable_value_cache = True
    with ExitStack() as ctx:
        def sb(name, shape):
            return ctx.enter_context(nc.sbuf_tensor("s_" + name, shape, F32))

        semaphores = []

        def sem(name):
            semaphores.append(ctx.enter_context(nc.semaphore("s_" + name)))
            return semaphores[-1]

        DEPTH, BANKS = 4, 8
        P = sb("P", [128, DEPTH, TOKENS])
        OE = sb("OE", [128, DEPTH, C])
        X = sb("X", [TP, DEPTH, 2, TK, C])
        ob = [ctx.enter_context(nc.psum_tensor(f"s_o{i}", [128, 512], F32)) for i in range(BANKS)]
        o_psum, added = sem("o_psum"), sem("added")
        landed = [sem(f"landed{i}") for i in range(DEPTH)]
        stored = [sem(f"stored{i}") for i in range(DEPTH)]
        STEPS2 = 2 * TGROUPS

        def image(dram, n):
            return dram.rearrange("b h w c -> b (h w) c").rearrange("b (p k) c -> b p k c", k=TK)[n]

        block = phase_block(nc, ctx, semaphores)

        @block.sync
        def _(sp):
            def load(n, i):
                sp.dma_start(P[:, i], probs[n]).then_inc(landed[i], 16)
                sp.dma_start(OE[:, i], expert_out.rearrange("(n u) e o -> n (u e) o", u=2)[n]).then_inc(landed[i], 16)
                for u in range(2):
                    sp.dma_start(X[:, i, u], image(x3, 2 * n + u)).then_inc(landed[i], 16)
            for i in range(DEPTH):
                load(i, i)
            with sp.Fori(0, TWINS // DEPTH - 1) as m:
                for i in range(DEPTH):
                    sp.wait_ge(stored[i], 32 * m + 32)
                    load(DEPTH * m + DEPTH + i, i)

        @block.scalar
        def _(act):
            with act.Fori(0, TWINS // DEPTH) as m:
                for i in range(DEPTH):
                    for u in range(2):
                        act.wait_ge(added, STEPS2 * (DEPTH * m + i) + TGROUPS * (u + 1) + BANKS)
                        act.dma_start(image(out, 2 * (DEPTH * m + i) + u), X[:, i, u]).then_inc(stored[i], 16)
            for i in range(DEPTH):
                act.wait_ge(stored[i], 32 * (TWINS // DEPTH))

        @block.vector
        def _(dve):
            dve.memset(ob[0][0:1, 0:1], 0.0).then_inc(added, BANKS)
            dve.wait_ge(added, BANKS)
            with dve.Fori(0, TWINS // DEPTH) as m:
                for i in range(DEPTH):
                    dve.wait_ge(landed[i], 64 * m + 64)
                    for g in range(STEPS2):
                        u, k = divmod(g, TGROUPS)
                        dve.wait_ge(o_psum, STEPS2 * (DEPTH * m + i) + g + 1)
                        x = X[:, i, u, TQ * k:TQ * (k + 1)].rearrange("p k c -> p (k c)")
                        dve.tensor_tensor(x, ob[(STEPS2 * i + g) % BANKS][0:TP, :], x, ALU.add).then_inc(added, 1)

        @block.tensor
        def _(pe):
            with pe.Fori(0, TWINS // DEPTH) as m:
                for i in range(DEPTH):
                    pe.wait_ge(landed[i], 64 * m + 64)
                    for g in range(STEPS2):
                        u, k = divmod(g, TGROUPS)
                        rows = slice(EXPERTS * u, EXPERTS * (u + 1))
                        pe.wait_ge(added, STEPS2 * (DEPTH * m + i) + g + 1)
                        for q in range(TQ):
                            pt = P[rows, i].rearrange("e (p k) -> e k p", k=TK)[:, TQ * k + q, :]
                            op = pe.matmul(ob[(STEPS2 * i + g) % BANKS][0:TP, C * q:C * (q + 1)], pt, OE[rows, i], start=True, stop=True)
                        op.then_inc(o_psum, 1)


def metaformer(nc, x, w_qkv_t, pos, mask, head_own, attn_w_out_t, attn_b_out, w, w_t, v_t, gamma, beta, kernel_a, kernel_b,
               kernel_gate_a, kernel_gate_b, conv_w_out, conv_b_out, gate_w_t, gate_b, weight1, weight2, out):
    def scratch(name, shape):
        return nc.dram_tensor(name, shape, F32, kind="Internal").ap()

    image = (B, H, W, C)
    x1, x2, xc, x3 = [scratch(name, image) for name in ("x1", "x2", "xc", "x3")]
    pos_rows = scratch("pos_rows", (WS, 2 * WS - 1, WS))
    rows = scratch("kernel_rows", (C, 2, TAPS + 1, 2 * W))
    toeplitz = scratch("toeplitz", (BLOCK, C, 2, TZ))
    probs = scratch("probs", (TWINS, 2 * EXPERTS, TOKENS))
    expert_out = scratch("expert_out", (B, EXPERTS, C))

    with nc.sbuf_tensor("gram", [C, C + 1], F32) as gram:
        attention_phase(nc, x, w_qkv_t, pos, pos_rows, mask, head_own, attn_w_out_t, attn_b_out, x1, gram)
        recurrent_phase(nc, x1, w, w_t, v_t, gamma, beta, gram, x2, xc)
    expand_phase(nc, kernel_b, kernel_gate_b, rows, toeplitz)
    convolution_phase(nc, xc, x2, toeplitz, kernel_a, kernel_gate_a, conv_w_out, conv_b_out, x3)
    with nc.sbuf_tensor("pooled", [C, EXPERTS, B], F32) as pooled:
        route_phase(nc, x3, gate_w_t, gate_b, probs, pooled)
        expert_phase(nc, pooled, weight1, weight2, expert_out)
    spread_phase(nc, x3, probs, expert_out, out)


def kernel(**inputs):
    import concourse.bacc as bacc
    from concourse.bass_utils import run_bass_kernel_spmd

    given = {name: np.asarray(a) for name, a in inputs.items()}
    arrays = {
        "x": given["x"],
        "w_qkv_t": given["L0_conv_w_qkv"].T,
        "pos": given["L0_conv_pos_embedding"],
        "mask": window_masks(),
        "head_own": head_channels(),
        "attn_w_out_t": given["L0_conv_w_out"].T,
        "attn_b_out": given["L0_conv_b_out"],
        "w": given["L0_ffn_W"],
        "w_t": given["L0_ffn_W"].T,
        "v_t": given["L0_ffn_V"].T,
        "gamma": given["L0_ffn_gamma"],
        "beta": given["L0_ffn_beta"],
        "kernel_a": given["L1_conv_A_kernel"],
        "kernel_b": given["L1_conv_B_kernel"],
        "kernel_gate_a": given["L1_conv_gate_A_kernel"],
        "kernel_gate_b": given["L1_conv_gate_B_kernel"],
        "conv_w_out": given["L1_conv_W_out"],
        "conv_b_out": given["L1_conv_b_out"],
        "gate_w_t": given["L1_ffn_gate_w"].T,
        "gate_b": given["L1_ffn_gate_b"],
        "weight1": given["L1_ffn_weight1"],
        "weight2": given["L1_ffn_weight2"],
    }
    arrays = {name: np.ascontiguousarray(a) for name, a in arrays.items()}
    nc = bacc.Bacc("TRN2", target_bir_lowering=False, num_devices=1)
    aps = {name: nc.dram_tensor(name, a.shape, mybir.dt.from_np(a.dtype), kind="ExternalInput").ap() for name, a in arrays.items()}
    out = nc.dram_tensor("out", (B, H, W, C), F32, kind="ExternalOutput").ap()
    metaformer(nc, out=out, **aps)
    result = run_bass_kernel_spmd(nc, [arrays], core_ids=[0])
    return result.results[0]["out"]
```

```python
from contextlib import ExitStack

import concourse.bass as bass
from concourse import mybir
import numpy as np

F32 = mybir.dt.float32
ALU = mybir.AluOpType
ACT = mybir.ActivationFunctionType
AX = mybir.AxisListType

B, H, W, C = 64, 56, 56, 128
TOKENS = H * W

WS = 7
SHIFT = WS // 2
HEADS, HEAD_DIM = 4, 32
QK_SCALE = HEADS ** -0.5
WIN = WS * WS
WROWS, WCOLS = H // WS, W // WS
STRIP = WS * W
SP4 = STRIP // 4
PAIRS = WCOLS // 2
UPPER = 64
ROWS2 = UPPER + WIN
HALF = PAIRS // 2 * HEADS * WIN
MASKED = -1e30

KS = 7
REACH = KS // 2
BLOCK = 2 * W
BLOCKS = H // 2
GROUP = 8
GROUPS = B // GROUP
SLOTS = BLOCKS + 3
NPIX = GROUP * BLOCKS
CHUNK = 4
TAPS = KS + 1
TZ = TAPS * W
SCAN = 8
EPS = 1e-6
NCORNER = KS * KS * GROUP
CR, CC = 2 * KS, 2 * KS - 1


def wait(eng, sem, value):
    if isinstance(value, int) and value <= 0:
        return
    eng.wait_ge(sem, value)


def clear(nc, semaphores):
    block = nc.Block()
    with block:
        @block.gpsimd
        def _(pool):
            for semaphore in semaphores:
                pool.sem_clear(semaphore)


def phase_block(nc, ctx, semaphores):
    ctx.callback(clear, nc, semaphores)
    return ctx.enter_context(nc.Block())


def make_identity(pool, ident, filled, ready):
    pool.memset(ident[:, :], 0.0).then_inc(filled, 1)
    pool.wait_ge(filled, 1)
    pool.affine_select(out=ident[:, :], in_=ident[:, :], compare_op=ALU.not_equal, fill=1.0, base=0,
                       pattern=[[-1, 128]], channel_multiplier=1).then_inc(ready, 1)


def kernel_rows_phase(nc, k_b, k_gb, rows):
    nc.disable_value_cache = True
    with ExitStack() as ctx:
        kern = ctx.enter_context(nc.sbuf_tensor("e_kern", [128, 2, KS * KS], F32))
        ext = ctx.enter_context(nc.sbuf_tensor("e_ext", [128, 2, TAPS + 1, 2 * W], F32))
        semaphores = [ctx.enter_context(nc.semaphore("e_" + n)) for n in ("landed", "zeroed", "spread", "rows_stored")]
        landed, zeroed, spread, rows_stored = semaphores
        block = phase_block(nc, ctx, semaphores)

        @block.vector
        def _(dve):
            dve.memset(ext[:, :, :, :], 0.0).then_inc(zeroed, 1)
            dve.wait_ge(zeroed, 1)
            dve.wait_ge(landed, 32)
            for i in range(2):
                k = kern[:, i, :].rearrange("c (a b) -> c a b", a=KS)
                dve.tensor_copy(ext[:, i, 1:1 + KS, W - REACH:W + REACH + 1], k)
                dve.tensor_copy(ext[:, i, 1:1 + KS, 0:REACH + 1], k[:, :, REACH:KS])
                op = dve.tensor_copy(ext[:, i, 1:1 + KS, 2 * W - REACH:2 * W], k[:, :, 0:REACH])
            op.then_inc(spread, 1)

        @block.sync
        def _(sp):
            for i, src in enumerate((k_b, k_gb)):
                sp.dma_start(kern[:, i, :], src.rearrange("c a b -> c (a b)")).then_inc(landed, 16)
            sp.wait_ge(spread, 1)
            sp.dma_start(rows, ext[:, :, :, :]).then_inc(rows_stored, 16)
            sp.wait_ge(rows_stored, 16)


def store_toeplitz(eng, rows, toeplitz, w, r, stored):
    eng.dma_start(toeplitz[w + W * r].rearrange("c i (a b) -> (c i) a b", a=TAPS),
                  rows.rearrange("c i a b -> (c i) a b")[:, 1 - r:1 - r + TAPS, bass.ds(W - w, W)]).then_inc(stored, 16)


def attention_phase(nc, x, w_qkv_t, pos, pos_rows, mask, head_own, w_out_t, b_out, rows, toeplitz, x1, gram):
    N = B * WROWS
    nc.disable_value_cache = True
    with ExitStack() as ctx:
        def sb(name, shape):
            return ctx.enter_context(nc.sbuf_tensor("a_" + name, shape, F32))

        def bank(name):
            return ctx.enter_context(nc.psum_tensor("a_" + name, [128, 512], F32))

        semaphores = []

        def sem(name):
            semaphores.append(ctx.enter_context(nc.semaphore("a_" + name)))
            return semaphores[-1]

        ident = sb("ident", [128, 128])
        wqkv = sb("wqkv", [128, 3 * C])
        wout = sb("wout", [128, C])
        bout = sb("bout", [SP4, 4, C])
        bias49 = sb("bias49", [ROWS2, WIN])
        masks = sb("masks", [ROWS2, 2, PAIRS, WIN])
        bias = sb("bias", [ROWS2, 2, PAIRS, HEADS, WIN])
        half_neg = sb("half_neg", [128, 4])
        eps5 = sb("eps5", [128, 4])
        eps6 = sb("eps6", [128, 4])
        carrier = sb("carrier", [128, 2])
        own = sb("own", [128, HEADS])
        X = sb("X", [SP4, WROWS, 4, C])
        X1 = sb("X1", [SP4, WROWS, 4, C])
        bn1 = sb("bn1", [SP4, 4, 6])
        mv1 = sb("mv1", [SP4, 2, 4, 2])
        ve1 = sb("ve1", [SP4, 4])
        rs1 = sb("rs1", [SP4, 2, 4])
        bn2 = sb("bn2", [SP4, 4, 6])
        mv2 = sb("mv2", [SP4, 2, 4, 2])
        ve2 = sb("ve2", [SP4, 4])
        minus = sb("minus", [SP4, 4])
        nb2 = sb("nb2", [SP4, 2, 4])
        rs2 = sb("rs2", [SP4, 2, 4])
        xn = sb("xn", [SP4, 2, 4, C])
        xg = sb("xg", [SP4, 2, 4, C + 1])
        xT = sb("xT", [128, 2, STRIP])
        qT = sb("qT", [128, 2, STRIP])
        kT = sb("kT", [128, STRIP])
        kh = sb("kh", [128, 2, WCOLS, HEADS, WIN])
        vh = sb("vh", [ROWS2, 4, WCOLS, 2, 64])
        sc = sb("sc", [ROWS2, 2, 8, WIN])
        nmax = sb("nmax", [ROWS2, 2, 8])
        psum_ = sb("psum", [ROWS2, 2, 8])
        prec = sb("prec", [ROWS2, 2, 8])
        pr = sb("pr", [ROWS2, 2, 8, 64])
        prT = sb("prT", [ROWS2, 2, 4, ROWS2])
        aT = sb("aT", [128, STRIP])

        POOL_HEADS = 2

        t_bank, qk_bank, v_bank, pt_bank, av_bank, out_bank = [bank(n) for n in ("t", "qk", "v", "pt", "av", "out")]
        s_bank = [bank("s0"), bank("s1")]

        names = """eps_ready ident_zero ident_ready const_landed pos_stored toeplitz_stored bias_landed zeroed bias_ready
            stats1 aggr1 var1 rstd1 xn_ready residual_ready
            xT_psum xT_ready k_psum k_ready kh_ready kh_ready2 q_psum q_ready v_psum v_ready
            s_psum s_biased s_max s_shifted p_exp p_sum p_recip p_ready pt_psum pt_ready
            av_psum aT_ready out_psum x1_ready stats2 aggr2 var2 inv2 rstd2 xg_ready gram_psum gram_added
            gram_zero""".split()
        S = {n: sem(n) for n in names}
        x_landed = [sem(f"x_landed{i}") for i in range(WROWS)]
        x1_stored = [sem(f"x1_stored{i}") for i in range(WROWS)]

        def strip_dmas(dram, img, wr, tile):
            down = [(0, WS, WS * wr + SHIFT)] if wr < WROWS - 1 else \
                   [(0, WS - SHIFT, WS * wr + SHIFT), (WS - SHIFT, WS, 0)]
            for r0, r1, y in down:
                yield (dram[img, y:y + r1 - r0].rearrange("r (q k) c -> (r q) (k c)", k=4),
                       tile[W // 4 * r0:W // 4 * r1, wr].rearrange("p k c -> p (k c)"))

        def window_order(image, strip):
            rows = image.rearrange("c (r y) -> c r y", r=WS)
            inner = rows[:, :, SHIFT:SHIFT + (WCOLS - 1) * WS].rearrange("c r (w k) -> c w r k", w=WCOLS - 1)
            windows = strip.rearrange("c (w r k) -> c w r k", w=WCOLS, r=WS)
            return [(inner, windows[:, 0:WCOLS - 1]),
                    (rows[:, :, W - WS + SHIFT:W], windows[:, WCOLS - 1, :, 0:WS - SHIFT]),
                    (rows[:, :, 0:SHIFT], windows[:, WCOLS - 1, :, WS - SHIFT:WS])]

        COUNT = [16] * (WROWS - 1) + [32]

        def load(sp, img, wr):
            for d, s in strip_dmas(x, img, wr, X):
                sp.dma_start(s, d).then_inc(x_landed[wr], 16)

        def store(sp, img, wr):
            for d, s in strip_dmas(x1, img, wr, X1):
                sp.dma_start(d, s).then_inc(x1_stored[wr], 16)

        def turns(eng, turn, extra=None):
            def span(img, lo, hi, base):
                for wr in range(lo, hi):
                    turn(img, wr, lambda o, n=base + wr: 0 <= n + o < N)
            span(-1, WROWS - 4, WROWS, -WROWS)
            span(0, 0, WROWS, 0)
            if extra:
                with eng.Fori(1, W + 1) as img:
                    for wr in range(WROWS):
                        turn(img, wr, lambda o: True)
                        if wr % 4 == 1:
                            extra(img, wr // 4)
            with eng.Fori(W + 1 if extra else 1, B - 1) as img:
                for wr in range(WROWS):
                    turn(img, wr, lambda o: True)
            span(B - 1, 0, WROWS, WROWS * (B - 1))
            span(B, 0, 5, N)

        def at(img, wr):
            return img + wr // WROWS, wr % WROWS

        block = phase_block(nc, ctx, semaphores)

        @block.sync
        def _(sp):
            sp.dma_start(wqkv[:, :], w_qkv_t).then_inc(S["const_landed"], 16)
            sp.dma_start(wout[:, :], w_out_t).then_inc(S["const_landed"], 16)
            sp.dma_start(bout[:, :, :], bass.AP(b_out.tensor, 0, [[0, SP4], [0, 4], [1, C]])).then_inc(S["const_landed"], 16)
            sp.dma_start(own[:, :], head_own).then_inc(S["const_landed"], 16)
            sp.dma_start(masks[:, :, :, :], mask).then_inc(S["const_landed"], 16)
            wide = 2 * WS - 1
            sp.dma_start(pos_rows.rearrange("a r b -> r a b"), bass.AP(pos.tensor, WS - 1, [[wide, wide], [-1, WS], [1, WS]])
                         ).then_inc(S["pos_stored"], 16)
            sp.wait_ge(S["pos_stored"], 16)
            sp.wait_ge(S["zeroed"], 1)
            for u in range(2):
                for xi in range(WS):
                    p = UPPER * u + WS * xi
                    sp.dma_start(bias49[p:p + WS, :].rearrange("p (a b) -> p a b", a=WS), pos_rows[:, WS - 1 - xi:2 * WS - 1 - xi, :]
                                 ).then_inc(S["bias_landed"], 16)

            def turn(img, wr, has):
                n = WROWS * img + wr
                if has(4):
                    wait(sp, S["x1_ready"], n + 4 - WROWS + 1)
                    load(sp, *at(img, wr + 4))
                if has(-2):
                    i, w = at(img, wr - 2)
                    wait(sp, S["x1_ready"], n - 1)
                    store(sp, i, w)
            turns(sp, turn, lambda img, r: store_toeplitz(sp, rows, toeplitz, img - 1, r, S["toeplitz_stored"]))
            for w in range(WROWS):
                sp.wait_ge(x1_stored[w], COUNT[w] * B)
            sp.wait_ge(S["toeplitz_stored"], 16 * BLOCK)

        @block.gpsimd
        def _(pool):
            make_identity(pool, ident, S["ident_zero"], S["ident_ready"])
            pool.memset(half_neg[:, :], -0.5)
            pool.memset(eps5[:, :], 1e-5)
            pool.memset(eps6[:, :], 1e-6).then_inc(S["eps_ready"], 1)
            pool.wait_ge(S["eps_ready"], 1)
            pool.wait_ge(S["const_landed"], 80)

            def turn(img, wr, has):
                n = WROWS * img + wr

                def rstd(o, mv, ve, rs, eps, stats, var, ready):
                    m, b = n + o, (wr + o) % 2
                    pool.wait_ge(S[stats], m + 1)
                    op = pool.tensor_tensor(ve[:, :], mv[:, b, :, 1], eps[0:SP4, :], ALU.add)
                    if o == -2:
                        op = pool.tensor_scalar(minus[:, :], mv[:, b, :, 0], -1.0, 1.0, ALU.mult, ALU.mult)
                    op.then_inc(S[var], 1)
                    pool.wait_ge(S[var], m + 1)
                    pool.tensor_tensor(rs[:, b, :], ve[:, :], half_neg[0:SP4, :], ALU.pow).then_inc(S[ready], 1)

                if has(0):
                    for h in range(2):
                        pool.wait_ge(S["s_max"], 2 * n + h + 1)
                        pool.tensor_tensor(sc[:, h, :, :], sc[:, h, :, :],
                                           nmax[:, h, :].unsqueeze(2).to_broadcast([ROWS2, 8, WIN]),
                                           ALU.add).then_inc(S["s_shifted"], 1)
                if has(2):
                    rstd(2, mv1, ve1, rs1, eps6, "aggr1", "var1", "rstd1")
                if has(1):
                    m, b = n + 1, (wr + 1) % 2
                    wait(pool, S["s_psum"], 2 * (m - 1))
                    pool.wait_ge(S["k_ready"], m + 1)
                    pool.tensor_tensor(carrier[:, 1:2], half_neg[:, 0:1], half_neg[:, 1:2], ALU.mult)
                    for h in range(POOL_HEADS):
                        op = pool.tensor_scalar(kh[:, b, :, h, :], kT[:, :].rearrange("p (w k) -> p w k", w=WCOLS),
                                                own[:, h:h + 1], 1.0, ALU.mult, ALU.mult)
                    op.then_inc(S["kh_ready"], 1)
                if has(0):
                    for h in range(2):
                        pool.wait_ge(S["p_recip"], 2 * n + h + 1)
                        pool.tensor_tensor(pr[:, h, :, 0:WIN], pr[:, h, :, 0:WIN],
                                           prec[:, h, :].unsqueeze(2).to_broadcast([ROWS2, 8, WIN]),
                                           ALU.mult).then_inc(S["p_ready"], 1)
                if has(2):
                    pool.wait_ge(S["xn_ready"], n + 3)
                    pool.tensor_tensor(X[:, (wr + 2) % WROWS], X[:, (wr + 2) % WROWS], bout[:, :, :], ALU.add).then_inc(S["residual_ready"], 1)
                if has(-2):
                    wait(pool, S["rstd2"], n - 2)
                    wait(pool, S["xg_ready"], n - 3)
                    rstd(-2, mv2, ve2, rs2, eps5, "aggr2", "var2", "inv2")
                    pool.wait_ge(S["inv2"], n - 1)
                    b = wr % 2
                    pool.tensor_tensor(nb2[:, b, :], minus[:, :], rs2[:, b, :], ALU.mult).then_inc(S["rstd2"], 1)
            turns(pool, turn)

        @block.scalar
        def _(act):
            def turn(img, wr, has):
                n = WROWS * img + wr
                b1 = (wr + 1) % 2

                def turn_probs(h):
                    act.wait_ge(S["pt_psum"], 2 * (n - 1) + h + 1)
                    act.copy(prT[:, h, :, :], pt_bank[0:ROWS2, 0:4 * ROWS2].rearrange("p (a b) -> p a b", a=4)).then_inc(S["pt_ready"], 1)

                def exps(h):
                    act.wait_ge(S["s_shifted"], 2 * n + h + 1)
                    act.activation(pr[:, h, :, 0:WIN], sc[:, h, :, :], ACT.Exp).then_inc(S["p_exp"], 1)

                if has(1):
                    act.wait_ge(S["xT_psum"], n + 2)
                    for rows, windows in window_order(t_bank[:, 0:STRIP], xT[:, b1, :]):
                        op = act.copy(windows, rows)
                    op.then_inc(S["xT_ready"], 1)
                if has(-1):
                    turn_probs(0)
                if has(1):
                    act.wait_ge(S["k_psum"], n + 2)
                    wait(act, S["kh_ready"], n + 1)
                    wait(act, S["kh_ready2"], n + 1)
                    act.copy(kT[:, :], qk_bank[:, 0:STRIP]).then_inc(S["k_ready"], 1)
                if has(0):
                    exps(0)
                if has(-1):
                    turn_probs(1)
                if has(0):
                    exps(1)
                if has(1):
                    act.wait_ge(S["k_ready"], n + 2)
                    for h in range(POOL_HEADS, HEADS):
                        op = act.activation(kh[:, b1, :, h, :], kT[:, :].rearrange("p (w k) -> p w k", w=WCOLS), ACT.Copy,
                                            scale=own[:, h:h + 1])
                    op.then_inc(S["kh_ready2"], 1)
                if has(1):
                    act.wait_ge(S["v_psum"], n + 2)
                    act.copy(vh[0:WIN, (wr + 1) % 4, :, :, 0:HEAD_DIM].rearrange("p w a d -> p (w a) d"),
                             v_bank[0:WIN, :].rearrange("p (w d) -> p w d", d=HEAD_DIM))
                    act.copy(vh[UPPER:ROWS2, (wr + 1) % 4, :, :, HEAD_DIM:64].rearrange("p w a d -> p (w a) d"),
                             v_bank[UPPER:ROWS2, :].rearrange("p (w d) -> p w d", d=HEAD_DIM)).then_inc(S["v_ready"], 1)
                    act.wait_ge(S["q_psum"], n + 2)
                    act.activation(qT[:, b1, :], qk_bank[:, 0:STRIP], ACT.Copy, scale=QK_SCALE).then_inc(S["q_ready"], 1)
                if has(-1):
                    act.wait_ge(S["av_psum"], n)
                    wait(act, S["out_psum"], n - 1)
                    for rows, windows in window_order(aT[:, :], av_bank[:, 0:STRIP]):
                        op = act.copy(rows, windows)
                    op.then_inc(S["aT_ready"], 1)
                if has(-3):
                    act.wait_ge(S["rstd2"], n - 2)
                    wait(act, S["gram_psum"], n - 4)
                    for k in range(4):
                        op = act.activation(xg[:, b1, k, 0:C], X1[:, (wr - 3) % WROWS, k, :], ACT.Identity,
                                            bias=nb2[:, b1, k:k + 1], scale=rs2[:, b1, k:k + 1])
                    op.then_inc(S["xg_ready"], 1)
            act.wait_ge(S["zeroed"], 1)
            turns(act, turn)

        @block.vector
        def _(dve):
            dve.memset(pr[:, :, :, :], 0.0)
            dve.memset(vh[:, :, :, :, :], 0.0)
            dve.memset(xg[:, :, :, C:C + 1], 1.0)
            dve.memset(gram[:, :], 0.0)
            dve.memset(s_bank[0][:, :], 0.0)
            dve.memset(s_bank[1][:, :], 0.0)
            dve.memset(bias49[:, :], 0.0).then_inc(S["zeroed"], 1)
            dve.wait_ge(S["const_landed"], 80)
            dve.wait_ge(S["bias_landed"], 16 * 2 * WS)
            for kind in range(2):
                for g in range(PAIRS):
                    op = dve.tensor_tensor(bias[:, kind, g], masks[:, kind, g].unsqueeze(1).to_broadcast([ROWS2, HEADS, WIN]),
                                           bias49[:, :].unsqueeze(1).to_broadcast([ROWS2, HEADS, WIN]), ALU.add)
            op.then_inc(S["bias_ready"], 1)
            dve.wait_ge(S["bias_ready"], 1)

            def turn(img, wr, has):
                n = WROWS * img + wr

                def stats(o, tile, bn, mv, done, aggr):
                    m, b, slot = n + o, (wr + o) % 2, (wr + o) % WROWS
                    for k in range(4):
                        op = dve.bn_stats(bn[:, k, :], tile[:, slot, k, :])
                    op.then_inc(S[done], 1)
                    dve.wait_ge(S[done], m + 1)
                    dve.memset(carrier[:, 0:1], 0.0)
                    for k in range(4):
                        op = dve.bn_aggr(mv[:, b, k, :], bn[:, k, :])
                    op.then_inc(S[aggr], 1)

                def normalise(o, tile, mv, rs, out, ready, done):
                    m, b, slot = n + o, (wr + o) % 2, (wr + o) % WROWS
                    dve.wait_ge(S[ready], m + 1)
                    for k in range(4):
                        op = dve.tensor_scalar(out[:, b, k, 0:C], tile[:, slot, k, :], mv[:, b, k, 0:1], rs[:, b, k:k + 1],
                                               ALU.subtract, ALU.mult)
                    op.then_inc(S[done], 1)

                if has(0):
                    for h in range(2):
                        dve.wait_ge(S["s_psum"], 2 * n + h + 1)
                        wait(dve, S["p_exp"], 2 * n + h - 1)
                        kind = int(wr == WROWS - 1)
                        dve.tensor_tensor(sc[:, h, :, :].rearrange("p a b -> p (a b)"), s_bank[h][0:ROWS2, 0:HALF],
                                          bias[:, kind, 2 * h:2 * h + 2].rearrange("p g a b -> p (g a b)"), ALU.add).then_inc(S["s_biased"], 1)
                        dve.wait_ge(S["s_biased"], 2 * n + h + 1)
                        dve.tensor_reduce(nmax[:, h, :], sc[:, h, :, :], AX.X, ALU.max, negate=True).then_inc(S["s_max"], 1)
                if has(2):
                    i, w = at(img, wr + 2)
                    dve.wait_ge(x_landed[w], COUNT[w] * (i + 1))
                    stats(2, X, bn1, mv1, "stats1", "aggr1")
                if has(0):
                    for h in range(2):
                        dve.wait_ge(S["p_exp"], 2 * n + h + 1)
                        dve.tensor_reduce(psum_[:, h, :], pr[:, h, :, 0:WIN], AX.X, ALU.add).then_inc(S["p_sum"], 1)
                        dve.wait_ge(S["p_sum"], 2 * n + h + 1)
                        dve.reciprocal(prec[:, h, :], psum_[:, h, :]).then_inc(S["p_recip"], 1)
                if has(2):
                    wait(dve, S["xT_psum"], n + 1)
                    normalise(2, X, mv1, rs1, xn, "rstd1", "xn_ready")
                if has(-4):
                    dve.wait_ge(S["gram_psum"], n - 3)
                    wait(dve, S["gram_added"], n - 4)
                    dve.tensor_tensor(gram[:, :], t_bank[:, 0:C + 1], gram[:, :], ALU.add).then_inc(S["gram_added"], 1)
                if has(-2):
                    i, w = at(img, wr - 2)
                    dve.wait_ge(S["out_psum"], n - 1)
                    dve.wait_ge(S["residual_ready"], n - 1)
                    wait(dve, x1_stored[w], COUNT[w] * i)
                    dve.tensor_tensor(X1[:, w].rearrange("p k c -> p (k c)"), out_bank[0:SP4, :],
                                      X[:, w].rearrange("p k c -> p (k c)"), ALU.add).then_inc(S["x1_ready"], 1)
                    dve.wait_ge(S["x1_ready"], n - 1)
                    wait(dve, S["var2"], n - 3)
                    stats(-2, X1, bn2, mv2, "stats2", "aggr2")
            turns(dve, turn)
            dve.wait_ge(S["gram_added"], N)

        @block.tensor
        def _(pe):
            pe.wait_ge(S["ident_ready"], 1)
            pe.wait_ge(S["const_landed"], 80)
            pe.wait_ge(S["zeroed"], 1)

            def turn(img, wr, has):
                n = WROWS * img + wr
                b0, b1 = wr % 2, (wr + 1) % 2

                def scores(h):
                    pe.wait_ge(S["kh_ready"], n + 1)
                    pe.wait_ge(S["kh_ready2"], n + 1)
                    pe.wait_ge(S["q_ready"], n + 1)
                    wait(pe, S["s_biased"], 2 * n + h - 1)
                    for g in range(2):
                        for u in range(2):
                            w = 4 * h + 2 * g + u
                            op = pe.matmul(s_bank[h][UPPER * u:UPPER * u + WIN, HALF // 2 * g:HALF // 2 * (g + 1)],
                                           qT[:, b0, WIN * w:WIN * (w + 1)], kh[:, b0, w].rearrange("c h k -> c (h k)"), start=True, stop=True)
                    op.then_inc(S["s_psum"], 1)

                def turn_probs(h):
                    m = n - 1
                    pe.wait_ge(S["p_ready"], 2 * m + h + 1)
                    wait(pe, S["pt_ready"], 2 * m + h)
                    for g in range(2):
                        for a in range(2):
                            q = 2 * g + a
                            op = pe.transpose(pt_bank[:, q * ROWS2:(q + 1) * ROWS2],
                                              pr[:, h, 4 * g + 2 * a:4 * g + 2 * a + 2, :].rearrange("p a b -> p (a b)"),
                                              ident[0:ROWS2, 0:ROWS2])
                    op.then_inc(S["pt_psum"], 1)

                def attend(h):
                    m, b = n - 1, (wr - 1) % 4
                    pe.wait_ge(S["pt_ready"], 2 * m + h + 1)
                    if h == 0:
                        pe.wait_ge(S["v_ready"], m + 1)
                        wait(pe, S["aT_ready"], m)
                    for g in range(2):
                        for u in range(2):
                            w = 4 * h + 2 * g + u
                            for a in range(2):
                                op = pe.matmul(av_bank[64 * a:64 * (a + 1), w * WIN:(w + 1) * WIN], vh[:, b, w, a, :],
                                               prT[:, h, 2 * g + a, UPPER * u:UPPER * u + WIN], start=True, stop=True)
                    if h == 1:
                        op.then_inc(S["av_psum"], 1)

                if has(1):
                    pe.wait_ge(S["xn_ready"], n + 2)
                    wait(pe, S["gram_added"], n - 4)
                    for k in range(4):
                        op = pe.transpose(t_bank[:, k:STRIP:4], xn[:, b1, k, :], ident[0:SP4, 0:SP4])
                    op.then_inc(S["xT_psum"], 1)
                if has(0):
                    scores(0)
                if has(-1):
                    turn_probs(0)
                if has(0):
                    scores(1)
                if has(-2):
                    pe.wait_ge(S["aT_ready"], n - 1)
                    wait(pe, S["x1_ready"], n - 2)
                    for k in range(4):
                        op = pe.matmul(out_bank[0:SP4, k * C:(k + 1) * C], aT[:, k::4], wout[:, :], start=True, stop=True)
                    op.then_inc(S["out_psum"], 1)
                if has(1):
                    pe.wait_ge(S["xT_ready"], n + 2)
                    wait(pe, S["q_ready"], n + 1)
                    pe.matmul(qk_bank[:, 0:STRIP], wqkv[:, C:2 * C], xT[:, b1, :], start=True, stop=True).then_inc(S["k_psum"], 1)
                if has(-1):
                    attend(0)
                    turn_probs(1)
                if has(1):
                    wait(pe, S["v_ready"], n + 1)
                    for w in range(WCOLS):
                        for e in range(2):
                            op = pe.matmul(v_bank[UPPER * e:UPPER * e + WIN, 64 * w:64 * (w + 1)], xT[:, b1, WIN * w:WIN * (w + 1)],
                                           wqkv[:, 2 * C:].rearrange("c (a e d) -> c e a d", a=2, e=2)[:, e], start=True, stop=True)
                    op.then_inc(S["v_psum"], 1)
                    pe.wait_ge(S["k_ready"], n + 2)
                    pe.matmul(qk_bank[:, 0:STRIP], wqkv[:, 0:C], xT[:, b1, :], start=True, stop=True).then_inc(S["q_psum"], 1)
                if has(-4):
                    pe.wait_ge(S["xg_ready"], n - 3)
                    wait(pe, S["gram_added"], n - 4)
                    for k in range(4):
                        op = pe.matmul(t_bank[:, 0:C + 1], xg[:, b0, k, 0:C], xg[:, b0, k, :], start=k == 0, stop=k == 3)
                    op.then_inc(S["gram_psum"], 1)
                if has(-1):
                    attend(1)
            turns(pe, turn)


def head_channels():
    return np.repeat(np.eye(HEADS, dtype=np.float32), HEAD_DIM, 0)


def window_masks():
    m = np.zeros((ROWS2, 2, PAIRS, WIN), np.float32)
    r, c = np.divmod(np.arange(WIN), WS)
    low, right = r >= WS - SHIFT, c >= WS - SHIFT
    up_down = low[:, None] != low[None, :]
    left_right = right[:, None] != right[None, :]
    for kind in range(2):
        for g in range(PAIRS):
            for u in range(2):
                bad = np.zeros((WIN, WIN), bool)
                if kind == 1:
                    bad |= up_down
                if g == PAIRS - 1 and u == 1:
                    bad |= left_right
                m[UPPER * u:UPPER * u + WIN, kind, g][bad] = MASKED
    return m


BF16 = mybir.dt.bfloat16
STEPS = 32
RUN = STEPS // 2
CHUNKS = TOKENS // STEPS
PER_BANK = 512 // B
BANKS = STEPS // PER_BANK


def recurrent_phase(nc, x1, w, w_t, v_t, gamma, beta, gram, x2, xc):
    nc.disable_value_cache = True
    with ExitStack() as ctx:
        def sb(name, shape, dt=F32):
            return ctx.enter_context(nc.sbuf_tensor("r_" + name, shape, dt))

        def bank(name):
            return ctx.enter_context(nc.psum_tensor("r_" + name, [128, 512], F32))

        semaphores = []

        def sem(name):
            semaphores.append(ctx.enter_context(nc.semaphore("r_" + name)))
            return semaphores[-1]

        ident = sb("ident", [128, 128])
        wn = sb("wn", [128, C])
        wt = sb("wt", [128, C])
        vt = sb("vt", [128, C])
        gb = sb("gb", [128, 2])
        ones = sb("ones", [128, 1])
        ones3 = sb("ones3", [3, 512], BF16)
        prod = sb("prod", [128, C])
        mom = sb("mom", [128, 4])
        col = sb("col", [128, 8])
        half_neg = sb("half_neg", [128, RUN])
        eps5 = sb("eps5", [128, RUN])
        eps6 = sb("eps6", [128, RUN])
        carrier = sb("carrier", [128, 3])
        ws = sb("ws", [128, C])
        wst = sb("wst", [128, C])
        part16 = sb("part16", [128, 4], BF16)
        parts = sb("parts", [128, 3])
        shift = sb("shift", [3, C], BF16)
        X = sb("X", [128, 4, RUN, C])
        xn = sb("xn", [128, 2, RUN, C])
        xT = sb("xT", [128, 2, 2, RUN, B])
        Y = sb("Y", [128, 2, RUN, 2, B])
        X2 = sb("X2", [128, 2, RUN, C])
        XC = sb("XC", [128, 2, RUN, C])
        bn = [sb("bn1", [128, RUN, 6]), sb("bn2", [128, RUN, 6])]
        mv = [sb("mv1", [128, RUN, 2]), sb("mv2", [128, RUN, 2])]
        ve = [sb("ve1", [128, RUN]), sb("ve2", [128, RUN])]
        rs = [sb("rs1", [128, RUN]), sb("rs2", [128, RUN])]
        nm = [sb("nm1", [128, RUN]), sb("nm2", [128, RUN])]
        nb = [sb("nb1", [128, RUN]), sb("nb2", [128, RUN])]

        z_bank = [bank(f"z{i}") for i in range(BANKS)]
        t_bank = [bank("t0"), bank("t1")]
        o_bank = [bank("o0"), bank("o1")]

        names = """eps_ready ident_zero ident_ready const_landed zeroed moments prod_ready sums col_step
            scaled transposed shift_ready bn_norm z_psum y_ready
            t_psum xT_ready o_psum x2_ready stats1 aggr1 stats2 aggr2
            var1 inv1 nb1 xn_ready var2 inv2 nb2 xc_ready""".split()
        S = {n: sem(n) for n in names}
        x_landed = [sem(f"x_landed{i}") for i in range(4)]
        x2_stored = [sem(f"x2_stored{i}") for i in range(2)]
        xc_stored = [sem(f"xc_stored{i}") for i in range(2)]
        z_psum, y_ready = S["z_psum"], S["y_ready"]

        def turns(eng, turn):
            def one(q):
                turn(q, q % 4, lambda o: 0 <= q + o < CHUNKS)
            for q in range(-3, 6):
                one(q)
            with eng.Fori(1, (CHUNKS - 6) // 4) as i:
                for j in range(2, 6):
                    turn(4 * i + j, j % 4, lambda o: True)
            for q in range(CHUNKS - 4, CHUNKS + 2):
                one(q)

        def chunk(dram, q, s):
            return dram.rearrange("b h w c -> b (h w) c").rearrange("b (n k) c -> b n k c", k=RUN)[:, 2 * q + s]

        block = phase_block(nc, ctx, semaphores)

        @block.sync
        def _(sp):
            for dst, src in ((wn, w), (wt, w_t), (vt, v_t)):
                sp.dma_start(dst[:, :], src).then_inc(S["const_landed"], 16)
            for i, src in enumerate((gamma, beta)):
                sp.dma_start(gb[:, i:i + 1], src.rearrange("(p a) -> p a", a=1)).then_inc(S["const_landed"], 16)

            def turn(q, j, has):
                if has(3):
                    wait(sp, S["x2_ready"], 4 * q)
                    for s in range(2):
                        sp.dma_start(X[B * s:B * (s + 1), (j + 3) % 4], chunk(x1, q + 3, s)).then_inc(x_landed[(j + 3) % 4], 16)
                if has(-1):
                    wait(sp, S["x2_ready"], 4 * q)
                    for s in range(2):
                        sp.dma_start(chunk(x2, q - 1, s), X2[B * s:B * (s + 1), (j - 1) % 2]).then_inc(x2_stored[(j - 1) % 2], 16)
                if has(-2):
                    wait(sp, S["xc_ready"], q - 1)
                    for s in range(2):
                        sp.dma_start(chunk(xc, q - 2, s), XC[B * s:B * (s + 1), j % 2]).then_inc(xc_stored[j % 2], 16)
            turns(sp, turn)
            for i in range(2):
                sp.wait_ge(x2_stored[i], 16 * CHUNKS)
                sp.wait_ge(xc_stored[i], 16 * CHUNKS)

        @block.gpsimd
        def _(pool):
            make_identity(pool, ident, S["ident_zero"], S["ident_ready"])
            pool.memset(half_neg[:, :], -0.5)
            pool.memset(eps5[:, :], 1e-5)
            pool.memset(eps6[:, :], 1e-6).then_inc(S["eps_ready"], 1)
            pool.wait_ge(S["eps_ready"], 1)
            pool.wait_ge(S["sums"], 2)
            pool.tensor_tensor(mom[:, 3:4], mom[:, 2:3], half_neg[:, 0:1], ALU.pow).then_inc(S["bn_norm"], 1)

            def turn(q, j, has):
                def normalise(w, o, m, eps, src, dst, done):
                    a, b, c = f"var{w + 1}", f"inv{w + 1}", f"nb{w + 1}"
                    pool.wait_ge(S[f"aggr{w + 1}"], m + 1)
                    pool.tensor_tensor(ve[w][:, :], mv[w][:, :, 1], eps[:, :], ALU.add)
                    pool.tensor_scalar(nm[w][:, :], mv[w][:, :, 0], -1.0, 1.0, ALU.mult, ALU.mult).then_inc(S[a], 1)
                    pool.wait_ge(S[a], m + 1)
                    pool.tensor_tensor(rs[w][:, :], ve[w][:, :], half_neg[:, :], ALU.pow).then_inc(S[b], 1)
                    pool.wait_ge(S[b], m + 1)
                    pool.tensor_tensor(nb[w][:, :], nm[w][:, :], rs[w][:, :], ALU.mult).then_inc(S[c], 1)
                    pool.wait_ge(S[c], m + 1)
                    pool.tensor_tensor(carrier[:, 0:1], half_neg[:, 0:1], half_neg[:, 1:2], ALU.mult)
                    for k in range(RUN):
                        op = pool.tensor_scalar(dst[:, k, :], src[:, k, :], rs[w][:, k:k + 1], nb[w][:, k:k + 1], ALU.mult, ALU.add)
                    op.then_inc(S[done], 1)
                if has(-2):
                    wait(pool, xc_stored[j % 2], 16 * (q - 2) if j % 2 == 0 else 16 * (q - 3))
                    normalise(1, -2, q - 2, eps6, X2[:, j % 2], XC[:, j % 2], "xc_ready")
                if has(2):
                    wait(pool, S["t_psum"], 4 * (q + 1))
                    normalise(0, 2, q + 2, eps5, X[:, (j + 2) % 4], xn[:, j % 2], "xn_ready")
            turns(pool, turn)

        @block.scalar
        def _(act):
            def turn(q, j, has):
                if has(0):
                    for t in range(STEPS):
                        n = t % PER_BANK
                        act.wait_ge(z_psum, STEPS * q + t + 1)
                        act.activation(Y[:, j % 2, t % RUN, t // RUN, :], z_bank[t // PER_BANK][:, B * n:B * (n + 1)],
                                       ACT.Sigmoid
                                       ).then_inc(y_ready, 1)
            turns(act, turn)

        @block.vector
        def _(dve):
            inv_n = 1.0 / (B * TOKENS)
            dve.memset(ones[:, :], 1.0)
            dve.memset(ones3[:, :], 1.0)
            dve.memset(Y[:, 1, RUN - 1, 1, :], 0.0).then_inc(S["zeroed"], 1)
            dve.wait_ge(S["const_landed"], 80)
            dve.wait_ge(S["moments"], 1)
            dve.tensor_tensor(prod[:, :], t_bank[0][:, 0:C], wt[:, :], ALU.mult).then_inc(S["prod_ready"], 1)
            dve.wait_ge(S["moments"], 2)
            dve.tensor_scalar(mom[:, 0:2], t_bank[1][:, 0:2], inv_n, None, ALU.mult).then_inc(S["col_step"], 1)
            dve.wait_ge(S["col_step"], 1)
            dve.tensor_tensor(col[:, 0:1], mom[:, 1:2], mom[:, 1:2], ALU.mult).then_inc(S["col_step"], 1)
            dve.wait_ge(S["col_step"], 2)
            dve.tensor_tensor(col[:, 1:2], mom[:, 0:1], col[:, 0:1], ALU.subtract).then_inc(S["col_step"], 1)
            dve.wait_ge(S["col_step"], 3)
            dve.tensor_scalar(mom[:, 2:3], col[:, 1:2], 1e-5, None, ALU.add).then_inc(S["sums"], 2)
            dve.wait_ge(S["bn_norm"], 1)
            dve.tensor_tensor(col[:, 2:3], mom[:, 3:4], gb[:, 0:1], ALU.mult).then_inc(S["col_step"], 1)
            dve.wait_ge(S["col_step"], 4)
            dve.tensor_scalar(ws[:, :], wn[:, :], col[:, 2:3], None, ALU.mult).then_inc(S["scaled"], 1)
            dve.tensor_tensor(col[:, 3:4], mom[:, 1:2], col[:, 2:3], ALU.mult).then_inc(S["col_step"], 1)
            dve.wait_ge(S["col_step"], 5)
            dve.tensor_tensor(col[:, 4:5], gb[:, 1:2], col[:, 3:4], ALU.subtract).then_inc(S["col_step"], 1)
            for i in range(3):
                dve.wait_ge(S["col_step"], 6 + 3 * i)
                dve.tensor_copy(part16[:, i:i + 1], col[:, 4 + i:5 + i]).then_inc(S["col_step"], 1)
                dve.wait_ge(S["col_step"], 7 + 3 * i)
                dve.tensor_copy(parts[:, i:i + 1], part16[:, i:i + 1]).then_inc(S["col_step"], 1)
                dve.wait_ge(S["col_step"], 8 + 3 * i)
                dve.tensor_tensor(col[:, 5 + i:6 + i], col[:, 4 + i:5 + i], parts[:, i:i + 1], ALU.subtract).then_inc(S["col_step"], 1)
            dve.wait_ge(S["col_step"], 15)
            dve.wait_ge(S["transposed"], 1)
            dve.tensor_copy(wst[:, :], o_bank[0][:, 0:C])
            dve.wait_ge(S["transposed"], 2)
            dve.tensor_copy(shift[:, :], o_bank[1][0:3, 0:C]).then_inc(S["shift_ready"], 1)

            def turn(q, j, has):
                p = (j - 1) % 2
                if has(2):
                    dve.wait_ge(x_landed[(j + 2) % 4], 8 * (q + 2) - 8 * ((j + 2) % 4) + 32)
                    wait(dve, S["nb1"], q + 2)
                    for k in range(RUN):
                        op = dve.bn_stats(bn[0][:, k, :], X[:, (j + 2) % 4, k, :])
                    op.then_inc(S["stats1"], 1)
                    dve.wait_ge(S["stats1"], q + 3)
                    dve.memset(carrier[:, 1:2], 0.0)
                    for k in range(RUN):
                        op = dve.bn_aggr(mv[0][:, k, :], bn[0][:, k, :])
                    op.then_inc(S["aggr1"], 1)
                if has(-1):
                    wait(dve, x2_stored[p], 16 * (q - 1) - 16 * p)
                    wait(dve, S["nb2"], q - 1)
                    wait(dve, S["xc_ready"], q - 2)
                for g in range(4):
                    ks = range(4 * g, 4 * g + 4)
                    if has(1):
                        dve.wait_ge(S["t_psum"], 4 * (q + 1) + g + 1)
                        dve.tensor_copy(xT[:, (j + 1) % 2, :, 4 * g:4 * g + 4, :].rearrange("c s k b -> c k s b"),
                                        t_bank[g % 2][:, :].rearrange("c (k s b) -> c k s b", k=4, s=2)).then_inc(S["xT_ready"], 1)
                    if has(-1):
                        dve.wait_ge(S["o_psum"], 4 * (q - 1) + g + 1)
                        dve.tensor_tensor(X2[:, p, 4 * g:4 * g + 4, :].rearrange("p k c -> p (k c)"), o_bank[g % 2][:, :],
                                          X[:, (j - 1) % 4, 4 * g:4 * g + 4, :].rearrange("p k c -> p (k c)"), ALU.add
                                          ).then_inc(S["x2_ready"], 1)
                    if has(-1):
                        dve.wait_ge(S["x2_ready"], 4 * (q - 1) + g + 1)
                        for k in ks:
                            op = dve.bn_stats(bn[1][:, k, :], X2[:, p, k, :])
                        if g == 3:
                            op.then_inc(S["stats2"], 1)
                if has(-1):
                    dve.wait_ge(S["stats2"], q)
                    dve.memset(carrier[:, 2:3], 0.0)
                    for k in range(RUN):
                        op = dve.bn_aggr(mv[1][:, k, :], bn[1][:, k, :])
                    op.then_inc(S["aggr2"], 1)
            turns(dve, turn)

        @block.tensor
        def _(pe):
            pe.wait_ge(S["const_landed"], 80)
            pe.wait_ge(S["zeroed"], 1)
            pe.matmul(t_bank[0][:, 0:C], gram[:, 0:C], wt[:, :], start=True, stop=True).then_inc(S["moments"], 1)
            pe.wait_ge(S["prod_ready"], 1)
            pe.matmul(t_bank[1][:, 0:1], prod[:, :], ones[:, :], start=True, stop=True)
            pe.matmul(t_bank[1][:, 1:2], wt[:, :], gram[:, C:C + 1], start=True, stop=True).then_inc(S["moments"], 1)
            pe.wait_ge(S["ident_ready"], 1)
            pe.wait_ge(S["scaled"], 1)
            pe.transpose(o_bank[0][:, 0:C], ws[:, :], ident[:, :]).then_inc(S["transposed"], 1)
            pe.wait_ge(S["col_step"], 15)
            pe.transpose(o_bank[1][0:3, 0:C], parts[:, :], ident[:, :]).then_inc(S["transposed"], 1)
            pe.wait_ge(S["shift_ready"], 1)

            def turn(q, j, has):
                def turn_in(k):
                    if k == 0:
                        pe.wait_ge(S["xn_ready"], q + 2)
                    if k % 4 == 0:
                        wait(pe, S["xT_ready"], 4 * (q + 1) + k // 4 - 1)
                    g = k // 4
                    op = pe.transpose(t_bank[g % 2][:, C * (k % 4):C * (k % 4 + 1)], xn[:, (j + 1) % 2, k, :], ident[:, :])
                    if k % 4 == 3:
                        op.then_inc(S["t_psum"], 1)

                def turn_out(k):
                    if k == 0:
                        pe.wait_ge(y_ready, STEPS * q)
                    if k % 4 == 0:
                        wait(pe, S["x2_ready"], 4 * (q - 1) + k // 4 - 1)
                    g = k // 4
                    op = pe.transpose(o_bank[g % 2][:, C * (k % 4):C * (k % 4 + 1)],
                                      Y[:, (j - 1) % 2, k].rearrange("c s b -> c (s b)"), ident[:, :])
                    if k % 4 == 3:
                        op.then_inc(S["o_psum"], 1)

                def start_bank(o, s):
                    wait(pe, y_ready, STEPS * (q + o - 1) + PER_BANK * (s + 1))
                    pe.matmul(z_bank[s][:, :], shift[:, :], ones3[:, :], start=True, stop=True)

                def inputs(o, s, piece):
                    t = PER_BANK * s + 2 * piece
                    half, k = divmod(t, RUN)
                    pe.wait_ge(S["xT_ready"], 4 * (q + o) + k // 4 + 1)
                    pe.matmul(z_bank[s][:, 2 * B * piece:2 * B * (piece + 1)], wst[:, :],
                              xT[:, (j + o) % 2, half, k:k + 2].rearrange("c k b -> c (k b)"), start=False, stop=True,
                              skip_group_check=True)

                def step(t):
                    before = Y[:, j % 2, (t - 1) % RUN, (t - 1) // RUN] if t else Y[:, (j - 1) % 2, RUN - 1, 1]
                    wait(pe, y_ready, STEPS * q + t)
                    n = t % PER_BANK
                    pe.matmul(z_bank[t // PER_BANK][:, B * n:B * (n + 1)], vt[:, :], before, start=False, stop=True,
                              skip_group_check=True).then_inc(z_psum, 1)

                first = [0, 1, 1, 4, 4, 6, 6, 8, 8]
                for t in range(STEPS):
                    if has(0):
                        step(t)
                    b, n = divmod(t, PER_BANK)
                    o, s = divmod(b + 1, BANKS)
                    if n == 0 and has(o):
                        start_bank(o, s)
                    if n % 2 == 1 and has(o):
                        inputs(o, s, n // 2)
                    for k in range(first[n], first[n + 1]):
                        if k % 2 == 0 and has(1):
                            turn_in(4 * b + k // 2)
                        if k % 2 == 1 and has(-1):
                            turn_out(4 * b + k // 2)
            turns(pe, turn)


def convolution_phase(nc, xc, x2, toeplitz, k_a, k_ga, w_out, b_out, x3):
    nc.disable_value_cache = True
    with ExitStack() as ctx:
        def sb(name, shape):
            return ctx.enter_context(nc.sbuf_tensor("c_" + name, shape, F32))

        semaphores = []

        def sem(name):
            semaphores.append(ctx.enter_context(nc.semaphore("c_" + name)))
            return semaphores[-1]

        ident = sb("ident", [128, 128])
        wout = sb("wout", [128, C])
        bout = sb("bout", [BLOCK, 4, C])
        ka = sb("ka", [128, KS * KS])
        kga = sb("kga", [128, KS * KS])
        xt = sb("xt", [BLOCK, GROUP, SLOTS, C])
        tz = sb("tz", [BLOCK, 2, CHUNK, 2, TZ])
        e1 = sb("e1", [BLOCK, 2, 2, NPIX])
        bt = sb("bt", [BLOCK, 2, 2, NPIX])
        ab = sb("ab", [BLOCK, 2, 2, NPIX])
        around = sb("around", [128, CR, CC, GROUP])
        tap = sb("tap", [128, 2, NCORNER])
        gate = sb("gate", [128, NCORNER])
        fac = sb("fac", [128, 4, NCORNER])
        hT = sb("hT", [128, 2, 4, BLOCK])
        XR = sb("XR", [BLOCK, 4, 4, C])
        X3 = sb("X3", [BLOCK, 4, 4, C])
        conv = [ctx.enter_context(nc.psum_tensor(f"c_conv{i}", [128, 2, 512], F32)) for i in range(2)]
        th = [ctx.enter_context(nc.psum_tensor(f"c_th{i}", [128, 512], F32)) for i in range(2)]
        ob = [ctx.enter_context(nc.psum_tensor(f"c_ob{i}", [128, 512], F32)) for i in range(2)]

        names = """ident_zero ident_ready const_landed conv_psum gate_exp plus1 recip b_ready abs_ready
            b_exp b_log h_ready turned evacuated around_ready tap_step gated corner_exp corner_step
            corner_ready ob_psum x3_ready residual_ready""".split()
        S = {n: sem(n) for n in names}
        image_landed = [sem(f"image_landed{i}") for i in range(GROUP)]
        tz_landed = [sem(f"tz_landed{i}") for i in range(2)]
        xr_landed = [sem(f"xr_landed{i}") for i in range(4)]
        x3_stored = [sem(f"x3_stored{i}") for i in range(4)]

        PAIRS_G = C // 2
        NEAR = 2 * GROUP
        STRIPS = BLOCKS // 4
        SECOND = GROUP * STRIPS
        TURNS = NEAR + SECOND
        CORNER_STEPS = 10
        near_blocks = [[BLOCKS - 3, BLOCKS - 2, BLOCKS - 1, 0], [1, 2, 3]]

        def second_dmas(s):
            img, k = divmod(s, STRIPS)
            if k < STRIPS - 1:
                return img, [(slice(0, BLOCK), slice(0, 4), 8 * k + 1)]
            return img, [(slice(0, BLOCK), slice(0, 3), 8 * k + 1), (slice(0, W), slice(3, 4), H - 1),
                         (slice(W, BLOCK), slice(3, 4), 0)]
        before = {s: 16 * sum(len(second_dmas(t)[1]) for t in range(s % 4, s, 4)) for s in range(SECOND + 4)}
        whole = [before[SECOND + i] if (SECOND + i) % 4 == i else None for i in range(4)]

        def second_views(dram, tile, g, s):
            img, parts = second_dmas(s)
            for p, k, row in parts:
                rows = (p.stop - p.start) // W
                n = k.stop - k.start
                tokens = dram[g * GROUP + img].rearrange("h w c -> (h w) c")
                yield (bass.AP(tokens.tensor, tokens.offset + row * W * C, [[C, rows * W], [BLOCK * C, n], [1, C]]),
                       tile[p, s % 4, k, :])

        block = phase_block(nc, ctx, semaphores)

        @block.sync
        def _(sp):
            sp.dma_start(wout[:, :], w_out).then_inc(S["const_landed"], 16)
            sp.dma_start(bout[:, :, :], bass.AP(b_out.tensor, 0, [[0, BLOCK], [0, 4], [1, C]])).then_inc(S["const_landed"], 16)
            sp.dma_start(ka[:, :], k_a.rearrange("c a b -> c (a b)")).then_inc(S["const_landed"], 16)
            sp.dma_start(kga[:, :], k_ga.rearrange("c a b -> c (a b)")).then_inc(S["const_landed"], 16)

            def image(g, i):
                src = xc[g * GROUP + i].rearrange("(n r) w c -> (r w) n c", r=2)
                sp.dma_start(xt[:, i, 1:1 + BLOCKS, :], src).then_inc(image_landed[i], 16)
                sp.dma_start(xt[:, i, 0:1, :], src[:, BLOCKS - 1:BLOCKS]).then_inc(image_landed[i], 16)
                sp.dma_start(xt[:, i, 1 + BLOCKS:SLOTS, :], src[:, 0:2]).then_inc(image_landed[i], 16)

            def matrices(g):
                with sp.Fori(0, C // (2 * CHUNK)) as i:
                    for b in range(2):
                        sp.wait_ge(S["b_ready"], PAIRS_G * g + 4 * i + 2 * b + 1)
                        sp.dma_start(tz[:, b].rearrange("p c i t -> p (c i t)"),
                                     toeplitz.rearrange("p (n c) i t -> p n (c i t)", c=CHUNK)[:, 2 * i + b]).then_inc(tz_landed[b], 16)

            for i in range(GROUP):
                image(0, i)
            with sp.Fori(0, GROUPS - 1) as g:
                matrices(g)
                for i in range(GROUP):
                    sp.wait_ge(S["turned"], TURNS * g + NEAR + STRIPS * (i + 1))
                    image(g + 1, i)
            matrices(GROUPS - 1)

        @block.gpsimd
        def _(pool):
            make_identity(pool, ident, S["ident_zero"], S["ident_ready"])
            pool.wait_ge(S["const_landed"], 64)
            with pool.Fori(0, GROUPS) as g:
                pool.wait_ge(S["around_ready"], g + 1)
                pool.tensor_tensor(tap[:, 0, 0:1], ka[:, 0:1], ka[:, 0:1], ALU.mult)
                for t in range(KS * KS):
                    a, b = KS - 1 - t // KS, KS - 1 - t % KS
                    view = around[:, a:a + KS, b:b + KS, :].rearrange("c a b i -> c a (b i)")
                    out = gate[:, :] if t == 0 else tap[:, t % 2, :]
                    pool.tensor_scalar(out.rearrange("c (a b) -> c a b", a=KS), view, kga[:, t:t + 1], 1.0, ALU.mult, ALU.mult
                                       ).then_inc(S["tap_step"], 1)
                    if t:
                        pool.wait_ge(S["tap_step"], 2 * KS * KS * g + 2 * t)
                        pool.tensor_tensor(gate[:, :], gate[:, :], tap[:, t % 2, :], ALU.add).then_inc(S["tap_step"], 1)
                pool.wait_ge(S["tap_step"], 2 * KS * KS * g + 2 * KS * KS - 1)
                pool.tensor_tensor(tap[:, 0, 0:1], ka[:, 0:1], ka[:, 0:1], ALU.mult).then_inc(S["tap_step"], 1)
                pool.tensor_tensor(tap[:, 1, 0:1], ka[:, 0:1], ka[:, 0:1], ALU.mult).then_inc(S["gated"], 1)
                for s in range(SECOND):
                    pool.wait_ge(xr_landed[s % 4], whole[s % 4] * g + before[s + 4])
                    pool.tensor_tensor(XR[:, s % 4], XR[:, s % 4], bout[:, :, :], ALU.add).then_inc(S["residual_ready"], 1)

        def load_residual(act, g, s):
            for d, t in second_views(x2, XR, g, s):
                act.dma_start(t, d).then_inc(xr_landed[s % 4], 16)

        @block.scalar
        def _(act):
            act.preload_act_table_set("natural_log_exp_and_others")
            with act.Fori(0, GROUPS) as g:
                with act.Fori(0, C // (2 * CHUNK)) as i:
                    def gates(k):
                        act.wait_ge(S["conv_psum"], PAIRS_G * g + 4 * i + k + 1)
                        act.activation(e1[:, k % 2], conv[k % 2][0:BLOCK, :, NPIX:2 * NPIX], ACT.Exp, scale=-1.0).then_inc(S["gate_exp"], 1)

                    def log_part(k):
                        n, p = PAIRS_G * g + 4 * i + k, k % 2
                        act.wait_ge(S["abs_ready"], n + 1)
                        act.activation(ab[:, p], ab[:, p], ACT.Exp, scale=-1.0).then_inc(S["b_exp"], 1)
                        act.wait_ge(S["b_exp"], n + 1)
                        act.activation(ab[:, p], ab[:, p], ACT.Ln, bias=1.0).then_inc(S["b_log"], 1)
                    gates(0)
                    for k in range(4):
                        if k + 1 < 4:
                            gates(k + 1)
                        log_part(k)
                for s in range(3):
                    load_residual(act, g, s)
                act.wait_ge(S["gated"], g + 1)
                act.activation(fac[:, 0, :], gate[:, :], ACT.Exp, scale=-1.0).then_inc(S["corner_exp"], 1)
                act.wait_ge(S["corner_step"], CORNER_STEPS * g + 3)
                act.activation(fac[:, 1, :], fac[:, 0, :], ACT.Exp).then_inc(S["corner_exp"], 1)
                act.activation(fac[:, 2, :], fac[:, 0, :], ACT.Exp, scale=-1.0).then_inc(S["corner_exp"], 1)
                for s in range(SECOND + 1):
                    if s + 3 < SECOND:
                        if s:
                            act.wait_ge(S["x3_ready"], SECOND * g + s + 2)
                        load_residual(act, g, s + 3)
                    if s:
                        act.wait_ge(S["x3_ready"], SECOND * g + s + 2)
                        for d, t in second_views(x3, X3, g, s - 1):
                            act.dma_start(d, t).then_inc(x3_stored[(s - 1) % 4], 16)
                for i in range(4):
                    act.wait_ge(x3_stored[i], whole[i] * g + whole[i])

        @block.vector
        def _(dve):
            dve.memset(e1[:, :, :, :], 0.0).then_inc(S["b_ready"], 3)
            dve.memset(hT[:, :, :, :], 0.0).then_inc(S["evacuated"], 2)
            dve.memset(X3[:, :, :, :], 0.0).then_inc(S["x3_ready"], 2)
            dve.wait_ge(S["const_landed"], 64)
            with dve.Fori(0, GROUPS) as g:
                n = 0
                for img in range(GROUP):
                    for half, blocks in enumerate(near_blocks):
                        dve.wait_ge(S["turned"], TURNS * g + n + 1)
                        m = len(blocks)
                        src = th[n % 2][:, 0:m * BLOCK].rearrange("c (a b) -> c a b", b=W)
                        rows = around[:, 8 * half:8 * half + 2 * m, :, img]
                        dve.tensor_copy(rows[:, :, 0:KS - 1], src[:, :, W - KS + 1:W])
                        op = dve.tensor_copy(rows[:, :, KS - 1:CC], src[:, :, 0:KS])
                        op.then_inc(S["evacuated"], 1)
                        n += 1
                dve.wait_ge(S["evacuated"], TURNS * g + NEAR + 2)
                dve.memset(tap[:, 0, 0:1], 0.0).then_inc(S["around_ready"], 1)
                with dve.Fori(0, C // (2 * CHUNK)) as i:
                    def gated_values(k):
                        n, p = PAIRS_G * g + 4 * i + k, k % 2
                        dve.wait_ge(S["gate_exp"], n + 1)
                        dve.tensor_scalar(e1[:, p], e1[:, p], 1.0, None, ALU.add).then_inc(S["plus1"], 1)
                        dve.wait_ge(S["plus1"], n + 1)
                        dve.reciprocal(e1[:, p], e1[:, p]).then_inc(S["recip"], 1)
                        dve.wait_ge(S["recip"], n + 1)
                        dve.tensor_tensor(bt[:, p], conv[p][0:BLOCK, :, 0:NPIX], e1[:, p], ALU.mult).then_inc(S["b_ready"], 1)
                        dve.wait_ge(S["b_ready"], n + 4)
                        dve.scalar_tensor_tensor(out=ab[:, p], in0=bt[:, p], scalar=-1.0, in1=bt[:, p], op0=ALU.mult, op1=ALU.max
                                                 ).then_inc(S["abs_ready"], 1)

                    def softplus(k):
                        n, p = PAIRS_G * g + 4 * i + k, k % 2
                        dve.wait_ge(S["b_log"], n + 1)
                        for c in range(2):
                            op = dve.scalar_tensor_tensor(out=xt[:, :, 1:1 + BLOCKS, bass.ds(8 * i + 2 * k + c, 1)].rearrange("p a b c -> p a (b c)"),
                                                          in0=bt[:, p, c, :].rearrange("p (a b) -> p a b", a=GROUP), scalar=0.0,
                                                          in1=ab[:, p, c, :].rearrange("p (a b) -> p a b", a=GROUP), op0=ALU.max, op1=ALU.add)
                        op.then_inc(S["h_ready"], 1)
                    gated_values(0)
                    for k in range(4):
                        if k + 1 < 4:
                            gated_values(k + 1)
                        softplus(k)

                done = [CORNER_STEPS * g]

                def link(op):
                    done[0] = done[0] + 1
                    op.then_inc(S["corner_step"], 1)
                    dve.wait_ge(S["corner_step"], done[0])
                f = [fac[:, k, :] for k in range(4)]
                impulse = ka[:, :].unsqueeze(2).to_broadcast([128, KS * KS, GROUP])
                dve.wait_ge(S["corner_exp"], 3 * g + 1)
                link(dve.tensor_scalar(f[0], f[0], 1.0, None, ALU.add))
                link(dve.reciprocal(f[0], f[0]))
                link(dve.tensor_tensor(f[0].rearrange("c (a b) -> c a b", b=GROUP), f[0].rearrange("c (a b) -> c a b", b=GROUP), impulse, ALU.mult))
                dve.wait_ge(S["corner_exp"], 3 * g + 3)
                link(dve.tensor_scalar(fac[:, 1:3, :], fac[:, 1:3, :], 1.0, None, ALU.add))
                link(dve.reciprocal(fac[:, 1:3, :], fac[:, 1:3, :]))
                link(dve.scalar_tensor_tensor(out=f[2], in0=f[1], scalar=1.0, in1=f[2], op0=ALU.add, op1=ALU.mult))
                link(dve.tensor_tensor(f[3], f[1], f[1], ALU.mult))
                link(dve.scalar_tensor_tensor(out=f[2], in0=f[3], scalar=1.0, in1=f[2], op0=ALU.add, op1=ALU.mult))
                link(dve.tensor_tensor(f[1], f[3], f[3], ALU.mult))
                link(dve.scalar_tensor_tensor(out=f[2], in0=f[1], scalar=1.0, in1=f[2], op0=ALU.add, op1=ALU.mult))
                factor = f[2].rearrange("c (a b i) -> c a b i", a=KS, b=KS)

                def corner(s):
                    img, k = divmod(s, STRIPS)
                    cols = [(slice(0, REACH + 1), slice(REACH, KS)), (slice(W - REACH, W), slice(0, REACH))]
                    for j, rows, a in {0: [(0, 2, 4), (1, 1, 6)], STRIPS - 1: [(2, 2, 0), (3, 2, 2)]}.get(k, []):
                        for w, b in cols:
                            yield (hT[:, s % 2, j, :].rearrange("c (r w) -> c r w", r=2)[:, 0:rows, w],
                                   th[s % 2][:, BLOCK * j:BLOCK * (j + 1)].rearrange("c (r w) -> c r w", r=2)[:, 0:rows, w],
                                   factor[:, a:a + rows, b, img])

                def evacuate(s):
                    dve.wait_ge(S["turned"], TURNS * g + NEAR + s + 1)
                    op = dve.tensor_scalar(hT[:, s % 2].rearrange("c a b -> c (a b)"), th[s % 2][:, 0:4 * BLOCK],
                                           EPS, 1.0 - 0.5 ** SCAN, ALU.add, ALU.mult)
                    op.then_inc(S["evacuated"], 1)
                    own = list(corner(s))
                    if own:
                        dve.wait_ge(S["evacuated"], TURNS * g + NEAR + s + 3)
                    for dst, src, by in own:
                        op = dve.scalar_tensor_tensor(out=dst, in0=src, scalar=EPS, in1=by, op0=ALU.add, op1=ALU.mult)
                    if own:
                        op.then_inc(S["corner_ready"], 1)

                evacuate(0)
                for s in range(SECOND):
                    if s + 1 < SECOND:
                        evacuate(s + 1)
                    dve.wait_ge(S["ob_psum"], SECOND * g + s + 1)
                    dve.wait_ge(S["residual_ready"], SECOND * g + s + 1)
                    if s >= 4:
                        dve.wait_ge(x3_stored[s % 4], whole[s % 4] * g + before[s])
                    dve.tensor_tensor(X3[:, s % 4].rearrange("p a b -> p (a b)"), ob[s % 2][0:BLOCK, :],
                                      XR[:, s % 4].rearrange("p a b -> p (a b)"), ALU.add).then_inc(S["x3_ready"], 1)

        @block.tensor
        def _(pe):
            pe.wait_ge(S["ident_ready"], 1)
            pe.wait_ge(S["const_landed"], 64)
            with pe.Fori(0, GROUPS) as g:
                n = 0
                for img in range(GROUP):
                    pe.wait_ge(image_landed[img], 48 * g + 48)
                    for blocks in near_blocks:
                        pe.wait_ge(S["evacuated"], TURNS * g + n + 1)
                        for k, i in enumerate(blocks):
                            op = pe.transpose(th[n % 2][:, k * BLOCK:(k + 1) * BLOCK], xt[:, img, i + 1, :], ident[0:BLOCK, 0:BLOCK])
                        op.then_inc(S["turned"], 1)
                        n += 1
                with pe.Fori(0, C // (2 * CHUNK)) as i:
                    for k in range(4):
                        n = PAIRS_G * g + 4 * i + k
                        if k % 2 == 0:
                            pe.wait_ge(tz_landed[k // 2], C // CHUNK * 8 * g + 16 * i + 16)
                        pe.wait_ge(S["b_ready"], n + 2)
                        for c in range(2):
                            ch = 8 * i + 2 * k + c
                            for kernel in range(2):
                                for o in range(4):
                                    q = 6 - 2 * o
                                    op = pe.matmul(conv[k % 2][0:BLOCK, c, NPIX * kernel:NPIX * (kernel + 1)],
                                                   tz[:, k // 2, 2 * (k % 2) + c, kernel, W * q:W * (q + 2)],
                                                   xt[:, :, o:o + BLOCKS, bass.ds(ch, 1)].rearrange("p a b c -> p a (b c)"),
                                                   start=o == 0, stop=o == 3)
                        op.then_inc(S["conv_psum"], 1)
                pe.wait_ge(S["h_ready"], PAIRS_G * g + PAIRS_G)

                def turn(s):
                    img, k = divmod(s, STRIPS)
                    pe.wait_ge(S["evacuated"], TURNS * g + NEAR + s + 1)
                    for b in range(4):
                        op = pe.transpose(th[s % 2][:, b * BLOCK:(b + 1) * BLOCK], xt[:, img, 4 * k + b + 1, :], ident[0:BLOCK, 0:BLOCK])
                    op.then_inc(S["turned"], 1)
                turn(0)
                for s in range(SECOND):
                    if s + 1 < SECOND:
                        turn(s + 1)
                    if s % STRIPS in (0, STRIPS - 1):
                        pe.wait_ge(S["corner_ready"], 2 * GROUP * g + 2 * (s // STRIPS) + (1 if s % STRIPS == 0 else 2))
                    else:
                        pe.wait_ge(S["evacuated"], TURNS * g + NEAR + s + 3)
                    pe.wait_ge(S["x3_ready"], SECOND * g + s + 1)
                    for b in range(4):
                        op = pe.matmul(ob[s % 2][0:BLOCK, b * C:(b + 1) * C], hT[:, s % 2, b, :], wout[:, :], start=True, stop=True)
                    op.then_inc(S["ob_psum"], 1)


EXPERTS = 64
TOP = 8
HIDDEN = 512
HCHUNKS = HIDDEN // 128
TP = 112
TK = TOKENS // TP
TQ = 4
TGROUPS = TK // TQ
TWINS = B // 2
TAKEN = -2.0 ** 127


def route_phase(nc, x3, gate_w_t, gate_b, probs, pooled):
    nc.disable_value_cache = True
    with ExitStack() as ctx:
        def sb(name, shape):
            return ctx.enter_context(nc.sbuf_tensor("m_" + name, shape, F32))

        def bank(name):
            return ctx.enter_context(nc.psum_tensor("m_" + name, [128, 512], F32))

        semaphores = []

        def sem(name):
            semaphores.append(ctx.enter_context(nc.semaphore("m_" + name)))
            return semaphores[-1]

        ACT_SHARE = TQ - 1
        NT = 2 * TK
        ident = sb("ident", [128, 128])
        gwt = sb("gwt", [128, EXPERTS])
        gb = sb("gb", [128, 1])
        half_neg = sb("half_neg", [TP, NT])
        eps5 = sb("eps5", [TP, NT])
        carrier = sb("carrier", [128, 6])
        xn = sb("xn", [TP, 4, 2, TK, C])
        xT = sb("xT", [128, 2, 2, TQ * TP])
        L = sb("L", [128, 2, TOKENS])
        E = sb("E", [128, TOKENS])
        P = sb("P", [128, 2, TOKENS])
        PT = sb("PT", [TP, 2, TQ, 128])
        top = sb("top", [128, 2, TOP])
        neg_max = sb("neg_max", [128, 2])
        total = sb("total", [128, 1])
        inv = sb("inv", [128, 1])
        bn = sb("bn", [TP, NT, 6])
        mv = sb("mv", [TP, NT, 2])
        ve = sb("ve", [TP, NT])
        rs = sb("rs", [TP, NT])
        nm = sb("nm", [TP, NT])
        nb = sb("nb", [TP, NT])

        th = [bank("th0"), bank("th1")]
        lg = [bank("lg0"), bank("lg1")]
        pt = [bank("pt0"), bank("pt1")]
        pb = [bank("pb0"), bank("pb1")]

        names = """ident_zero ident_ready const_landed consts stats aggr var dev shift xn_ready xn_ready2 turned xT_ready
            lg_psum l_ready top_ready max_ready replaced exp_ready inv_ready masked p_ready pt_psum PT_ready
            pooled_psum pooled_out""".split()
        S = {n: sem(n) for n in names}
        x_landed = [sem(f"x_landed{i}") for i in range(4)]
        p_stored = [sem(f"p_stored{i}") for i in range(2)]

        def turns(eng, turn):
            def one(t):
                turn(t, t % 4, lambda o: 0 <= t + o < TWINS)
            for t in range(-2, 6):
                one(t)
            with eng.Fori(1, (TWINS - 4) // 4) as i:
                for j in range(2, 6):
                    turn(4 * i + j, j % 4, lambda o: True)
            for t in range(TWINS - 2, TWINS + 1):
                one(t)

        block = phase_block(nc, ctx, semaphores)

        @block.sync
        def _(sp):
            sp.dma_start(gwt[:, :], gate_w_t).then_inc(S["const_landed"], 16)
            for u in range(2):
                sp.dma_start(gb[EXPERTS * u:EXPERTS * (u + 1), :], gate_b.rearrange("(p a) -> p a", a=1)
                             ).then_inc(S["const_landed"], 16)

            def turn(t, j, has):
                if has(2):
                    wait(sp, S["pooled_psum"], t - 1)
                    for u in range(2):
                        sp.dma_start(xn[:, (j + 2) % 4, u], x3.rearrange("b h w c -> b (h w) c").rearrange(
                            "b (p k) c -> b p k c", k=TK)[2 * (t + 2) + u]).then_inc(x_landed[(j + 2) % 4], 16)
                if has(-1):
                    sp.wait_ge(S["p_ready"], t)
                    sp.dma_start(probs[t - 1], P[:, (j - 1) % 2]).then_inc(p_stored[(j - 1) % 2], 16)
            turns(sp, turn)
            for i in range(2):
                sp.wait_ge(p_stored[i], 16 * (TWINS // 2))

        @block.gpsimd
        def _(pool):
            make_identity(pool, ident, S["ident_zero"], S["ident_ready"])
            pool.memset(half_neg[:, :], -0.5)
            pool.memset(eps5[:, :], 1e-5).then_inc(S["consts"], 1)
            pool.wait_ge(S["consts"], 1)

            def turn(t, j, has):
                if not has(1):
                    return
                m, slot = t + 1, (j + 1) % 4
                pool.wait_ge(S["aggr"], m + 1)
                pool.tensor_tensor(ve[:, :], mv[:, :, 1], eps5[:, :], ALU.add)
                pool.tensor_scalar(nm[:, :], mv[:, :, 0], -1.0, 1.0, ALU.mult, ALU.mult).then_inc(S["var"], 1)
                pool.wait_ge(S["var"], m + 1)
                wait(pool, S["xn_ready2"], TGROUPS * m)
                pool.tensor_tensor(carrier[0:TP, 3:4], half_neg[:, 0:1], half_neg[:, 1:2], ALU.mult)
                pool.tensor_tensor(rs[:, :], ve[:, :], half_neg[:, :], ALU.pow).then_inc(S["dev"], 1)
                pool.wait_ge(S["dev"], m + 1)
                pool.tensor_tensor(nb[:, :], nm[:, :], rs[:, :], ALU.mult).then_inc(S["shift"], 1)
                pool.wait_ge(S["shift"], m + 1)
                pool.tensor_tensor(carrier[0:TP, 0:1], half_neg[:, 0:1], half_neg[:, 1:2], ALU.mult)
                for g in range(TGROUPS):
                    for u in range(2):
                        for k in range(TQ * g, TQ * (g + 1)):
                            n = TK * u + k
                            if k % TQ != ACT_SHARE:
                                op = pool.tensor_scalar(xn[:, slot, u, k], xn[:, slot, u, k], rs[:, n:n + 1], nb[:, n:n + 1],
                                                        ALU.mult, ALU.add)
                    op.then_inc(S["xn_ready"], 1)
            turns(pool, turn)

        @block.scalar
        def _(act):
            act.wait_ge(S["const_landed"], 48)

            def turn(t, j, has):
                m, p = t - 1, (j - 1) % 2

                def logits_out(g):
                    act.wait_ge(S["lg_psum"], TGROUPS * t + g + 1)
                    if g == 0:
                        wait(act, S["replaced"], t - 1)
                    act.activation(L[:, j % 2].rearrange("e (p k) -> e k p", k=TK)[:, TQ * g:TQ * (g + 1), :],
                                   lg[g % 2][:, 0:TQ * TP].rearrange("e (k p) -> e k p", k=TQ),
                                   ACT.Identity, bias=gb[:, 0:1]).then_inc(S["l_ready"], 1)
                if has(-1):
                    wait(act, S["masked"], m)
                    act.wait_ge(S["max_ready"], m + 1)
                    act.activation(E[:, :], L[:, p], ACT.Exp, bias=neg_max[:, p:p + 1], accum_out=total[:, 0:1]
                                   ).then_inc(S["exp_ready"], 1)
                for g in range(TGROUPS):
                    if has(-1) and g == 4:
                        act.wait_ge(S["inv_ready"], m + 1)
                        act.wait_ge(S["masked"], m + 1)
                        act.activation(P[:, p], P[:, p], ACT.Copy, scale=inv[:, 0:1]).then_inc(S["p_ready"], 1)
                    if has(0):
                        if g >= 2:
                            act.wait_ge(S["lg_psum"], TGROUPS * t + g - 1)
                        else:
                            wait(act, S["lg_psum"], TGROUPS * t + g - 1)
                        for u in range(2):
                            act.wait_ge(S["turned"], 2 * (TGROUPS * t + g) + u + 1)
                            act.activation(xT[:, g % 2, u], th[u][:, 0:TQ * TP], ACT.Copy).then_inc(S["xT_ready"], 1)
                        if g:
                            logits_out(g - 1)
                if has(0):
                    logits_out(TGROUPS - 1)
                if has(1):
                    act.wait_ge(S["shift"], t + 2)
                for g in range(TGROUPS):
                    if has(1):
                        for u in range(2):
                            k = TQ * g + ACT_SHARE
                            n = TK * u + k
                            op = act.activation(xn[:, (j + 1) % 4, u, k], xn[:, (j + 1) % 4, u, k], ACT.Identity,
                                                scale=rs[:, n:n + 1], bias=nb[:, n:n + 1])
                        op.then_inc(S["xn_ready2"], 1)
                    if has(-1):
                        act.wait_ge(S["pt_psum"], TGROUPS * m + g + 1)
                        act.activation(PT[:, g % 2].rearrange("p k e -> p (k e)"), pt[g % 2][0:TP, :], ACT.Copy
                                       ).then_inc(S["PT_ready"], 1)
                if has(-1):
                    act.wait_ge(S["pooled_psum"], m + 1)
                    for u in range(2):
                        op = act.activation(pooled[:, :, bass.ds(2 * m + u, 1)].rearrange("c e a -> c (e a)"),
                                            pb[u][:, 0:EXPERTS], ACT.Copy)
                    op.then_inc(S["pooled_out"], 1)
            turns(act, turn)

        @block.vector
        def _(dve):
            def turn(t, j, has):
                m, p = t - 1, (j - 1) % 2

                if has(1):
                    slot = (j + 1) % 4
                    wait(dve, S["aggr"], t + 1)
                    dve.wait_ge(x_landed[slot], 8 * (t + 1 - slot) + 32)
                    dve.memset(carrier[:, 1:2], 0.0)
                    for n in range(NT):
                        op = dve.bn_stats(bn[:, n, :], xn[:, slot, n // TK, n % TK, :])
                    op.then_inc(S["stats"], 1)
                    dve.wait_ge(S["stats"], t + 2)
                    wait(dve, S["xn_ready"], TGROUPS * (t + 1))
                    dve.memset(carrier[:, 4:5], 0.0)
                    for n in range(NT):
                        op = dve.bn_aggr(mv[:, n, :], bn[:, n, :])
                    op.then_inc(S["aggr"], 1)
                if has(-1):
                    dve.wait_ge(S["l_ready"], TGROUPS * (m + 1))
                    dve.memset(carrier[:, 2:3], 0.0)
                    dve.max(top[:, p], L[:, p]).then_inc(S["top_ready"], 1)
                    dve.wait_ge(S["top_ready"], m + 1)
                    dve.tensor_scalar(neg_max[:, p:p + 1], top[:, p, 0:1], -1.0, None, ALU.mult).then_inc(S["max_ready"], 1)
                    wait(dve, p_stored[p], 8 * (m - p))
                    wait(dve, S["pooled_psum"], m - 1)
                    dve.memset(carrier[:, 5:6], 0.0)
                    dve.match_replace(P[:, p], top[:, p], L[:, p], TAKEN).then_inc(S["replaced"], 1)
                    dve.wait_ge(S["exp_ready"], m + 1)
                    dve.reciprocal(inv[:, 0:1], total[:, 0:1]).then_inc(S["inv_ready"], 1)
                    dve.wait_ge(S["replaced"], m + 1)
                    dve.scalar_tensor_tensor(out=P[:, p], in0=P[:, p], scalar=TAKEN, in1=E[:, :], op0=ALU.is_equal,
                                             op1=ALU.mult).then_inc(S["masked"], 1)
            turns(dve, turn)

        @block.tensor
        def _(pe):
            pe.wait_ge(S["ident_ready"], 1)
            pe.wait_ge(S["const_landed"], 48)

            def turn(t, j, has):
                m, p = t - 1, (j - 1) % 2

                def transposes(g):
                    pe.wait_ge(S["xn_ready"], TGROUPS * t + g + 1)
                    pe.wait_ge(S["xn_ready2"], TGROUPS * t + g + 1)
                    for u in range(2):
                        wait(pe, S["xT_ready"], 2 * (TGROUPS * t + g - 1) + u + 1)
                        for k in range(TQ):
                            op = pe.transpose(th[u][:, TP * k:TP * (k + 1)], xn[:, j, u, TQ * g + k, :], ident[0:TP, 0:TP])
                        op.then_inc(S["turned"], 1)
                if has(0):
                    transposes(0)
                    for g in range(TGROUPS):
                        if g + 1 < TGROUPS:
                            transposes(g + 1)
                        pe.wait_ge(S["xT_ready"], 2 * (TGROUPS * t + g) + 2)
                        wait(pe, S["l_ready"], TGROUPS * t + g - 1)
                        for u in range(2):
                            op = pe.matmul(lg[g % 2][EXPERTS * u:EXPERTS * (u + 1), 0:TQ * TP], gwt[:, :], xT[:, g % 2, u],
                                           start=True, stop=True)
                        op.then_inc(S["lg_psum"], 1)
                if has(-1):
                    pe.wait_ge(S["p_ready"], m + 1)
                    wait(pe, S["pooled_out"], m)

                    def turn_probs(g):
                        wait(pe, S["PT_ready"], TGROUPS * m + g - 1)
                        for k in range(TQ):
                            rows = P[:, p].rearrange("e (p k) -> e k p", k=TK)[:, TQ * g + k, :]
                            op = pe.transpose(pt[g % 2][0:TP, 128 * k:128 * (k + 1)], rows, ident[:, :])
                        op.then_inc(S["pt_psum"], 1)
                    turn_probs(0)
                    for g in range(TGROUPS):
                        if g + 1 < TGROUPS:
                            turn_probs(g + 1)
                        pe.wait_ge(S["PT_ready"], TGROUPS * m + g + 1)
                        for k in range(TQ):
                            for u in range(2):
                                n = TQ * g + k
                                op = pe.matmul(pb[u][:, 0:EXPERTS], xn[:, (j - 1) % 4, u, n, :], PT[:, g % 2, k, EXPERTS * u:EXPERTS * (u + 1)],
                                               start=n == 0, stop=n == TK - 1)
                    op.then_inc(S["pooled_psum"], 1)
            turns(pe, turn)


def expert_phase(nc, pooled, weight1, weight2, expert_out):
    nc.disable_value_cache = True
    with ExitStack() as ctx:
        def sb(name, shape):
            return ctx.enter_context(nc.sbuf_tensor("x_" + name, shape, F32))

        def bank(name):
            return ctx.enter_context(nc.psum_tensor("x_" + name, [128, 512], F32))

        semaphores = []

        def sem(name):
            semaphores.append(ctx.enter_context(nc.semaphore("x_" + name)))
            return semaphores[-1]

        DEPTH = 4
        one = sb("one", [1, B])
        w1 = sb("w1", [128, DEPTH, HIDDEN])
        w1_bias = sb("w1_bias", [1, DEPTH, HIDDEN])
        w2 = sb("w2", [128, DEPTH, HCHUNKS, C])
        w2_bias = sb("w2_bias", [1, DEPTH, C])
        hid = sb("hid", [128, 2, HCHUNKS * B])
        OE = sb("OE", [B, EXPERTS, C])
        h_bank = [bank("h0"), bank("h1")]
        o_bank = [bank("o0"), bank("o1")]
        S = {n: sem(n) for n in "ready h_psum h_ready o_psum o_ready stored".split()}
        w_landed = [sem(f"w_landed{i}") for i in range(DEPTH)]

        block = phase_block(nc, ctx, semaphores)

        @block.sync
        def _(sp):
            def load(e, i):
                sp.dma_start(w1[:, i], weight1[e, 0:C, :]).then_inc(w_landed[i], 16)
                sp.dma_start(w1_bias[:, i], weight1[e, C:C + 1, :]).then_inc(w_landed[i], 16)
                sp.dma_start(w2[:, i], weight2[e, 0:HIDDEN, :].rearrange("(p k) o -> p k o", k=HCHUNKS)).then_inc(w_landed[i], 16)
                sp.dma_start(w2_bias[:, i], weight2[e, HIDDEN:HIDDEN + 1, :]).then_inc(w_landed[i], 16)
            for i in range(DEPTH):
                load(i, i)
            with sp.Fori(0, EXPERTS // DEPTH - 1) as n:
                for i in range(DEPTH):
                    sp.wait_ge(S["o_psum"], DEPTH * n + i + 1)
                    load(DEPTH * n + DEPTH + i, i)
            sp.wait_ge(S["o_ready"], EXPERTS + 2)
            sp.dma_start(expert_out.rearrange("b e o -> b (e o)"), OE.ap().rearrange("b e o -> b (e o)")).then_inc(S["stored"], 16)
            sp.wait_ge(S["stored"], 16)

        @block.scalar
        def _(act):
            with act.Fori(0, EXPERTS // 2) as n:
                for i in range(2):
                    act.wait_ge(S["h_psum"], 2 * n + i + 1)
                    act.activation(hid[:, i], h_bank[i][:, 0:HCHUNKS * B], ACT.Gelu).then_inc(S["h_ready"], 1)

        @block.vector
        def _(dve):
            dve.memset(one[:, :], 1.0).then_inc(S["ready"], 1)
            dve.memset(OE[:, 0, 0:1], 0.0).then_inc(S["o_ready"], 2)
            dve.wait_ge(S["o_ready"], 2)
            with dve.Fori(0, EXPERTS // 2) as n:
                for i in range(2):
                    dve.wait_ge(S["o_psum"], 2 * n + i + 1)
                    dve.tensor_copy(OE[:, bass.ds(2 * n + i, 1), :].rearrange("b e o -> b (e o)"), o_bank[i][0:B, 0:C]
                                    ).then_inc(S["o_ready"], 1)

        @block.tensor
        def _(pe):
            pe.wait_ge(S["ready"], 1)

            def hidden(e, slot, landed):
                i = slot % 2
                pe.wait_ge(w_landed[slot], landed)
                pe.wait_ge(S["o_ready"], e + 1)
                for k in range(HCHUNKS):
                    part = slice(k, HIDDEN, HCHUNKS)
                    out = h_bank[i][:, B * k:B * (k + 1)]
                    pe.matmul(out, w1[:, slot, part], pooled[:, bass.ds(e, 1), :].rearrange("c e b -> c (e b)"), start=True, stop=False)
                    op = pe.matmul(out, w1_bias[:, slot, part], one[:, :], start=False, stop=True)
                op.then_inc(S["h_psum"], 1)

            def outputs(e, slot):
                i = slot % 2
                pe.wait_ge(S["h_ready"], e + 1)
                for k in range(HCHUNKS):
                    pe.matmul(o_bank[i][0:B, 0:C], hid[:, i, B * k:B * (k + 1)], w2[:, slot, k], start=k == 0, stop=False)
                pe.matmul(o_bank[i][0:B, 0:C], one[:, :], w2_bias[:, slot], start=False, stop=True).then_inc(S["o_psum"], 1)
            with pe.Fori(0, EXPERTS // DEPTH) as n:
                hidden(DEPTH * n, 0, 64 * n + 64)
                for i in range(DEPTH):
                    if i + 1 < DEPTH:
                        hidden(DEPTH * n + i + 1, i + 1, 64 * n + 64)
                    outputs(DEPTH * n + i, i)


def spread_phase(nc, x3, probs, expert_out, out):
    nc.disable_value_cache = True
    with ExitStack() as ctx:
        def sb(name, shape):
            return ctx.enter_context(nc.sbuf_tensor("s_" + name, shape, F32))

        semaphores = []

        def sem(name):
            semaphores.append(ctx.enter_context(nc.semaphore("s_" + name)))
            return semaphores[-1]

        DEPTH, BANKS = 4, 8
        P = sb("P", [128, DEPTH, TOKENS])
        OE = sb("OE", [128, DEPTH, C])
        X = sb("X", [TP, DEPTH, 2, TK, C])
        ob = [ctx.enter_context(nc.psum_tensor(f"s_o{i}", [128, 512], F32)) for i in range(BANKS)]
        o_psum, added = sem("o_psum"), sem("added")
        landed = [sem(f"landed{i}") for i in range(DEPTH)]
        stored = [sem(f"stored{i}") for i in range(DEPTH)]
        STEPS2 = 2 * TGROUPS

        def image(dram, n):
            return dram.rearrange("b h w c -> b (h w) c").rearrange("b (p k) c -> b p k c", k=TK)[n]

        block = phase_block(nc, ctx, semaphores)

        @block.sync
        def _(sp):
            def load(n, i):
                sp.dma_start(P[:, i], probs[n]).then_inc(landed[i], 16)
                sp.dma_start(OE[:, i], expert_out.rearrange("(n u) e o -> n (u e) o", u=2)[n]).then_inc(landed[i], 16)
                for u in range(2):
                    sp.dma_start(X[:, i, u], image(x3, 2 * n + u)).then_inc(landed[i], 16)
            for i in range(DEPTH):
                load(i, i)
            with sp.Fori(0, TWINS // DEPTH - 1) as m:
                for i in range(DEPTH):
                    sp.wait_ge(stored[i], 32 * m + 32)
                    load(DEPTH * m + DEPTH + i, i)

        @block.scalar
        def _(act):
            with act.Fori(0, TWINS // DEPTH) as m:
                for i in range(DEPTH):
                    for u in range(2):
                        act.wait_ge(added, STEPS2 * (DEPTH * m + i) + TGROUPS * (u + 1) + BANKS)
                        act.dma_start(image(out, 2 * (DEPTH * m + i) + u), X[:, i, u]).then_inc(stored[i], 16)
            for i in range(DEPTH):
                act.wait_ge(stored[i], 32 * (TWINS // DEPTH))

        @block.vector
        def _(dve):
            dve.memset(ob[0][0:1, 0:1], 0.0).then_inc(added, BANKS)
            dve.wait_ge(added, BANKS)
            with dve.Fori(0, TWINS // DEPTH) as m:
                for i in range(DEPTH):
                    dve.wait_ge(landed[i], 64 * m + 64)
                    for g in range(STEPS2):
                        u, k = divmod(g, TGROUPS)
                        dve.wait_ge(o_psum, STEPS2 * (DEPTH * m + i) + g + 1)
                        x = X[:, i, u, TQ * k:TQ * (k + 1)].rearrange("p k c -> p (k c)")
                        dve.tensor_tensor(x, ob[(STEPS2 * i + g) % BANKS][0:TP, :], x, ALU.add).then_inc(added, 1)

        @block.tensor
        def _(pe):
            with pe.Fori(0, TWINS // DEPTH) as m:
                for i in range(DEPTH):
                    pe.wait_ge(landed[i], 64 * m + 64)
                    for g in range(STEPS2):
                        u, k = divmod(g, TGROUPS)
                        rows = slice(EXPERTS * u, EXPERTS * (u + 1))
                        pe.wait_ge(added, STEPS2 * (DEPTH * m + i) + g + 1)
                        for q in range(TQ):
                            pt = P[rows, i].rearrange("e (p k) -> e k p", k=TK)[:, TQ * k + q, :]
                            op = pe.matmul(ob[(STEPS2 * i + g) % BANKS][0:TP, C * q:C * (q + 1)], pt, OE[rows, i], start=True, stop=True)
                        op.then_inc(o_psum, 1)


def metaformer(nc, x, w_qkv_t, pos, mask, head_own, attn_w_out_t, attn_b_out, w, w_t, v_t, gamma, beta, kernel_a, kernel_b,
               kernel_gate_a, kernel_gate_b, conv_w_out, conv_b_out, gate_w_t, gate_b, weight1, weight2, out):
    def scratch(name, shape):
        return nc.dram_tensor(name, shape, F32, kind="Internal").ap()

    image = (B, H, W, C)
    x1, x2, xc, x3 = [scratch(name, image) for name in ("x1", "x2", "xc", "x3")]
    pos_rows = scratch("pos_rows", (WS, 2 * WS - 1, WS))
    rows = scratch("kernel_rows", (C, 2, TAPS + 1, 2 * W))
    toeplitz = scratch("toeplitz", (BLOCK, C, 2, TZ))
    probs = scratch("probs", (TWINS, 2 * EXPERTS, TOKENS))
    expert_out = scratch("expert_out", (B, EXPERTS, C))

    kernel_rows_phase(nc, kernel_b, kernel_gate_b, rows)
    with nc.sbuf_tensor("gram", [C, C + 1], F32) as gram:
        attention_phase(nc, x, w_qkv_t, pos, pos_rows, mask, head_own, attn_w_out_t, attn_b_out, rows, toeplitz, x1, gram)
        recurrent_phase(nc, x1, w, w_t, v_t, gamma, beta, gram, x2, xc)
    convolution_phase(nc, xc, x2, toeplitz, kernel_a, kernel_gate_a, conv_w_out, conv_b_out, x3)
    with nc.sbuf_tensor("pooled", [C, EXPERTS, B], F32) as pooled:
        route_phase(nc, x3, gate_w_t, gate_b, probs, pooled)
        expert_phase(nc, pooled, weight1, weight2, expert_out)
    spread_phase(nc, x3, probs, expert_out, out)


def kernel(**inputs):
    import concourse.bacc as bacc
    from concourse.bass_utils import run_bass_kernel_spmd

    given = {name: np.asarray(a) for name, a in inputs.items()}
    arrays = {
        "x": given["x"],
        "w_qkv_t": given["L0_conv_w_qkv"].T,
        "pos": given["L0_conv_pos_embedding"],
        "mask": window_masks(),
        "head_own": head_channels(),
        "attn_w_out_t": given["L0_conv_w_out"].T,
        "attn_b_out": given["L0_conv_b_out"],
        "w": given["L0_ffn_W"],
        "w_t": given["L0_ffn_W"].T,
        "v_t": given["L0_ffn_V"].T,
        "gamma": given["L0_ffn_gamma"],
        "beta": given["L0_ffn_beta"],
        "kernel_a": given["L1_conv_A_kernel"],
        "kernel_b": given["L1_conv_B_kernel"],
        "kernel_gate_a": given["L1_conv_gate_A_kernel"],
        "kernel_gate_b": given["L1_conv_gate_B_kernel"],
        "conv_w_out": given["L1_conv_W_out"],
        "conv_b_out": given["L1_conv_b_out"],
        "gate_w_t": given["L1_ffn_gate_w"].T,
        "gate_b": given["L1_ffn_gate_b"],
        "weight1": given["L1_ffn_weight1"],
        "weight2": given["L1_ffn_weight2"],
    }
    arrays = {name: np.ascontiguousarray(a) for name, a in arrays.items()}
    nc = bacc.Bacc("TRN2", target_bir_lowering=False, num_devices=1)
    aps = {name: nc.dram_tensor(name, a.shape, mybir.dt.from_np(a.dtype), kind="ExternalInput").ap() for name, a in arrays.items()}
    out = nc.dram_tensor("out", (B, H, W, C), F32, kind="ExternalOutput").ap()
    metaformer(nc, out=out, **aps)
    result = run_bass_kernel_spmd(nc, [arrays], core_ids=[0])
    return result.results[0]["out"]
```
